# Optimizing a Trainium2 kernel written in Bass

```python
import numpy as np
import jax
import jax.numpy as jnp

def _softmax(x, axis=-1):
    return jax.nn.softmax(x, axis=axis)

def _gelu(x):
    return jax.nn.gelu(x, approximate=True)

def _silu(x):
    return jax.nn.silu(x)

def _sigmoid(x):
    return jax.nn.sigmoid(x)

def _layernorm(x, axis=-1, eps=1e-05):
    m = jnp.mean(x, axis=axis, keepdims=True)
    v = jnp.var(x, axis=axis, keepdims=True)
    return (x - m) / jnp.sqrt(v + eps)

def _scatter_add(tgt, idx, src, axis=0):
    return tgt.at[idx].add(src)

def _segment_sum(src, seg, n):
    return jax.ops.segment_sum(src, seg, n)
kernel_name = 'mk_gnn_preln_d4_gnn_r8_50d02f'

def setup_inputs(seed: int=0):
    np.random.seed(seed)
    _w = jnp.asarray

    def _rec_inputs():
        import jax
        import jax.numpy as jnp
        _gk = jax.random.key(seed)
        x = -0.0005121 + 1.001 * jax.random.normal(jax.random.fold_in(_gk, 1), (12500, 32), jnp.float32)
        src = jax.random.randint(jax.random.fold_in(_gk, 2), (200000,), 0, 12500, jnp.int32)
        dst = jnp.minimum((12500 * jax.random.uniform(jax.random.fold_in(_gk, 3), (200000,)) ** 2.0).astype(jnp.int32), 99999)
        _o = jnp.argsort(dst, stable=True)
        src = src[_o]
        dst = dst[_o]
        edge_attr_3 = jax.random.uniform(jax.random.fold_in(_gk, 12), (200000, 3), jnp.float32, 0.0, 0.999998)
        edge_weight = 0.000452788 + 0.999756 * jax.random.normal(jax.random.fold_in(_gk, 14), (200000,), jnp.float32)
        return (x, src, dst, edge_attr_3, edge_weight)
    x, src, dst, edge_attr_3, edge_weight = _rec_inputs()

    def _L0_gnn_setup():
        import jax, jax.numpy as jnp
        import numpy as np
        N_NODES = 12500
        N_EDGES = 200000
        D_FEAT = 32
        key = jax.random.key(seed)
        k1, k2 = jax.random.split(key)
        x = jax.random.normal(k1, (N_NODES, D_FEAT), dtype=jnp.float32)
        edge_neighbors = jax.random.randint(k2, (2, N_EDGES), 0, N_NODES, dtype=jnp.int64)
        return {'x': x, 'edge_neighbors': edge_neighbors}
    _L0_gnn_all = _L0_gnn_setup()
    _L0_gnn_in = {k: v for k, v in _L0_gnn_all.items() if k in ()}
    del _L0_gnn_all

    def _L1_gnn_setup():
        import jax, jax.numpy as jnp
        import numpy as np
        D = 3
        KS = 5
        K = KS ** D
        S = 2 ** D
        _COMBOS = np.array([[s >> d & 1 for d in range(D)] for s in range(S)], dtype=np.int32)
        _STRIDES = np.array([KS ** (D - 1 - d) for d in range(D)], dtype=np.int32)

        def spline_basis(pseudo):
            pos = pseudo * (KS - 1)
            i0 = jnp.clip(jnp.floor(pos), 0, KS - 2).astype(jnp.int32)
            frac = pos - i0
            combos = jnp.asarray(_COMBOS)
            basis = jnp.prod(jnp.where(combos[None] == 1, frac[:, None, :], 1.0 - frac[:, None, :]), axis=-1)
            idx = jnp.sum((i0[:, None, :] + combos[None]) * jnp.asarray(_STRIDES)[None, None, :], axis=-1)
            return (basis, idx)

        def spline_conv(x, row, col, basis, idx, W, b):
            N = x.shape[0]
            Fout = W.shape[2]
            z = jnp.einsum('ni,kio->nko', x, W).reshape(N * K, Fout)
            gathered = z[col[:, None] * K + idx]
            msg = jnp.einsum('es,eso->eo', basis, gathered)
            out = jax.ops.segment_sum(msg, row, num_segments=N)
            deg = jax.ops.segment_sum(jnp.ones_like(msg[:, 0]), row, num_segments=N)
            return out / jnp.maximum(deg, 1.0)[:, None] + b
        key = jax.random.key(seed)
        ks = jax.random.split(key, 13)
        N, E, Fin, Fout = (2500, 40000, 32, 32)

        def u(k, shape, size):
            bound = 1.0 / np.sqrt(size)
            return jax.random.uniform(k, shape, jnp.float32, -bound, bound)
        return dict(x=jax.random.normal(ks[0], (N, Fin), jnp.float32), edge_index=jax.random.randint(ks[1], (2, E), 0, N, dtype=jnp.int32), pseudo=jax.random.uniform(ks[2], (E, D), jnp.float32), stn1_w=u(ks[3], (K, 1, 64), 1 * S), stn1_b=u(ks[4], (64,), 1 * S), stn2_w=u(ks[5], (K, 64, 64), 64 * S), stn2_b=u(ks[6], (64,), 64 * S), stn3_w=u(ks[7], (64, 64), 64), stn3_b=u(ks[8], (64,), 64), stn4_w=u(ks[9], (64, 3), 64), stn4_b=u(ks[10], (3,), 64), conv_w=u(ks[11], (K, Fin, Fout), Fin * S), conv_b=u(ks[12], (Fout,), Fin * S))
    _L1_gnn_all = _L1_gnn_setup()
    _L1_gnn_in = {k: v for k, v in _L1_gnn_all.items() if k in ('stn1_w', 'stn1_b', 'stn2_w', 'stn2_b', 'stn3_w', 'stn3_b', 'stn4_w', 'stn4_b', 'conv_w', 'conv_b')}
    del _L1_gnn_all

    def _L2_gnn_setup():
        import jax, jax.numpy as jnp
        import numpy as np
        N_NODES = 12500
        N_EDGES = 200000
        D_FEAT = 32
        key = jax.random.key(seed)
        k1, k2, k3 = jax.random.split(key, 3)
        x = jax.random.normal(k1, (N_NODES, D_FEAT), dtype=jnp.float32)
        a = jax.random.randint(k2, (2, N_EDGES), 0, N_NODES, dtype=jnp.int64)
        e = jax.random.normal(k3, (N_EDGES,), dtype=jnp.float32)
        return {'x': x, 'a': a, 'e': e}
    _L2_gnn_all = _L2_gnn_setup()
    _L2_gnn_in = {k: v for k, v in _L2_gnn_all.items() if k in ()}
    del _L2_gnn_all

    def _L3_gnn_setup():
        import jax, jax.numpy as jnp
        import numpy as np
        N_NODES = 6250
        N_EDGES = 100000
        IN_FEATS = 32
        OUT_FEATS = 32
        NUM_HEADS = 4
        key = jax.random.key(seed)
        ks = jax.random.split(key, 12)
        H, F, IN = (NUM_HEADS, OUT_FEATS, IN_FEATS)
        h = jax.random.normal(ks[0], (N_NODES, IN), dtype=jnp.float32)
        src = jax.random.randint(ks[1], (N_EDGES,), 0, N_NODES, dtype=jnp.int64)
        dst = jax.random.randint(ks[2], (N_EDGES,), 0, N_NODES, dtype=jnp.int64)
        s = 0.1
        W_gat = jax.random.normal(ks[3], (IN, H * F), dtype=jnp.float32) * s
        attn_l = jax.random.normal(ks[4], (H, F), dtype=jnp.float32) * s
        attn_r = jax.random.normal(ks[5], (H, F), dtype=jnp.float32) * s
        W_ih = jax.random.normal(ks[6], (3 * F, H * F), dtype=jnp.float32) * s
        W_hh = jax.random.normal(ks[7], (3 * F, F), dtype=jnp.float32) * s
        b_ih = jax.random.normal(ks[8], (3 * F,), dtype=jnp.float32) * s
        b_hh = jax.random.normal(ks[9], (3 * F,), dtype=jnp.float32) * s
        return {'h': h, 'W_gat': W_gat, 'attn_l': attn_l, 'attn_r': attn_r, 'W_ih': W_ih, 'W_hh': W_hh, 'b_ih': b_ih, 'b_hh': b_hh, 'src': src, 'dst': dst}
    _L3_gnn_all = _L3_gnn_setup()
    _L3_gnn_in = {k: v for k, v in _L3_gnn_all.items() if k in ('W_gat', 'attn_l', 'attn_r', 'W_ih', 'W_hh', 'b_ih', 'b_hh')}
    del _L3_gnn_all
    return {'x': x, 'src': src, 'dst': dst, 'edge_attr_3': edge_attr_3, 'edge_weight': edge_weight, 'L1_gnn_stn1_w': _L1_gnn_in['stn1_w'], 'L1_gnn_stn1_b': _L1_gnn_in['stn1_b'], 'L1_gnn_stn2_w': _L1_gnn_in['stn2_w'], 'L1_gnn_stn2_b': _L1_gnn_in['stn2_b'], 'L1_gnn_stn3_w': _L1_gnn_in['stn3_w'], 'L1_gnn_stn3_b': _L1_gnn_in['stn3_b'], 'L1_gnn_stn4_w': _L1_gnn_in['stn4_w'], 'L1_gnn_stn4_b': _L1_gnn_in['stn4_b'], 'L1_gnn_conv_w': _L1_gnn_in['conv_w'], 'L1_gnn_conv_b': _L1_gnn_in['conv_b'], 'L3_gnn_W_gat': _L3_gnn_in['W_gat'], 'L3_gnn_attn_l': _L3_gnn_in['attn_l'], 'L3_gnn_attn_r': _L3_gnn_in['attn_r'], 'L3_gnn_W_ih': _L3_gnn_in['W_ih'], 'L3_gnn_W_hh': _L3_gnn_in['W_hh'], 'L3_gnn_b_ih': _L3_gnn_in['b_ih'], 'L3_gnn_b_hh': _L3_gnn_in['b_hh']}

def reference(x, src, dst, edge_attr_3, edge_weight, L1_gnn_stn1_w, L1_gnn_stn1_b, L1_gnn_stn2_w, L1_gnn_stn2_b, L1_gnn_stn3_w, L1_gnn_stn3_b, L1_gnn_stn4_w, L1_gnn_stn4_b, L1_gnn_conv_w, L1_gnn_conv_b, L3_gnn_W_gat, L3_gnn_attn_l, L3_gnn_attn_r, L3_gnn_W_ih, L3_gnn_W_hh, L3_gnn_b_ih, L3_gnn_b_hh):
    import jax
    import jax.numpy as jnp

    def _L0_gnn_ref(x, edge_neighbors):
        import jax, jax.numpy as jnp
        import numpy as np
        N_NODES = 12500
        N_EDGES = 200000
        D_FEAT = 32
        msgs = x[edge_neighbors[1]]
        out = jax.ops.segment_sum(msgs, edge_neighbors[0], num_segments=x.shape[0])
        return out

    def _L1_gnn_ref(x, edge_index, pseudo, stn1_w, stn1_b, stn2_w, stn2_b, stn3_w, stn3_b, stn4_w, stn4_b, conv_w, conv_b):
        import jax, jax.numpy as jnp
        import numpy as np
        D = 3
        KS = 5
        K = KS ** D
        S = 2 ** D
        _COMBOS = np.array([[s >> d & 1 for d in range(D)] for s in range(S)], dtype=np.int32)
        _STRIDES = np.array([KS ** (D - 1 - d) for d in range(D)], dtype=np.int32)

        def spline_basis(pseudo):
            pos = pseudo * (KS - 1)
            i0 = jnp.clip(jnp.floor(pos), 0, KS - 2).astype(jnp.int32)
            frac = pos - i0
            combos = jnp.asarray(_COMBOS)
            basis = jnp.prod(jnp.where(combos[None] == 1, frac[:, None, :], 1.0 - frac[:, None, :]), axis=-1)
            idx = jnp.sum((i0[:, None, :] + combos[None]) * jnp.asarray(_STRIDES)[None, None, :], axis=-1)
            return (basis, idx)

        def spline_conv(x, row, col, basis, idx, W, b):
            N = x.shape[0]
            Fout = W.shape[2]
            z = jnp.einsum('ni,kio->nko', x, W).reshape(N * K, Fout)
            gathered = z[col[:, None] * K + idx]
            msg = jnp.einsum('es,eso->eo', basis, gathered)
            out = jax.ops.segment_sum(msg, row, num_segments=N)
            deg = jax.ops.segment_sum(jnp.ones_like(msg[:, 0]), row, num_segments=N)
            return out / jnp.maximum(deg, 1.0)[:, None] + b
        N = x.shape[0]
        row, col = (edge_index[0], edge_index[1])
        basis, idx = spline_basis(pseudo)
        h = jnp.ones((N, 1), x.dtype)
        h = jax.nn.elu(spline_conv(h, row, col, basis, idx, stn1_w, stn1_b))
        h = jax.nn.elu(spline_conv(h, row, col, basis, idx, stn2_w, stn2_b))
        h = jax.nn.elu(h @ stn3_w + stn3_b)
        t = h @ stn4_w + stn4_b
        new_pseudo = jnp.clip(pseudo + t[col] - t[row], 0.0, 1.0)
        basis2, idx2 = spline_basis(new_pseudo)
        return spline_conv(x, row, col, basis2, idx2, conv_w, conv_b)

    def _L2_gnn_ref(x, a, e):
        import jax, jax.numpy as jnp
        import numpy as np
        N_NODES = 12500
        N_EDGES = 200000
        D_FEAT = 32
        src = a[0]
        tgt = a[1]
        msgs = x[src] * e[:, None]
        out = jax.ops.segment_sum(msgs, tgt, num_segments=x.shape[0])
        return out

    def _L3_gnn_ref(h, W_gat, attn_l, attn_r, W_ih, W_hh, b_ih, b_hh, src, dst):
        import jax, jax.numpy as jnp
        import numpy as np
        N_NODES = 6250
        N_EDGES = 100000
        IN_FEATS = 32
        OUT_FEATS = 32
        NUM_HEADS = 4
        N = h.shape[0]
        H, F = attn_l.shape
        feat = (h @ W_gat).reshape(N, H, F)
        el = jnp.einsum('nhf,hf->nh', feat, attn_l)
        er = jnp.einsum('nhf,hf->nh', feat, attn_r)
        e = jax.nn.leaky_relu(el[src] + er[dst], 0.2)
        emax = jax.ops.segment_max(e, dst, num_segments=N)
        ee = jnp.exp(e - emax[dst])
        denom = jax.ops.segment_sum(ee, dst, num_segments=N)
        alpha = ee / denom[dst]
        msg = feat[src] * alpha[:, :, None]
        agg = jax.ops.segment_sum(msg, dst, num_segments=N)
        x = agg.reshape(N, H * F)
        gi = x @ W_ih.T + b_ih
        gh = h @ W_hh.T + b_hh
        i_r, i_z, i_n = jnp.split(gi, 3, axis=1)
        h_r, h_z, h_n = jnp.split(gh, 3, axis=1)
        r = jax.nn.sigmoid(i_r + h_r)
        z = jax.nn.sigmoid(i_z + h_z)
        n = jnp.tanh(i_n + r * h_n)
        h_new = (1.0 - z) * n + z * h
        return jax.nn.elu(h_new)
    edge_index = jnp.stack([src, dst])
    h = jnp.maximum(_layernorm(x, axis=-1), 0.0)
    x = x + _L0_gnn_ref(h, edge_index)
    h = jnp.maximum(_layernorm(x, axis=-1), 0.0)
    x = x + _L1_gnn_ref(h, edge_index, edge_attr_3, L1_gnn_stn1_w, L1_gnn_stn1_b, L1_gnn_stn2_w, L1_gnn_stn2_b, L1_gnn_stn3_w, L1_gnn_stn3_b, L1_gnn_stn4_w, L1_gnn_stn4_b, L1_gnn_conv_w, L1_gnn_conv_b)
    h = jnp.maximum(_layernorm(x, axis=-1), 0.0)
    x = x + _L2_gnn_ref(h, edge_index, edge_weight)
    h = jnp.maximum(_layernorm(x, axis=-1), 0.0)
    x = x + _L3_gnn_ref(h, L3_gnn_W_gat, L3_gnn_attn_l, L3_gnn_attn_r, L3_gnn_W_ih, L3_gnn_W_hh, L3_gnn_b_ih, L3_gnn_b_hh, src, dst)
    return x

_drawn_inputs = setup_inputs


def setup_inputs(seed=0):
    import zlib

    import numpy as np

    out = dict(_drawn_inputs(seed))
    spreads = {}
    factors = {'edge_attr_3': 8.0,
     'L1_gnn_stn1_w': 8.0,
     'L1_gnn_stn1_b': 200.0,
     'L1_gnn_stn2_w': 112.069,
     'L1_gnn_stn2_b': 8.0,
     'L1_gnn_stn3_w': 8.0,
     'L1_gnn_stn3_b': 8.0,
     'L1_gnn_stn4_w': 8.0,
     'L1_gnn_stn4_b': 8.0,
     'L1_gnn_conv_w': 8.0,
     'L1_gnn_conv_b': 8.0,
     'L3_gnn_W_gat': 3.621,
     'L3_gnn_attn_l': 8.0,
     'L3_gnn_attn_r': 22.364,
     'L3_gnn_W_ih': 3.672,
     'L3_gnn_W_hh': 4.049,
     'L3_gnn_b_ih': 25.163,
     'L3_gnn_b_hh': 31.675}
    for name, (base, spread) in spreads.items():
        noise = np.random.default_rng([zlib.crc32(name.encode()), seed]).standard_normal(out[name].shape)
        drawn = base * np.exp(spread * noise) if base else spread * noise
        out[name] = jnp.asarray(drawn.astype(out[name].dtype))
    for name, factor in factors.items():
        out[name] = (out[name] * factor).astype(out[name].dtype)
    return out
```

```python
from contextlib import ExitStack

import concourse.bass as bass
from concourse import mybir

F32 = mybir.dt.float32
I32 = mybir.dt.int32
BF16 = mybir.dt.bfloat16
ALU = mybir.AluOpType
ACT = mybir.ActivationFunctionType
AX = mybir.AxisListType.X

P = 128
N = 12500
E = 200000
D = 32
NB = -(-N // P)
NP = NB * P
L = 1568
SC = 16
SN = L // SC
NBIN = NB + 1
CH = 8
RING = 4
T = 1664
NC = T // CH
NI = NC // RING
ROWS = (NC + 1) * CH * P
WA, WB = 8, 4
PIECE = NC // 8
PT = PIECE * CH
FULL = E // L
REST = E - FULL * L
LASTN = N - (NB - 1) * P
NEG = float(2.0 ** 100)
SPANS = (7 * 64, 32 * 32)

assert P * L >= E and L % SC == 0 and T >= NB + E / P and NC % RING == 0 and NC % 8 == 0


class Phase:

    def __init__(self, nc, name):
        self.nc, self.name, self.stack, self.sems = nc, name, ExitStack(), []

    def sb(self, name, shape, dt=F32):
        return self.stack.enter_context(self.nc.sbuf_tensor(f"{self.name}_{name}", shape, dt))

    def ps(self, name, shape, dt=F32):
        return self.stack.enter_context(self.nc.psum_tensor(f"{self.name}_{name}", shape, dt))

    def sem(self, name):
        s = self.nc.alloc_semaphore(f"{self.name}_{name}")
        self.sems.append(s)
        return s

    def ring(self, name):
        return [self.sem(f"{name}{q}") for q in range(RING)]

    def __enter__(self):
        return self

    def __exit__(self, *a):
        self.nc.clear_and_free_semaphores(self.sems)
        self.nc.all_engine_barrier()
        self.stack.close()


def at(ap, k):
    if isinstance(k, int):
        return ap[k]
    names = "pqr"[:len(ap.shape) - 1]
    return ap[bass.ds(k, 1)].rearrange(f"a {' '.join(names)} -> (a {names[0]}) {' '.join(names[1:])}")


def part(tile, k, size):
    return tile[:, bass.ds(k * size, size)]


def snap(eng, v):
    return v if isinstance(v, int) else eng.snap(v)


def looped(eng, n, body):
    body(0, True)
    with eng.Fori(1, n) as i:
        body(i, False)


def constants(nc, k):
    with Phase(nc, "cst") as ph:
        made = ph.sem("made")
        raw = ph.sb("raw", [P, T], I32)
        with nc.Block() as block:
            @block.gpsimd
            def _(pool):
                pool.iota(raw[:, :], pattern=[[1, T]], base=0, channel_multiplier=0).then_inc(made, 1)
                pool.iota(k["part_i"][:, :], pattern=[[0, 1]], base=0, channel_multiplier=1).then_inc(made, 1)
                pool.memset(k["ident"][:, :], 0.0).then_inc(made, 1)
                pool.memset(k["before"][:, :], 1.0).then_inc(made, 1)
                pool.wait_ge(made, 4)
                pool.affine_select(out=k["ident"][:, :], in_=k["ident"][:, :], compare_op=ALU.not_equal, fill=1.0,
                                   base=0, pattern=[[-1, P]], channel_multiplier=1).then_inc(made, 1)
                pool.affine_select(out=k["before"][:, :], in_=k["before"][:, :], compare_op=ALU.is_gt, fill=0.0,
                                   base=0, pattern=[[1, P]], channel_multiplier=-1).then_inc(made, 1)

            @block.vector
            def _(dve):
                dve.memset(k["ones"][:, :], 1.0)
                dve.memset(k["ones_b"][:, :], 1.0)
                dve.wait_ge(made, 6)
                dve.tensor_copy(k["iota"][:, :], raw[:, :])
                dve.tensor_copy(k["part"][:, :], k["part_i"][:, :])
                dve.tensor_copy(k["ident_b"][:, :], k["ident"][:, :])
                dve.tensor_copy(k["before_b"][:, :], k["before"][:, :])


def load_nodes(nc, x, xs):
    with Phase(nc, "ld") as ph:
        zeroed, loaded = ph.sem("zeroed"), ph.sem("loaded")
        with nc.Block() as block:
            @block.vector
            def _(dve):
                dve.memset(xs[:, NB - 1, :], 0.0).then_inc(zeroed, 1)

            @block.sync
            def _(sp):
                sp.dma_start(xs[:, 0:NB - 1, :], x[0:(NB - 1) * P].rearrange("(b p) f -> p b f", p=P)).then_inc(loaded, 16)
                sp.wait_ge(zeroed, 1)
                sp.dma_start(xs[0:LASTN, NB - 1, :], x[(NB - 1) * P:N]).then_inc(loaded, 16)
                sp.wait_ge(loaded, 32)


def layernorm_relu(nc, name, xs, hs, table, width=D):
    with Phase(nc, name) as ph:
        sq = ph.sb("sq", [P, NB, D])
        s, v = ph.sb("s", [P, NB]), ph.sb("v", [P, NB])
        var_ready, std_ready, h_ready, stored = (ph.sem(n) for n in ("var", "std", "h", "st"))
        with nc.Block() as block:
            @block.vector
            def _(dve):
                dve.tensor_reduce(s[:, :], xs[:, :, :], axis=AX, op=ALU.add)
                dve.drain()
                dve.tensor_scalar(s[:, :], s[:, :], 1.0 / D, None, ALU.mult)
                dve.drain()
                dve.tensor_tensor(hs[:, :, :], xs[:, :, :], s[:, :].unsqueeze(2).to_broadcast([P, NB, D]), ALU.subtract)
                dve.drain()
                dve.tensor_tensor(sq[:, :, :], hs[:, :, :], hs[:, :, :], ALU.mult)
                dve.drain()
                dve.tensor_reduce(v[:, :], sq[:, :, :], axis=AX, op=ALU.add)
                dve.drain()
                dve.tensor_scalar(v[:, :], v[:, :], 1.0 / D, 1e-5, ALU.mult, ALU.add).then_inc(var_ready, 1)
                dve.wait_ge(std_ready, 1)
                dve.reciprocal(v[:, :], s[:, :])
                dve.drain()
                dve.tensor_tensor(hs[:, :, :], hs[:, :, :], v[:, :].unsqueeze(2).to_broadcast([P, NB, D]), ALU.mult)
                dve.drain()
                dve.tensor_scalar(hs[:, :, :], hs[:, :, :], 0.0, None, ALU.max).then_inc(h_ready, 1)

            @block.scalar
            def _(act):
                act.wait_ge(var_ready, 1)
                act.activation(s[:, :], v[:, :], ACT.Sqrt).then_inc(std_ready, 1)

            if table is not None:
                @block.sync
                def _(sp):
                    sp.wait_ge(h_ready, 1)
                    sp.dma_start(table[:, 0:D].rearrange("(b p) f -> p b f", p=P), hs[:, :, :]).then_inc(stored, 16)
                    sp.wait_ge(stored, 16)


def sort_edges(nc, name, k, key, fields, rec, W):
    with Phase(nc, name) as ph:
        recs = ph.sb("recs", [P, L, W])
        blk = ph.sb("blk", [P, L])
        key_i = ph.sb("key_i", [P, L], I32)
        tmp_i = ph.sb("tmp_i", [P, L], I32)
        raw = [ph.sb(f"raw{n}", [P, L * w], dt) for n, (_, w, dt) in enumerate(fields)]
        fill = ph.sb("fill", [P, 152, W])
        onehot = ph.sb("onehot", [P, 2, SC, NBIN], BF16)
        ranked = ph.sb("ranked", [P, SC, NBIN])
        base = ph.sb("base", [P, NBIN])
        step_blk = ph.sb("step_blk", [P, 2, SC])
        step_rec = ph.sb("step_rec", [P, 2, SC, W])
        pos = ph.sb("pos", [P, SC])
        pos_i = ph.sb("pos_i", [P, 4, SC], I32)
        row = ph.sb("row", [P, 2, SC], I32)
        small = ph.sb("small", [P, 8])
        small_i = ph.sb("small_i", [P, 4], I32)
        spread = ph.sb("spread", [P, T])
        last_i = ph.sb("last_i", [P, 2, NB], I32)
        hist = ph.ps("hist", [P, 512])
        rank = [ph.ps(f"rank{g}", [P, 512]) for g in range(4)]
        total = ph.ps("total", [P, 512])

        zeroed, loaded, filled, refilled = (ph.sem(n) for n in ("zeroed", "loaded", "filled", "refilled"))
        with nc.Block() as block:
            @block.vector
            def _(dve):
                dve.memset(key_i[:, :], NP).then_inc(zeroed, 1)
                for r in raw:
                    dve.memset(r[:, :], 0).then_inc(zeroed, 1)
                dve.memset(fill[:, :, :], 0.0)
                dve.drain()
                dve.memset(fill[:, :, 0:1], -1.0).then_inc(filled, 1)
                dve.memset(recs[:, :, :], 0.0)
                dve.wait_ge(loaded, 32 * (1 + len(raw)))
                dve.tensor_scalar(tmp_i[:, :], key_i[:, :], 7, None, ALU.logical_shift_right)
                dve.drain()
                dve.tensor_copy(blk[:, :], tmp_i[:, :])
                dve.drain()
                dve.tensor_scalar(tmp_i[:, :], key_i[:, :], P - 1, None, ALU.bitwise_and)
                dve.drain()
                dve.tensor_copy(recs[:, :, 0], tmp_i[:, :])
                o = 1
                for r, (_, w, _) in zip(raw, fields):
                    dve.tensor_copy(recs[:, :, o:o + w], r[:, :].rearrange("p (l w) -> p l w", w=w))
                    o += w

            @block.sync
            def _(sp):
                sp.wait_ge(zeroed, 1 + len(raw))
                for tile, (src, w, _) in zip([key_i] + raw, [(key, 1, I32)] + list(fields)):
                    sp.dma_start(tile[0:FULL, :], src[0:FULL * L * w].rearrange("(p l) -> p l", l=L * w)).then_inc(loaded, 16)
                    sp.dma_start(tile[FULL:FULL + 1, 0:REST * w], src[FULL * L * w:E * w].rearrange("(a l) -> a l", a=1)).then_inc(loaded, 16)
                sp.wait_ge(filled, 1)
                fill_rows = rec.rearrange("(n p r) w -> n p r w", p=P, r=152)
                for n in range(fill_rows.shape[0]):
                    sp.dma_start(fill_rows[n], fill[:, :, :]).then_inc(refilled, 16)
                sp.wait_ge(refilled, 16 * fill_rows.shape[0])

        taken, hot, counted = ([ph.sem(f"{n}{q}") for q in range(2)] for n in ("taken", "hot", "counted"))
        iota_bins = k["iota"][:, 0:NBIN].unsqueeze(1).to_broadcast([P, SC, NBIN])

        with nc.Block() as block:
            @block.scalar
            def _(act):
                with act.Fori(0, SN // 2) as i:
                    for q in range(2):
                        act.wait_ge(hot[q], i)
                        act.activation(step_blk[:, q], part(blk, i * 2 + q, SC), ACT.Copy).then_inc(taken[q], 1)

            @block.vector
            def _(dve):
                with dve.Fori(0, SN // 2) as i:
                    done = dve.snap(i + 1)
                    for q in range(2):
                        dve.wait_ge(taken[q], done)
                        dve.wait_ge(counted[q], i)
                        dve.tensor_tensor(onehot[:, q], iota_bins,
                                          step_blk[:, q].unsqueeze(2).to_broadcast([P, SC, NBIN]),
                                          ALU.is_equal).then_inc(hot[q], 1)

            @block.tensor
            def _(pe):
                def step(i, first, last):
                    for q in range(2):
                        pe.wait_ge(hot[q], i + 1)
                        for j in range(SC):
                            ins = pe.matmul(hist[0:NBIN, 0:1], onehot[:, q, j, :], k["ones_b"][:, 0:1],
                                            start=first and q == 0 and j == 0, stop=last and q == 1 and j == SC - 1,
                                            skip_group_check=True)
                        ins.then_inc(counted[q], 1)
                step(0, True, False)
                with pe.Fori(1, SN // 2 - 1) as i:
                    step(i, False, False)
                step(SN // 2 - 1, False, True)

        tiles, start, end, is_pad, not_pad = (small[0:NBIN, n:n + 1] for n in range(5))
        tiles_ready, start_found, start_ready, spread_done, spread_read, keep_found, ended_ready, ended_found = (
            ph.sem(n) for n in ("tiles_ready", "start_found", "start_ready", "spread_done", "spread_read",
                                "keep_found", "ended_ready", "ended_found"))
        with nc.Block() as block:
            @block.vector
            def _(dve):
                dve.tensor_scalar(small_i[0:NBIN, 0:1], hist[0:NBIN, 0:1], 1.0, float(P - 1), ALU.max, ALU.add)
                dve.tensor_scalar(is_pad, k["part"][0:NBIN, :], float(NB), None, ALU.is_equal)
                dve.drain()
                dve.tensor_scalar(small_i[0:NBIN, 1:2], small_i[0:NBIN, 0:1], 7, None, ALU.logical_shift_right)
                dve.tensor_scalar(not_pad, is_pad, -1.0, 1.0, ALU.mult, ALU.add)
                dve.drain()
                dve.tensor_copy(tiles, small_i[0:NBIN, 1:2]).then_inc(tiles_ready, 1)
                dve.wait_ge(start_found, 1)
                dve.tensor_tensor(start, rank[0][0:NBIN, 0:1], not_pad, ALU.mult)
                dve.drain()
                dve.scalar_tensor_tensor(start, is_pad, float(T), start, ALU.mult, ALU.add)
                dve.drain()
                dve.tensor_tensor(end, start, tiles, ALU.add)
                dve.tensor_scalar(spread[0:NB, :], k["iota"][0:NB, :], small[0:NB, 1:2], None, ALU.is_equal)
                dve.drain().then_inc(start_ready, 1)
                dve.wait_ge(spread_done, 1)
                dve.tensor_scalar(base[:, :], rank[1][:, 0:NBIN], float(P), None, ALU.mult)
                dve.tensor_scalar(last_i[:, 0, :], rank[2][:, 0:NB], -1.0, None, ALU.add)
                dve.drain().then_inc(spread_read, 1)
                dve.tensor_scalar(last_i[:, 1, :], last_i[:, 0, :], 3, 10, ALU.logical_shift_right, ALU.logical_shift_left)
                dve.drain()
                dve.tensor_scalar(last_i[:, 0, :], last_i[:, 0, :], CH - 1, None, ALU.bitwise_and)
                dve.tensor_scalar(small_i[:, 3:4], k["part_i"][:, :], 3, None, ALU.logical_shift_left)
                dve.drain()
                dve.tensor_tensor(last_i[:, 1, :], last_i[:, 1, :], last_i[:, 0, :], ALU.bitwise_or)
                dve.drain()
                dve.tensor_tensor(k["last"][:, :], last_i[:, 1, :], small_i[:, 3:4].to_broadcast([P, NB]), ALU.bitwise_or)
                dve.wait_ge(keep_found, 1)
                for n in range(4):
                    dve.tensor_scalar(k["keep"][:, n * (T // 4):(n + 1) * (T // 4)], rank[n][:, 0:T // 4], -1.0, 1.0,
                                      ALU.mult, ALU.add)
                dve.tensor_scalar(spread[0:NB, :], k["iota"][0:NB, :], small[0:NB, 2:3], None,
                                  ALU.is_ge).then_inc(ended_ready, 1)
                dve.wait_ge(ended_found, 1)
                dve.tensor_scalar(k["tile_block"][:, :], total[:, 0:T // P], float(NB - 1), None, ALU.min)

            @block.tensor
            def _(pe):
                pe.wait_ge(tiles_ready, 1)
                pe.matmul(rank[0][0:NBIN, 0:1], k["before"][0:NBIN, 0:NBIN], tiles, start=True,
                          stop=True).then_inc(start_found, 1)
                pe.wait_ge(start_ready, 1)
                pe.matmul(rank[1][:, 0:NBIN], start.to_broadcast([NBIN, P]), k["ident"][0:NBIN, 0:NBIN],
                          start=True, stop=True)
                pe.matmul(rank[2][:, 0:NB], small[0:NB, 2:3].to_broadcast([NB, P]), k["ident"][0:NB, 0:NB],
                          start=True, stop=True).then_inc(spread_done, 1)
                pe.wait_ge(spread_read, 1)
                for n in range(4):
                    ins = pe.matmul(rank[n][:, 0:T // 4], k["ones"][0:NB, :],
                                    spread[0:NB, n * (T // 4):(n + 1) * (T // 4)], start=True, stop=True)
                ins.then_inc(keep_found, 1)
                pe.wait_ge(ended_ready, 1)
                for n in range(T // P):
                    ins = pe.matmul(total[:, n:n + 1], spread[0:NB, n * P:(n + 1) * P], k["ones"][0:NB, 0:1],
                                    start=True, stop=True)
                ins.then_inc(ended_found, 1)

        G = SC // 4
        step_taken, step_hot, step_ranked, step_placed, scattered = (
            [ph.sem(f"{n}{q}") for q in range(2)] for n in ("st", "sh", "sr", "sp", "sc"))
        with nc.Block() as block:
            @block.scalar
            def _(act):
                with act.Fori(0, SN // 2) as i:
                    gone = act.snap(i * (16 * SC))
                    for q in range(2):
                        act.wait_ge(step_placed[q], i)
                        act.wait_ge(scattered[q], gone)
                        act.activation(step_blk[:, q], part(blk, i * 2 + q, SC), ACT.Copy)
                        act.activation(step_rec[:, q], part(recs, i * 2 + q, SC), ACT.Copy).then_inc(step_taken[q], 1)

            @block.vector
            def _(dve):
                with dve.Fori(0, SN // 2) as i:
                    done = dve.snap(i + 1)
                    gone = dve.snap(i * (16 * SC))
                    for q in range(2):
                        dve.wait_ge(step_taken[q], done)
                        dve.tensor_tensor(onehot[:, q], iota_bins,
                                          step_blk[:, q].unsqueeze(2).to_broadcast([P, SC, NBIN]),
                                          ALU.is_equal).then_inc(step_hot[q], 1)
                        dve.wait_ge(step_ranked[q], done)
                        for g in range(4):
                            dve.tensor_tensor(ranked[:, g * G:(g + 1) * G, :],
                                              rank[g][:, 0:G * NBIN].rearrange("p (j b) -> p j b", b=NBIN),
                                              base[:, :].unsqueeze(1).to_broadcast([P, G, NBIN]), ALU.add)
                        dve.drain()
                        dve.tensor_tensor(ranked[:, :, :], ranked[:, :, :], onehot[:, q], ALU.mult)
                        dve.tensor_tensor(base[:, :], base[:, :], total[:, 0:NBIN], ALU.add)
                        dve.drain()
                        dve.tensor_reduce(pos[:, :], ranked[:, :, :], axis=AX, op=ALU.add)
                        dve.drain()
                        dve.tensor_copy(pos_i[:, 0, :], pos[:, :])
                        dve.drain()
                        dve.tensor_scalar(pos_i[:, 1, :], pos_i[:, 0, :], 10, 10, ALU.logical_shift_right,
                                          ALU.logical_shift_left)
                        dve.tensor_scalar(pos_i[:, 2, :], pos_i[:, 0, :], P - 1, 3, ALU.bitwise_and,
                                          ALU.logical_shift_left)
                        dve.tensor_scalar(pos_i[:, 3, :], pos_i[:, 0, :], 7, CH - 1, ALU.logical_shift_right,
                                          ALU.bitwise_and)
                        dve.drain()
                        dve.tensor_tensor(pos_i[:, 1, :], pos_i[:, 1, :], pos_i[:, 2, :], ALU.bitwise_or)
                        dve.drain()
                        dve.wait_ge(scattered[q], gone)
                        dve.tensor_tensor(row[:, q, :], pos_i[:, 1, :], pos_i[:, 3, :],
                                          ALU.bitwise_or).then_inc(step_placed[q], 1)

            @block.tensor
            def _(pe):
                with pe.Fori(0, SN // 2) as i:
                    done = pe.snap(i + 1)
                    for q in range(2):
                        pe.wait_ge(step_hot[q], done)
                        pe.wait_ge(step_placed[1 - q], done if q else i)
                        hots = onehot[:, q]
                        for g in range(4):
                            out = rank[g]
                            pe.matmul(out[:, 0:G * NBIN], k["before_b"][:, :],
                                      hots[:, g * G:(g + 1) * G, :].rearrange("p j b -> p (j b)"),
                                      start=True, stop=False, skip_group_check=True)
                            for j in range(g * G + G - 1):
                                lo = max(0, j - g * G + 1)
                                pe.matmul(out[:, lo * NBIN:G * NBIN], k["ones_b"][:, :],
                                          hots[:, j:j + 1, :].to_broadcast([P, G - lo, NBIN]),
                                          start=False, stop=j == g * G + G - 2, skip_group_check=True)
                        for j in range(SC):
                            ins = pe.matmul(total[:, 0:NBIN], k["ones_b"][:, :], hots[:, j, :],
                                            start=j == 0, stop=j == SC - 1)
                        ins.then_inc(step_ranked[q], 1)

            @block.gpsimd
            def _(pool):
                with pool.Fori(0, SN // 2) as i:
                    done = pool.snap(i + 1)
                    for q in range(2):
                        pool.wait_ge(step_placed[q], done)
                        pool.wait_ge(step_taken[q], done)
                        pool.nop(nofuse=True)
                        for j in range(SC):
                            pool.indirect_dma_start(
                                out=rec, out_offset=bass.IndirectOffsetOnAxis(ap=row[:, q, j:j + 1], axis=0),
                                in_=step_rec[:, q, j, :], in_offset=None).then_inc(scattered[q], 16)
                for q in range(2):
                    pool.wait_ge(scattered[q], 16 * SC * (SN // 2))


R1 = dict(lo=0, col=8, keep=16, hats=24, words=144)
R2 = dict(lo=0, keep=8, idx=(16, 24), w=32, words=96)
R3 = dict(lo=0, keep=8, idx=(16,), w=24, words=88)
R4 = dict(lo=0, keep=8, col=16, w=24, words=32)


def piece_of(dram, i):
    return dram[bass.ds(i * PIECE, PIECE)].rearrange("c p w -> p c w")


def cells(ph):
    return {"pos": ph.sb("pos", [P, PT, 3]), "in": ph.sb("in", [P, PT, 3]), "whole": ph.sb("whole", [P, PT, 3], I32),
            "cell": ph.sb("cell", [P, PT, 3]), "w2": ph.sb("w2", [P, PT, 3, 2]), "bc": ph.sb("bc", [P, PT, 2, 2])}


def spline_cells(dve, u, s):
    dve.tensor_scalar(s["pos"][:, :, :], u, 4.0, None, ALU.mult)
    dve.drain()
    dve.tensor_scalar(s["in"][:, :, :], s["pos"][:, :, :], 0.0, 3.5, ALU.max, ALU.min)
    dve.drain()
    dve.tensor_copy(s["whole"][:, :, :], s["in"][:, :, :])
    dve.drain()
    dve.tensor_tensor(s["cell"][:, :, :], s["whole"][:, :, :], s["in"][:, :, :], ALU.is_gt)
    dve.drain()
    dve.tensor_tensor(s["cell"][:, :, :], s["whole"][:, :, :], s["cell"][:, :, :], ALU.subtract)
    dve.drain()
    dve.tensor_tensor(s["w2"][:, :, :, 1], s["pos"][:, :, :], s["cell"][:, :, :], ALU.subtract)
    dve.drain()
    dve.tensor_scalar(s["w2"][:, :, :, 0], s["w2"][:, :, :, 1], -1.0, 1.0, ALU.mult, ALU.add)
    dve.drain()
    dve.tensor_tensor(s["bc"][:, :, :, :], s["w2"][:, :, 1, :].unsqueeze(3).to_broadcast([P, PT, 2, 2]),
                      s["w2"][:, :, 2, :].unsqueeze(2).to_broadcast([P, PT, 2, 2]), ALU.mult)
    dve.drain()


def prepare_by_source(nc, k, rec, r1, r2):
    with Phase(nc, "pa") as ph:
        r = ph.sb("r", [P, PT, WA])
        s = cells(ph)
        knots = ph.sb("knots", [P, PT * 3, 5])
        low = ph.sb("low", [P, PT * 3, 5])
        odd, even, w_a, t0, t1, t2 = (ph.sb(n, [P, PT]) for n in ("odd", "even", "w_a", "t0", "t1", "t2"))
        ends = ph.sb("ends", [P, PT, 2])
        corners = ph.sb("corners", [P, PT, 2, 4])
        one = ph.sb("one", [P, PIECE, R1["words"]])
        two = ph.sb("two", [P, PIECE, R2["words"]])
        loaded, computed, packed, stored = (ph.sem(n) for n in ("loaded", "computed", "packed", "stored"))
        rec3 = rec.rearrange("(c p t) w -> c p (t w)", p=P, t=CH)

        def by_chunk(ap):
            return ap.rearrange("p (c t) -> p c t", t=CH)

        with nc.Block() as block:
            @block.sync
            def _(sp):
                with sp.Fori(0, NC // PIECE) as i:
                    sp.wait_ge(packed, i)
                    sp.dma_start(r[:, :, :].rearrange("p (c t) w -> p c (t w)", t=CH), piece_of(rec3, i)).then_inc(loaded, 16)
                    sp.wait_ge(packed, i + 1)
                    sp.dma_start(piece_of(r1, i), one[:, :, :]).then_inc(stored, 16)
                    sp.dma_start(piece_of(r2, i), two[:, :, :]).then_inc(stored, 16)
                sp.wait_ge(stored, 32 * (NC // PIECE))

            @block.vector
            def _(dve):
                with dve.Fori(0, NC // PIECE) as i:
                    dve.wait_ge(loaded, (i + 1) * 16)
                    dve.wait_ge(packed, i)
                    dve.wait_ge(stored, i * 32)
                    lo, col = r[:, :, 0], r[:, :, 1]
                    spline_cells(dve, r[:, :, 2:5], s)
                    cell = s["cell"][:, :, :].rearrange("p t a -> p (t a)").unsqueeze(2)
                    w2 = s["w2"][:, :, :, :].rearrange("p t a w -> p (t a) w")
                    dve.tensor_tensor(low[:, :, :], k["iota"][:, 0:5].unsqueeze(1).to_broadcast([P, PT * 3, 5]),
                                      cell.to_broadcast([P, PT * 3, 5]), ALU.is_equal)
                    dve.drain()
                    dve.tensor_tensor(knots[:, :, :], low[:, :, :], w2[:, :, 0:1].to_broadcast([P, PT * 3, 5]), ALU.mult)
                    dve.drain()
                    dve.tensor_tensor(low[:, :, 0:4], low[:, :, 0:4], w2[:, :, 1:2].to_broadcast([P, PT * 3, 4]), ALU.mult)
                    dve.drain()
                    dve.tensor_tensor(knots[:, :, 1:5], knots[:, :, 1:5], low[:, :, 0:4], ALU.add)
                    ia, ib, ic = (s["cell"][:, :, n] for n in range(3))
                    dve.tensor_scalar(t0[:, :], ia, 3.0, None, ALU.is_equal)
                    dve.drain()
                    dve.scalar_tensor_tensor(odd[:, :], ia, 1.0, t0[:, :], ALU.is_equal, ALU.add)
                    dve.drain()
                    dve.tensor_scalar(even[:, :], odd[:, :], -1.0, 1.0, ALU.mult, ALU.add)
                    dve.drain()
                    lo_w, hi_w = s["w2"][:, :, 0, 0], s["w2"][:, :, 0, 1]
                    dve.tensor_tensor(t0[:, :], lo_w, even[:, :], ALU.mult)
                    dve.tensor_tensor(t1[:, :], hi_w, odd[:, :], ALU.mult)
                    dve.tensor_tensor(t2[:, :], lo_w, odd[:, :], ALU.mult)
                    dve.tensor_tensor(w_a[:, :], hi_w, even[:, :], ALU.mult)
                    dve.drain()
                    dve.tensor_tensor(ends[:, :, 0], t0[:, :], t1[:, :], ALU.add)
                    dve.tensor_tensor(ends[:, :, 1], t2[:, :], w_a[:, :], ALU.add)
                    dve.drain()
                    dve.tensor_tensor(corners[:, :, :, :], ends[:, :, :].unsqueeze(3).to_broadcast([P, PT, 2, 4]),
                                      s["bc"][:, :, :, :].rearrange("p t b c -> p t (b c)").unsqueeze(2).to_broadcast([P, PT, 2, 4]),
                                      ALU.mult)
                    dve.scalar_tensor_tensor(t2[:, :], ib, 5.0, ic, ALU.mult, ALU.add)
                    dve.tensor_tensor(t0[:, :], ia, odd[:, :], ALU.add)
                    dve.tensor_tensor(t1[:, :], ia, odd[:, :], ALU.subtract)
                    dve.drain()
                    dve.scalar_tensor_tensor(t0[:, :], t0[:, :], 12.5, t2[:, :], ALU.mult, ALU.add)
                    dve.scalar_tensor_tensor(t1[:, :], t1[:, :], 12.5, t2[:, :], ALU.mult, ALU.add)
                    dve.drain()
                    for n, (t, rows) in enumerate(((t0, 75.0), (t1, 50.0))):
                        o = R2["idx"][n]
                        dve.scalar_tensor_tensor(two[:, :, o:o + CH].bitcast(I32), by_chunk(col), rows, by_chunk(t[:, :]),
                                                 ALU.mult, ALU.add)
                    dve.tensor_copy(one[:, :, R1["col"]:R1["col"] + CH].bitcast(I32), by_chunk(col))
                    for dst, rr in ((one, R1), (two, R2)):
                        dve.tensor_copy(dst[:, :, rr["lo"]:rr["lo"] + CH], by_chunk(lo))
                        dve.tensor_copy(dst[:, :, rr["keep"]:rr["keep"] + CH], by_chunk(part(k["keep"], i, PT)))
                    dve.drain().then_inc(computed, 1)

            @block.scalar
            def _(act):
                with act.Fori(0, NC // PIECE) as i:
                    act.wait_ge(computed, i + 1)
                    act.activation(one[:, :, R1["hats"]:], knots[:, :, :].rearrange("p (c t) n -> p c (t n)", t=CH * 3), ACT.Copy)
                    act.activation(two[:, :, R2["w"]:], corners[:, :, :, :].rearrange("p (c t) a w -> p c (t a w)", t=CH), ACT.Copy)
                    act.drain().then_inc(packed, 1)


def prepare_moved(nc, k, r1, moved, r3):
    with Phase(nc, "pm") as ph:
        old = ph.sb("old", [P, PIECE, 24])
        u = ph.sb("u", [P, PIECE, CH * 3])
        s = cells(ph)
        t0 = ph.sb("t0", [P, PT])
        corners = ph.sb("corners", [P, PT, 2, 4])
        out = ph.sb("out", [P, PIECE, R3["words"]])
        loaded, computed, packed, stored = (ph.sem(n) for n in ("loaded", "computed", "packed", "stored"))
        with nc.Block() as block:
            @block.sync
            def _(sp):
                with sp.Fori(0, NC // PIECE) as i:
                    sp.wait_ge(packed, i)
                    sp.dma_start(old[:, :, :], piece_of(r1[:, :, 0:24], i)).then_inc(loaded, 16)
                    sp.dma_start(u[:, :, :], piece_of(moved, i)).then_inc(loaded, 16)
                    sp.wait_ge(packed, i + 1)
                    sp.dma_start(piece_of(r3, i), out[:, :, :]).then_inc(stored, 16)
                sp.wait_ge(stored, 16 * (NC // PIECE))

            @block.vector
            def _(dve):
                with dve.Fori(0, NC // PIECE) as i:
                    dve.wait_ge(loaded, (i + 1) * 32)
                    dve.wait_ge(packed, i)
                    dve.wait_ge(stored, i * 16)
                    spline_cells(dve, u[:, :, :].rearrange("p c (t a) -> p (c t) a", a=3), s)
                    dve.tensor_tensor(corners[:, :, :, :], s["w2"][:, :, 0, :].unsqueeze(3).to_broadcast([P, PT, 2, 4]),
                                      s["bc"][:, :, :, :].rearrange("p t b c -> p t (b c)").unsqueeze(2).to_broadcast([P, PT, 2, 4]),
                                      ALU.mult)
                    ia, ib, ic = (s["cell"][:, :, n] for n in range(3))
                    dve.scalar_tensor_tensor(t0[:, :], ib, 5.0, ic, ALU.mult, ALU.add)
                    dve.drain()
                    dve.scalar_tensor_tensor(t0[:, :], ia, 25.0, t0[:, :], ALU.mult, ALU.add)
                    dve.drain()
                    o = R3["idx"][0]
                    dve.scalar_tensor_tensor(out[:, :, o:o + CH].bitcast(I32), old[:, :, R1["col"]:R1["col"] + CH].bitcast(I32),
                                             125.0, t0[:, :].rearrange("p (c t) -> p c t", t=CH), ALU.mult, ALU.add)
                    dve.tensor_copy(out[:, :, 0:CH], old[:, :, 0:CH])
                    dve.tensor_copy(out[:, :, R3["keep"]:R3["keep"] + CH], old[:, :, R1["keep"]:R1["keep"] + CH])
                    dve.drain().then_inc(computed, 1)

            @block.scalar
            def _(act):
                with act.Fori(0, NC // PIECE) as i:
                    act.wait_ge(computed, i + 1)
                    act.activation(out[:, :, R3["w"]:], corners[:, :, :, :].rearrange("p (c t) a w -> p c (t a w)", t=CH), ACT.Copy)
                    act.drain().then_inc(packed, 1)


def prepare_by_target(nc, k, rec, r4):
    with Phase(nc, "pb") as ph:
        r = ph.sb("r", [P, PT, WB])
        out = ph.sb("out", [P, PIECE, R4["words"]])
        loaded, packed, stored = (ph.sem(n) for n in ("loaded", "packed", "stored"))
        rec3 = rec.rearrange("(c p t) w -> c p (t w)", p=P, t=CH)
        with nc.Block() as block:
            @block.sync
            def _(sp):
                with sp.Fori(0, NC // PIECE) as i:
                    sp.wait_ge(packed, i)
                    sp.dma_start(r[:, :, :].rearrange("p (c t) w -> p c (t w)", t=CH), piece_of(rec3, i)).then_inc(loaded, 16)
                    sp.wait_ge(packed, i + 1)
                    sp.dma_start(piece_of(r4, i), out[:, :, :]).then_inc(stored, 16)
                sp.wait_ge(stored, 16 * (NC // PIECE))

            @block.vector
            def _(dve):
                with dve.Fori(0, NC // PIECE) as i:
                    dve.wait_ge(loaded, (i + 1) * 16)
                    dve.wait_ge(stored, i * 16)
                    for o, field in ((R4["lo"], 0), (R4["w"], 2)):
                        dve.tensor_copy(out[:, :, o:o + CH], r[:, :, field].rearrange("p (c t) -> p c t", t=CH))
                    dve.tensor_copy(out[:, :, R4["col"]:R4["col"] + CH].bitcast(I32), r[:, :, 1].rearrange("p (c t) -> p c t", t=CH))
                    dve.tensor_copy(out[:, :, R4["keep"]:R4["keep"] + CH],
                                    part(k["keep"], i, PT).rearrange("p (c t) -> p c t", t=CH))
                    dve.drain().then_inc(packed, 1)


class Count:

    def __init__(self, eng, i):
        self.eng, self.i, self.known = eng, i, {}

    def __call__(self, times, more):
        if (times, more) not in self.known:
            v = (self.i + more) * times
            self.known[times, more] = v if isinstance(v, int) else self.eng.snap(v)
        return self.known[times, more]


def wait(eng, sem, value):
    if not isinstance(value, int) or value > 0:
        eng.wait_ge(sem, value)


def stages(eng, steps):
    def body(c, first, last):
        for q in range(RING):
            for lag, step in steps:
                if (first and q < lag) or (last and q >= lag):
                    continue
                step(c, (q - lag) % RING, 1 if q >= lag else 0)
    body(Count(eng, 0), True, False)
    with eng.Fori(1, NI) as i:
        body(Count(eng, i), False, False)
    body(Count(eng, NI), False, True)


def two_before(q, m):
    return (q + 2) % RING, m if q >= 2 else m - 1


def banks_of(ph, name, width):
    per = min(CH, 512 // width)
    tiles = [[ph.ps(f"{name}{r}_{b}", [P, 512]) for b in range(-(-CH // per))] for r in range(2)]
    return lambda r, j: tiles[r][j // per][:, (j % per) * width:(j % per + 1) * width]


def segment_pass(nc, name, k, rec, r, gathers, outs, products, prepare=None, weigh=None, scale=None):
    words, ng = r["words"], len(gathers)
    with Phase(nc, name) as ph:
        recs = ph.sb("recs", [P, RING, words])
        rows = [ph.sb(f"rows{n}", [P, 2, CH, run]) for n, (_, _, run) in enumerate(gathers)]
        onehot = ph.sb("onehot", [P, 2, CH, P])
        carried = [ph.sb(f"carried{n}", [P, 2, CH, w]) for n, (w, _) in enumerate(outs)]
        sums = [banks_of(ph, f"sums{n}", w) for n, (w, _) in enumerate(outs)]
        extra = prepare(ph) if prepare else None
        loaded, gathered, built, summed, chained, stored = (
            ph.ring(n) for n in ("ld", "ga", "bu", "su", "ch", "st"))
        GATHERED, STORED = 16 * CH * ng, 16 * len(outs)

        with nc.Block() as block:
            @block.sync
            def _(sp):
                def load(c, q, m):
                    wait(sp, chained[q], c(1, m - 1))
                    sp.dma_start(recs[:, q, :], at(rec, chunk(c, q, m))).then_inc(loaded[q], 16)
                stages(sp, [(0, load)])

            @block.gpsimd
            def _(pool):
                def gather(c, q, m):
                    free, n = two_before(q, m)
                    pool.wait_ge(loaded[q], c(16, m))
                    wait(pool, summed[free], c(1, n))
                    pool.nop(nofuse=True)
                    for j in range(CH):
                        for (table, col, run), dst in zip(gathers, rows):
                            pool.indirect_dma_start(
                                out=dst[:, q % 2, j, :], out_offset=None, in_=table,
                                in_offset=bass.IndirectOffsetOnAxis(ap=recs[:, q, col + j:col + j + 1].bitcast(I32), axis=0),
                            ).then_inc(gathered[q], 16)
                stages(pool, [(0, gather)])

            @block.vector
            def _(dve):
                for t in carried:
                    dve.memset(t[:, :, :, :], 0.0)
                if extra:
                    extra["init"](dve)
                dve.drain()

                def build(c, q, m):
                    free, n = two_before(q, m)
                    dve.wait_ge(loaded[q], c(16, m))
                    wait(dve, summed[free], c(1, n))
                    for j in range(CH):
                        lo = recs[:, q, r["lo"] + j:r["lo"] + j + 1]
                        if scale is None:
                            dve.tensor_scalar(onehot[:, q % 2, j, :], k["iota"][:, 0:P], lo, None, ALU.is_equal)
                        else:
                            dve.tensor_scalar(onehot[:, q % 2, j, :], k["iota"][:, 0:P], lo,
                                              recs[:, q, scale + j:scale + j + 1], ALU.is_equal, ALU.mult)
                    if extra:
                        extra["build"](dve, recs[:, q, :], q % 2)
                    if weigh:
                        dve.wait_ge(gathered[q], c(GATHERED, m))
                        weigh(dve, recs[:, q, :], [t[:, q % 2] for t in rows])
                    dve.drain().then_inc(built[q], 1)

                def chain(c, q, m):
                    free, n = two_before(q, m)
                    dve.wait_ge(summed[q], c(1, m))
                    wait(dve, stored[free], c(STORED, n))
                    for j in range(CH):
                        for t, s in zip(carried, sums):
                            before = t[:, q % 2, j - 1, :] if j else t[:, 1 - q % 2, CH - 1, :]
                            dve.scalar_tensor_tensor(t[:, q % 2, j, :], before, recs[:, q, r["keep"] + j:r["keep"] + j + 1],
                                                     s(q % 2, j), ALU.mult, ALU.add)
                        last = dve.drain()
                    last.then_inc(chained[q], 1)
                stages(dve, [(0, build), (1, chain)])

            @block.tensor
            def _(pe):
                def multiply(c, q, m):
                    free, n = two_before(q, m)
                    pe.wait_ge(built[q], c(1, m))
                    pe.wait_ge(gathered[q], c(GATHERED, m))
                    wait(pe, chained[free], c(1, n))
                    for j in range(CH):
                        for out, operands in enumerate(products([t[:, q % 2, j] for t in rows], q % 2, j, extra)):
                            for a, rhs in enumerate(operands):
                                ins = pe.matmul(sums[out](q % 2, j), onehot[:, q % 2, j, :], rhs,
                                                start=a == 0, stop=a == len(operands) - 1)
                    ins.then_inc(summed[q], 1)
                stages(pe, [(0, multiply)])

            @block.scalar
            def _(act):
                def store(c, q, m):
                    act.wait_ge(chained[q], c(1, m))
                    for t, (w, dram) in zip(carried, outs):
                        act.dma_start(at(dram, chunk(c, q, m)), t[:, q % 2].rearrange("p j w -> p (j w)")).then_inc(stored[q], 16)
                stages(act, [(0, store)])
                for q in range(RING):
                    act.wait_ge(stored[q], STORED * NI)


def chunk(c, q, m):
    return (c.i + (m - 1)) * RING + q


def block_sums(nc, name, k, results):
    with Phase(nc, name) as ph:
        got = ph.sem("got")
        with nc.Block() as block:
            @block.gpsimd
            def _(pool):
                for w, dram, tile in results:
                    rows = dram.rearrange("c p (j w) -> (c p j) w", w=w)
                    for b in range(NB):
                        pool.indirect_dma_start(out=tile[:, b, :], out_offset=None, in_=rows,
                                                in_offset=bass.IndirectOffsetOnAxis(ap=k["last"][:, b:b + 1], axis=0)
                                                ).then_inc(got, 16)
                pool.wait_ge(got, 16 * NB * len(results))


def corner_products(spans, run):
    def of(rows, r, j, extra):
        return [[t[:, o * run:(o + 1) * run] for t, offsets in zip(rows, spans) for o in offsets]]
    return of


def weigh_corners(r, spans, run):
    def of(dve, rec, rows):
        w = rec[:, r["w"]:r["w"] + 8 * CH]
        for j in range(CH):
            n = 0
            for t, groups in zip(rows, spans):
                for o in groups:
                    for b in range(2):
                        first = (o + 5 * b) * run
                        v = t[:, j, first:first + 2 * run].rearrange("p (c f) -> p c f", f=run)
                        dve.tensor_tensor(v, v, w[:, 8 * j + n:8 * j + n + 2].unsqueeze(2).to_broadcast([P, 2, run]), ALU.mult)
                        n += 2
    return of


def transform(nc, name, k, src, K, weights, M, dst):
    G = 7
    per = 512 // M
    with Phase(nc, name) as ph:
        taken = ph.sb("taken", [P, G, K])
        turned = ph.sb("turned", [P, G * P])
        t_ps = [ph.ps(f"t{n}", [P, 512]) for n in range(2)]
        o_ps = [ph.ps(f"o{n}", [P, 512]) for n in range(-(-G // per))]
        copied, transposed, moved, multiplied, out_copied = (
            ph.sem(n) for n in ("copied", "transposed", "moved", "multiplied", "out_copied"))
        with nc.Block() as block:
            @block.scalar
            def _(act):
                with act.Fori(0, NB // G) as i:
                    done = act.snap(i + 1)
                    act.wait_ge(transposed, i)
                    act.activation(taken[:, :, :], part(src, i, G)[:, :, 0:K], ACT.Copy).then_inc(copied, 1)
                    act.wait_ge(multiplied, done)
                    for n, o in enumerate(o_ps):
                        g = min(per, G - n * per)
                        act.activation(dst[:, bass.ds(i * G + n * per, g), :],
                                       o[:, 0:g * M].rearrange("p (g m) -> p g m", m=M), ACT.Copy)
                    act.drain().then_inc(out_copied, 1)

            @block.vector
            def _(dve):
                with dve.Fori(0, NB // G) as i:
                    dve.wait_ge(transposed, i + 1)
                    dve.wait_ge(multiplied, i)
                    dve.tensor_copy(turned[0:K, 0:4 * P], t_ps[0][0:K, :])
                    dve.tensor_copy(turned[0:K, 4 * P:], t_ps[1][0:K, 0:(G - 4) * P])
                    dve.drain().then_inc(moved, 1)

            @block.tensor
            def _(pe):
                with pe.Fori(0, NB // G) as i:
                    done = pe.snap(i + 1)
                    pe.wait_ge(copied, done)
                    pe.nop(nofuse=True)
                    for g in range(G):
                        ins = pe.transpose(t_ps[g // 4][0:K, (g % 4) * P:(g % 4 + 1) * P], taken[:, g, :], k["ident"][:, :])
                    ins.then_inc(transposed, 1)
                    pe.wait_ge(moved, done)
                    pe.wait_ge(out_copied, i)
                    for g in range(G):
                        ins = pe.matmul(o_ps[g // per][:, (g % per) * M:(g % per + 1) * M],
                                        turned[0:K, g * P:(g + 1) * P], weights, start=True, stop=True)
                    ins.then_inc(multiplied, 1)


def node_tables(nc, name, k, src, K, weights, cols, tables):
    STEP = 500
    NG = cols // (2 * STEP)
    ND = len(tables)
    with Phase(nc, name) as ph:
        taken = ph.sb("taken", [P, 2, K])
        turned = ph.sb("turned", [P, 2, P])
        z = [ph.sb(f"z{r}", [P, cols]) for r in range(2)]
        t_ps = ph.ps("t", [P, 512])
        z_ps = [[ph.ps(f"z{a}{b}", [P, 512]) for b in range(2)] for a in range(2)]
        copied, transposed, moved, stored = ([ph.sem(f"{n}{r}") for r in range(2)] for n in ("co", "tr", "mo", "st"))
        made, read = ([[ph.sem(f"{n}{r}{g}") for g in range(NG)] for r in range(2)] for n in ("ma", "re"))
        with nc.Block() as block:
            def evacuate(eng, half, copy):
                def of(i, done, r):
                    eng.wait_ge(stored[r], eng.snap(i * (16 * ND)))
                    for g in range(NG):
                        eng.wait_ge(made[r][g], done)
                        at0 = (2 * g + half) * STEP
                        copy(z[r][:, at0:at0 + STEP], z_ps[g % 2][half][:, 0:STEP]).then_inc(read[r][g], 1)
                return of

            @block.scalar
            def _(act):
                take = evacuate(act, 0, lambda o, s: act.activation(o, s, ACT.Copy))
                with act.Fori(0, NB // 2) as i:
                    done = act.snap(i + 1)
                    for r in range(2):
                        act.wait_ge(transposed[r], i)
                        act.activation(taken[:, r:r + 1, :], src[:, bass.ds(i * 2 + r, 1), 0:K], ACT.Copy).then_inc(copied[r], 1)
                        take(i, done, r)

            @block.vector
            def _(dve):
                take = evacuate(dve, 1, lambda o, s: dve.tensor_copy(o, s))
                with dve.Fori(0, NB // 2) as i:
                    done = dve.snap(i + 1)
                    for r in range(2):
                        dve.wait_ge(transposed[r], done)
                        dve.wait_ge(made[r][NG - 1], i)
                        dve.tensor_copy(turned[0:K, r, :], t_ps[0:K, 0:P]).then_inc(moved[r], 1)
                        take(i, done, r)

            @block.tensor
            def _(pe):
                with pe.Fori(0, NB // 2) as i:
                    done = pe.snap(i + 1)
                    both, both_before = pe.snap(i * 2 + 2), pe.snap(i * 2)
                    for r in range(2):
                        pe.wait_ge(copied[r], done)
                        pe.wait_ge(moved[1 - r], done if r else i)
                        pe.nop(nofuse=True)
                        pe.transpose(t_ps[0:K, 0:P], taken[:, r, :], k["ident"][:, :]).then_inc(transposed[r], 1)
                        pe.wait_ge(moved[r], done)
                        for g in range(NG):
                            if g >= 2:
                                pe.wait_ge(read[r][g - 2], both)
                            else:
                                pe.wait_ge(read[1 - r][NG - 2 + g], both if r else both_before)
                            for half in range(2):
                                at0 = (2 * g + half) * STEP
                                ins = pe.matmul(z_ps[g % 2][half][:, 0:STEP], turned[0:K, r, :],
                                                weights[:, at0:at0 + STEP], start=True, stop=True)
                            ins.then_inc(made[r][g], 1)

            @block.sync
            def _(sp):
                with sp.Fori(0, NB // 2) as i:
                    both = sp.snap(i * 2 + 2)
                    for r in range(2):
                        sp.wait_ge(read[r][NG - 1], both)
                        for columns, table in tables:
                            sp.dma_start(at(table, i * 2 + r), columns(z[r])).then_inc(stored[r], 16)
                for r in range(2):
                    sp.wait_ge(stored[r], 16 * ND * (NB // 2))


def elu(nc, name, h, scale=None, bias=None):
    M = h.shape[2]
    with Phase(nc, name) as ph:
        low = ph.sb("low", [P, NB, M])
        ready, powered = ph.sem("ready"), ph.sem("powered")
        with nc.Block() as block:
            @block.vector
            def _(dve):
                if scale is not None:
                    dve.tensor_tensor(h[:, :, :], h[:, :, :], scale.unsqueeze(2).to_broadcast([P, NB, M]), ALU.mult)
                    dve.drain()
                if bias is not None:
                    dve.tensor_tensor(h[:, :, :], h[:, :, :], bias.unsqueeze(1).to_broadcast([P, NB, M]), ALU.add)
                    dve.drain()
                dve.tensor_scalar(low[:, :, :], h[:, :, :], 0.0, None, ALU.min).then_inc(ready, 1)
                dve.tensor_scalar(h[:, :, :], h[:, :, :], 0.0, None, ALU.max)
                dve.wait_ge(powered, 1)
                dve.drain()
                dve.scalar_tensor_tensor(h[:, :, :], low[:, :, :], -1.0, h[:, :, :], ALU.add, ALU.add)

            @block.scalar
            def _(act):
                act.wait_ge(ready, 1)
                act.activation(low[:, :, :], low[:, :, :], ACT.Exp).then_inc(powered, 1)


def on_vector(nc, name, work):
    with nc.Block() as block:
        @block.vector
        def _(dve):
            work(dve)


def load(nc, name, pairs):
    with Phase(nc, name) as ph:
        moved = ph.sem("moved")
        with nc.Block() as block:
            @block.sync
            def _(sp):
                with nc.allow_non_contiguous_dma(reason="small transposed weights"):
                    for dst, src in pairs:
                        sp.dma_start(dst, src).then_inc(moved, 16)
                sp.wait_ge(moved, 16 * len(pairs))


def by_tile(nc, name, k, table, w, spread):
    with Phase(nc, name) as ph:
        rows = ph.sb("rows", [P, T // P, P * w])
        got, stored = ph.sem("got"), ph.sem("stored")
        blocks = table.rearrange("(b p) w -> b (p w)", p=P)
        with nc.Block() as block:
            @block.gpsimd
            def _(pool):
                for n in range(T // P):
                    pool.indirect_dma_start(out=rows[:, n, :], out_offset=None, in_=blocks,
                                            in_offset=bass.IndirectOffsetOnAxis(ap=k["tile_block"][:, n:n + 1], axis=0)
                                            ).then_inc(got, 16)

            @block.sync
            def _(sp):
                sp.wait_ge(got, 16 * (T // P))
                sp.dma_start(spread.rearrange("(n p) w -> p n w", p=P), rows[:, :, :]).then_inc(stored, 16)
                sp.wait_ge(stored, 16)


def turn_steps(ph, k, recs, lo, loaded, per_load, users_done, onehot, turned, t_ps, hot, transposed, copied):
    def make_hot(dve):
        def step(c, q, m):
            free, n = two_before(q, m)
            dve.wait_ge(loaded[q], c(per_load, m))
            wait(dve, users_done[free], c(1, n))
            for j in range(CH):
                dve.tensor_scalar(onehot[:, q % 2, j, :], k["iota"][:, 0:P], recs[:, q, lo + j:lo + j + 1], None, ALU.is_equal)
            dve.drain().then_inc(hot[q], 1)
        return step

    def transpose(pe):
        def step(c, q, m):
            free, n = two_before(q, m)
            pe.wait_ge(hot[q], c(1, m))
            wait(pe, copied[free], c(1, n))
            for j in range(CH):
                ins = pe.transpose(t_ps[q % 2][j // 4][:, (j % 4) * P:(j % 4 + 1) * P], onehot[:, q % 2, j, :], k["ident"][:, :])
            ins.then_inc(transposed[q], 1)
        return step

    def copy(act):
        def step(c, q, m):
            free, n = two_before(q, m)
            act.wait_ge(transposed[q], c(1, m))
            wait(act, users_done[free], c(1, n))
            for b in range(2):
                act.activation(turned[:, q % 2, b * 4 * P:(b + 1) * 4 * P], t_ps[q % 2][b][:, :], ACT.Copy)
            act.drain().then_inc(copied[q], 1)
        return step
    return make_hot, transpose, copy


def move_pass(nc, k, rec, r1, table, spread, moved):
    W = 4
    with Phase(nc, "mv") as ph:
        recs = ph.sb("recs", [P, RING, 24])
        raw = ph.sb("raw", [P, RING, CH, WA])
        tabs = ph.sb("tabs", [P, RING, CH, W])
        rows = ph.sb("rows", [P, 2, CH, W])
        out = ph.sb("out", [P, 2, CH, 3])
        onehot = ph.sb("onehot", [P, 2, CH, P])
        turned = ph.sb("turned", [P, 2, CH * P])
        t_ps = [[ph.ps(f"t{r}{b}", [P, 512]) for b in range(2)] for r in range(2)]
        l_ps = [ph.ps(f"l{r}", [P, 512]) for r in range(2)]
        loaded, gathered, hot, transposed, copied, looked, finished, stored = (
            ph.ring(n) for n in ("ld", "ga", "ho", "tr", "co", "lo", "fi", "st"))
        make_hot, transpose, copy = turn_steps(ph, k, recs, R1["lo"], loaded, 48, finished, onehot, turned, t_ps,
                                               hot, transposed, copied)
        rec3 = rec.rearrange("(c p t) w -> c p (t w)", p=P, t=CH)
        spread4 = spread.rearrange("(c t) (n w) -> c n t w", t=CH, w=W)
        with nc.Block() as block:
            @block.sync
            def _(sp):
                def step(c, q, m):
                    wait(sp, finished[q], c(1, m - 1))
                    n = chunk(c, q, m)
                    sp.dma_start(recs[:, q, :], at(r1[:, :, 0:24], n)).then_inc(loaded[q], 16)
                    sp.dma_start(raw[:, q].rearrange("p t w -> p (t w)"), at(rec3, n)).then_inc(loaded[q], 16)
                    sp.dma_start(tabs[:, q], at(spread4, n)).then_inc(loaded[q], 16)
                stages(sp, [(0, step)])

            @block.gpsimd
            def _(pool):
                def step(c, q, m):
                    free, n = two_before(q, m)
                    pool.wait_ge(loaded[q], c(48, m))
                    wait(pool, finished[free], c(1, n))
                    pool.nop(nofuse=True)
                    for j in range(CH):
                        o = R1["col"] + j
                        pool.indirect_dma_start(out=rows[:, q % 2, j, :], out_offset=None, in_=table,
                                                in_offset=bass.IndirectOffsetOnAxis(ap=recs[:, q, o:o + 1].bitcast(I32), axis=0)
                                                ).then_inc(gathered[q], 16)
                stages(pool, [(0, step)])

            @block.vector
            def _(dve):
                def finish(c, q, m):
                    free, n = two_before(q, m)
                    dve.wait_ge(gathered[q], c(16 * CH, m))
                    dve.wait_ge(looked[q], c(1, m))
                    wait(dve, stored[free], c(16, n))
                    o = out[:, q % 2]
                    own = l_ps[q % 2][:, 0:CH * W].rearrange("p (t w) -> p t w", w=W)
                    dve.tensor_tensor(o, raw[:, q, :, 2:5], rows[:, q % 2, :, 0:3], ALU.add)
                    dve.drain()
                    dve.tensor_tensor(o, o, own[:, :, 0:3], ALU.subtract)
                    dve.drain()
                    dve.tensor_scalar(o, o, 0.0, 1.0, ALU.max, ALU.min).then_inc(finished[q], 1)
                stages(dve, [(0, make_hot(dve)), (1, finish)])

            @block.tensor
            def _(pe):
                def look_up(c, q, m):
                    free, n = two_before(q, m)
                    pe.wait_ge(copied[q], c(1, m))
                    pe.wait_ge(loaded[q], c(48, m))
                    wait(pe, finished[free], c(1, n))
                    for j in range(CH):
                        ins = pe.matmul(l_ps[q % 2][:, j * W:(j + 1) * W], turned[:, q % 2, j * P:(j + 1) * P], tabs[:, q, j, :],
                                        start=True, stop=True)
                    ins.then_inc(looked[q], 1)
                stages(pe, [(0, transpose(pe)), (1, look_up)])

            @block.scalar
            def _(act):
                def store(c, q, m):
                    act.wait_ge(finished[q], c(1, m))
                    act.dma_start(at(moved, chunk(c, q, m)), out[:, q % 2].rearrange("p t w -> p (t w)")).then_inc(stored[q], 16)
                stages(act, [(0, copy(act)), (1, store)])
                for q in range(RING):
                    act.wait_ge(stored[q], 16 * NI)


def max_pass(nc, k, r4, table, kept_rows, maxima):
    W = D + 4
    HALF = CH // 2
    with Phase(nc, "mx") as ph:
        recs = ph.sb("recs", [P, RING, R4["words"]])
        rows = ph.sb("rows", [P, 2, CH, W])
        other = ph.sb("other", [P, 2, CH, P], BF16)
        tile_max = ph.sb("tile_max", [P, CH, 4])
        drop = ph.sb("drop", [P, CH])
        carried = ph.sb("carried", [P, 2, CH, 4])
        banks = [ph.ps(f"s{n}", [P, 512]) for n in range(CH)]
        loaded, gathered, masked, chained, stored, rows_stored = (ph.ring(n) for n in ("ld", "ga", "ma", "ch", "st", "rs"))
        scored, reduced = ([[ph.sem(f"{n}{q}{h}") for h in range(2)] for q in range(RING)] for n in ("sc", "re"))

        def one_before(q, m):
            return (q + 3) % RING, m if q >= 1 else m - 1

        with nc.Block() as block:
            @block.sync
            def _(sp):
                def step(c, q, m):
                    wait(sp, chained[q], c(1, m - 1))
                    sp.dma_start(recs[:, q, :], at(r4, chunk(c, q, m))).then_inc(loaded[q], 16)

                def keep_rows(c, q, m):
                    sp.wait_ge(gathered[q], c(16 * CH, m))
                    sp.dma_start(at(kept_rows, chunk(c, q, m)), rows[:, q % 2].rearrange("p j w -> p (j w)")).then_inc(rows_stored[q], 16)
                stages(sp, [(0, step), (2, keep_rows)])
                for q in range(RING):
                    sp.wait_ge(rows_stored[q], 16 * NI)

            @block.gpsimd
            def _(pool):
                def step(c, q, m):
                    free, n = two_before(q, m)
                    pool.wait_ge(loaded[q], c(16, m))
                    wait(pool, scored[free][1], c(1, n))
                    wait(pool, rows_stored[free], c(16, n))
                    pool.nop(nofuse=True)
                    for j in range(CH):
                        o = R4["col"] + j
                        pool.indirect_dma_start(out=rows[:, q % 2, j, :], out_offset=None, in_=table,
                                                in_offset=bass.IndirectOffsetOnAxis(ap=recs[:, q, o:o + 1].bitcast(I32), axis=0)
                                                ).then_inc(gathered[q], 16)
                stages(pool, [(0, step)])

            @block.vector
            def _(dve):
                dve.memset(carried[:, :, :, :], 0.0)
                dve.drain()

                def mask(c, q, m):
                    free, n = two_before(q, m)
                    dve.wait_ge(loaded[q], c(16, m))
                    wait(dve, scored[free][1], c(1, n))
                    for j in range(CH):
                        o = R4["lo"] + j
                        dve.tensor_scalar(other[:, q % 2, j, :], k["iota"][:, 0:P], recs[:, q, o:o + 1], -NEG, ALU.not_equal, ALU.mult)
                    dve.drain().then_inc(masked[q], 1)

                def chain(c, q, m):
                    free, n = two_before(q, m)
                    dve.tensor_scalar(drop[:, :], recs[:, q, R4["keep"]:R4["keep"] + CH], -1.0, NEG, ALU.add, ALU.mult)
                    for h in range(2):
                        dve.wait_ge(scored[q][h], c(1, m))
                        for j in range(HALF * h, HALF * (h + 1)):
                            ins = dve.tensor_reduce(tile_max[:, j, :], banks[j][:, :].rearrange("p (h e) -> p h e", e=P), axis=AX, op=ALU.max)
                        ins.then_inc(reduced[q][h], 1)
                    dve.drain()
                    wait(dve, stored[free], c(16, n))
                    for j in range(CH):
                        if j:
                            dve.drain()
                        before = carried[:, q % 2, j - 1, :] if j else carried[:, 1 - q % 2, CH - 1, :]
                        dve.scalar_tensor_tensor(carried[:, q % 2, j, :], before, drop[:, j:j + 1], tile_max[:, j, :], ALU.add, ALU.max)
                    dve.drain().then_inc(chained[q], 1)
                stages(dve, [(0, mask), (1, chain)])

            @block.tensor
            def _(pe):
                def score(c, q, m):
                    free, n = one_before(q, m)
                    pe.wait_ge(masked[q], c(1, m))
                    pe.wait_ge(gathered[q], c(16 * CH, m))
                    for h in range(2):
                        wait(pe, reduced[free][h], c(1, n))
                        for j in range(HALF * h, HALF * (h + 1)):
                            pe.matmul(banks[j][:, :], other[:, q % 2, j, :], k["ident_b"][:, :].unsqueeze(1).to_broadcast([P, 4, P]),
                                      start=True, stop=False, skip_group_check=True)
                            for head in range(4):
                                ins = pe.matmul(banks[j][:, head * P:(head + 1) * P],
                                                rows[:, q % 2, j, D + head:D + head + 1].to_broadcast([P, P]), k["ident"][:, :],
                                                start=False, stop=head == 3, skip_group_check=True)
                        ins.then_inc(scored[q][h], 1)
                stages(pe, [(0, score)])

            @block.scalar
            def _(act):
                def store(c, q, m):
                    act.wait_ge(chained[q], c(1, m))
                    act.dma_start(at(maxima, chunk(c, q, m)), carried[:, q % 2].rearrange("p j w -> p (j w)")).then_inc(stored[q], 16)
                stages(act, [(0, store)])
                for q in range(RING):
                    act.wait_ge(stored[q], 16 * NI)


def attention_pass(nc, k, r4, kept_rows, spread, result):
    W, OUT = 8, 4 * D + 4
    with Phase(nc, "at") as ph:
        recs = ph.sb("recs", [P, RING, R4["words"]])
        rows = ph.sb("rows", [P, RING, CH, D + 4])
        tabs = ph.sb("tabs", [P, RING, CH, W])
        onehot = ph.sb("onehot", [P, 2, CH, P])
        turned = ph.sb("turned", [P, 2, CH * P])
        score = ph.sb("score", [P, 2, CH, 4])
        weighted = ph.sb("weighted", [P, 2, CH, OUT])
        carried = ph.sb("carried", [P, 2, CH, OUT])
        t_ps = [[ph.ps(f"t{b}", [P, 512]) for b in range(2)]] * 2
        l_ps = [ph.ps("l", [P, 512])] * 2
        s_ps = [ph.ps(f"s{b}", [P, 512]) for b in range(3)]
        loaded, hot, transposed, copied, looked, scored, powered, built, summed, chained, stored = (
            ph.ring(n) for n in ("ld", "ho", "tr", "co", "lo", "sd", "po", "bu", "su", "ch", "st"))
        spread4 = spread.rearrange("(c t) (n w) -> c n t w", t=CH, w=W)

        def one_before(q, m):
            return (q + 3) % RING, m if q >= 1 else m - 1

        with nc.Block() as block:
            @block.sync
            def _(sp):
                def step(c, q, m):
                    wait(sp, chained[q], c(1, m - 1))
                    n = chunk(c, q, m)
                    sp.dma_start(recs[:, q, :], at(r4, n)).then_inc(loaded[q], 16)
                    sp.dma_start(rows[:, q].rearrange("p j w -> p (j w)"), at(kept_rows, n)).then_inc(loaded[q], 16)
                    sp.dma_start(tabs[:, q], at(spread4, n)).then_inc(loaded[q], 16)
                stages(sp, [(0, step)])

            @block.vector
            def _(dve):
                dve.memset(carried[:, :, :, :], 0.0)
                dve.drain()

                def make_hot(c, q, m):
                    free, n = two_before(q, m)
                    dve.wait_ge(loaded[q], c(48, m))
                    wait(dve, summed[free], c(1, n))
                    for j in range(CH):
                        o = R4["lo"] + j
                        dve.tensor_scalar(onehot[:, q % 2, j, :], k["iota"][:, 0:P], recs[:, q, o:o + 1], None, ALU.is_equal)
                    dve.drain().then_inc(hot[q], 1)

                def scores(c, q, m):
                    dve.wait_ge(looked[q], c(1, m))
                    own = l_ps[0][:, 0:CH * W].rearrange("p (t w) -> p t w", w=W)
                    s = score[:, q % 2]
                    dve.tensor_tensor(s, rows[:, q, :, D:D + 4], own[:, :, 0:4], ALU.add)
                    dve.drain()
                    dve.scalar_tensor_tensor(s, s, 0.2, s, ALU.mult, ALU.max)
                    dve.drain()
                    dve.tensor_tensor(s, s, own[:, :, 4:8], ALU.subtract)
                    dve.drain()
                    dve.tensor_scalar(s, s, 1.0, None, ALU.min).then_inc(scored[q], 1)

                def weigh(c, q, m):
                    free, n = two_before(q, m)
                    dve.wait_ge(powered[q], c(1, m))
                    wt = weighted[:, q % 2]
                    for head in range(4):
                        dve.tensor_tensor(wt[:, :, head * D:(head + 1) * D], rows[:, q, :, 0:D],
                                          wt[:, :, 4 * D + head:4 * D + head + 1].to_broadcast([P, CH, D]), ALU.mult)
                    dve.drain().then_inc(built[q], 1)

                def chain(c, q, m):
                    free, n = two_before(q, m)
                    dve.wait_ge(summed[q], c(1, m))
                    wait(dve, stored[free], c(16, n))
                    for j in range(CH):
                        before = carried[:, q % 2, j - 1, :] if j else carried[:, 1 - q % 2, CH - 1, :]
                        o = R4["keep"] + j
                        dve.scalar_tensor_tensor(carried[:, q % 2, j, :], before, recs[:, q, o:o + 1],
                                                 s_ps[j // 3][:, (j % 3) * OUT:(j % 3 + 1) * OUT], ALU.mult, ALU.add)
                        last = dve.drain()
                    last.then_inc(chained[q], 1)
                stages(dve, [(0, make_hot), (1, scores), (1, weigh), (1, chain)])

            @block.tensor
            def _(pe):
                def transpose(c, q, m):
                    before, n = one_before(q, m)
                    pe.wait_ge(hot[q], c(1, m))
                    wait(pe, copied[before], c(1, n))
                    for j in range(CH):
                        ins = pe.transpose(t_ps[0][j // 4][:, (j % 4) * P:(j % 4 + 1) * P], onehot[:, q % 2, j, :], k["ident"][:, :])
                    ins.then_inc(transposed[q], 1)

                def look_up(c, q, m):
                    before, n = one_before(q, m)
                    pe.wait_ge(copied[q], c(1, m))
                    wait(pe, scored[before], c(1, n))
                    for j in range(CH):
                        ins = pe.matmul(l_ps[0][:, j * W:(j + 1) * W], turned[:, q % 2, j * P:(j + 1) * P], tabs[:, q, j, :],
                                        start=True, stop=True)
                    ins.then_inc(looked[q], 1)

                def multiply(c, q, m):
                    before, n = one_before(q, m)
                    pe.wait_ge(built[q], c(1, m))
                    wait(pe, chained[before], c(1, n))
                    for j in range(CH):
                        ins = pe.matmul(s_ps[j // 3][:, (j % 3) * OUT:(j % 3 + 1) * OUT], onehot[:, q % 2, j, :],
                                        weighted[:, q % 2, j, :], start=True, stop=True)
                    ins.then_inc(summed[q], 1)
                stages(pe, [(0, transpose), (0, look_up), (1, multiply)])

            @block.scalar
            def _(act):
                def copy(c, q, m):
                    free, n = two_before(q, m)
                    act.wait_ge(transposed[q], c(1, m))
                    wait(act, looked[free], c(1, n))
                    for b in range(2):
                        act.activation(turned[:, q % 2, b * 4 * P:(b + 1) * 4 * P], t_ps[0][b][:, :], ACT.Copy)
                    act.drain().then_inc(copied[q], 1)

                def power(c, q, m):
                    free, n = two_before(q, m)
                    act.wait_ge(scored[q], c(1, m))
                    wait(act, summed[free], c(1, n))
                    act.activation(weighted[:, q % 2, :, 4 * D:OUT], score[:, q % 2], ACT.Exp).then_inc(powered[q], 1)

                def store(c, q, m):
                    act.wait_ge(chained[q], c(1, m))
                    act.dma_start(at(result, chunk(c, q, m)), carried[:, q % 2].rearrange("p j w -> p (j w)")).then_inc(stored[q], 16)
                stages(act, [(0, copy), (1, power), (2, store)])
                for q in range(RING):
                    act.wait_ge(stored[q], 16 * NI)


def spline_gnn(nc, x, src, dst, edge_attr, edge_weight, stn1_w, stn1_b, stn2_w, stn2_b, stn3_w, stn3_b, stn4_w, stn4_b,
               conv_w, conv_b, w_gat, attn_l, attn_r, w_ih, w_hh, b_ih, b_hh, out):
    def dram(name, shape):
        return nc.dram_tensor(name, shape, F32, kind="Internal").ap()

    rec_src, rec_dst = dram("rec_src", [ROWS, WA]), dram("rec_dst", [ROWS, WB])
    r1, r2, r3, r4 = (dram(f"r{n}", [NC, P, r["words"]]) for n, r in enumerate((R1, R2, R3, R4), 1))
    h_table = dram("h_table", [NP, D])
    sums_d, sums_knots = dram("sums_d", [NC, P, CH * D]), dram("sums_knots", [NC, P, CH * 126])
    sums_64 = dram("sums_64", [NC, P, CH * 64])
    z_even, z_odd = dram("z_even", [NP * 75, 64]), dram("z_odd", [NP * 50, 64])
    z_conv = dram("z_conv", [NP * 125, D])
    t_table, t_spread = dram("t_table", [NP, 4]), dram("t_spread", [T, P * 4])
    moved = dram("moved", [NC, P, CH * 3])
    q_table, kept_rows = dram("q_table", [NP, D + 4]), dram("kept_rows", [NC, P, CH * (D + 4)])
    maxima = dram("maxima", [NC, P, CH * 4])
    m_table, m_spread = dram("m_table", [NP, 8]), dram("m_spread", [T, P * 8])
    sums_att = dram("sums_att", [NC, P, CH * 132])

    with ExitStack() as whole:
        def sb(name, shape, dt=F32):
            return whole.enter_context(nc.sbuf_tensor(name, shape, dt))

        k = {"iota": sb("iota", [P, T]), "part": sb("part", [P, 1]), "part_i": sb("part_i", [P, 1], I32),
             "ident": sb("ident", [P, P]), "before": sb("before", [P, P]), "ident_b": sb("ident_b", [P, P], BF16),
             "before_b": sb("before_b", [P, P], BF16), "ones": sb("ones", [P, P]), "ones_b": sb("ones_b", [P, P], BF16),
             "keep": sb("keep", [P, T]), "last": sb("last", [P, NB], I32), "tile_block": sb("tile_block", [P, T // P], I32)}
        xs, hs = sb("xs", [P, NB, D]), sb("hs", [P, NB, D])
        degree = sb("degree", [P, NB])

        def add_to_x(name, sums, scale=None, bias=None):
            def work(dve):
                if scale is not None:
                    dve.tensor_tensor(sums[:, :, :], sums[:, :, :], scale.unsqueeze(2).to_broadcast([P, NB, D]), ALU.mult)
                    dve.drain()
                if bias is not None:
                    dve.tensor_tensor(sums[:, :, :], sums[:, :, :], bias.unsqueeze(1).to_broadcast([P, NB, D]), ALU.add)
                    dve.drain()
                dve.tensor_tensor(xs[:, :, :], xs[:, :, :], sums[:, :, :], ALU.add)
            on_vector(nc, name, work)

        constants(nc, k)
        load_nodes(nc, x, xs)
        layernorm_relu(nc, "ln0", xs, hs, h_table)
        sort_edges(nc, "sa", k, src, [(dst, 1, I32), (edge_attr, 3, F32)], rec_src, WA)
        prepare_by_source(nc, k, rec_src, r1, r2)

        def knot_products(ph):
            bc = ph.sb("bc", [P, CH, 5, 5])
            knots = ph.sb("knots", [P, 2, CH, 126])

            def init(dve):
                dve.memset(knots[:, :, :, :], 1.0)

            def build(dve, rec, r):
                v = rec[:, R1["hats"]:].rearrange("p (t a n) -> p t a n", t=CH, a=3)
                dve.tensor_tensor(bc[:, :, :, :], v[:, :, 1, :].unsqueeze(3).to_broadcast([P, CH, 5, 5]),
                                  v[:, :, 2, :].unsqueeze(2).to_broadcast([P, CH, 5, 5]), ALU.mult)
                dve.drain()
                dve.tensor_tensor(knots[:, r, :, 0:125].rearrange("p t (a n) -> p t a n", a=5),
                                  v[:, :, 0, :].unsqueeze(3).to_broadcast([P, CH, 5, 25]),
                                  bc[:, :, :, :].rearrange("p t b c -> p t (b c)").unsqueeze(2).to_broadcast([P, CH, 5, 25]),
                                  ALU.mult)
            return {"knots": knots, "init": init, "build": build}

        segment_pass(nc, "p1", k, r1, R1, [(h_table, R1["col"], D)], [(D, sums_d), (126, sums_knots)],
                     lambda rows, r, j, extra: [[rows[0]], [extra["knots"][:, r, j, :]]], prepare=knot_products)

        with Phase(nc, "tables") as ph:
            h1 = ph.sb("h1", [P, NB, 64])
            with Phase(nc, "first") as ph1:
                knots, sums = ph1.sb("knots", [P, NB, 126]), ph1.sb("sums", [P, NB, D])
                w1, b1 = ph1.sb("w1", [125, 64]), ph1.sb("b1", [P, 64])
                load(nc, "lw1", [(w1[:, :], stn1_w), (b1[:, :], stn1_b.partition_broadcast(P))])
                block_sums(nc, "bs1", k, [(D, sums_d, sums), (126, sums_knots, knots)])
                add_to_x("x1", sums)

                def invert(dve):
                    dve.tensor_scalar(degree[:, :], knots[:, :, 125], 1.0, None, ALU.max)
                    dve.drain()
                    dve.reciprocal(degree[:, :], degree[:, :])
                on_vector(nc, "degree", invert)
                transform(nc, "t1", k, knots, 125, w1[:, :], 64, h1)
                elu(nc, "e1", h1, degree[:, :], b1[:, :])
            layernorm_relu(nc, "ln1", xs, hs, None)
            w2 = ph.sb("w2", [64, 125 * 64])
            load(nc, "lw2", [(w2[:, :].rearrange("i (n o) -> i n o", o=64), stn2_w.rearrange("n i o -> i n o"))])
            node_tables(nc, "z2", k, h1, 64, w2[:, :], 8000,
                        [(lambda z: z[:, :].rearrange("p (a m) -> p a m", m=1600)[:, 0:5:2, :],
                          z_even.rearrange("(b p a m) f -> b p a (m f)", p=P, a=3, m=25)),
                         (lambda z: z[:, :].rearrange("p (a m) -> p a m", m=1600)[:, 1:5:2, :],
                          z_odd.rearrange("(b p a m) f -> b p a (m f)", p=P, a=2, m=25))])

        near = (0, 1, 5, 6)
        segment_pass(nc, "c2", k, r2, R2, [(z_even, R2["idx"][0], 7 * 64), (z_odd, R2["idx"][1], 7 * 64)], [(64, sums_64)],
                     corner_products((near, near), 64), weigh=weigh_corners(R2, ((0,), (0,)), 64))

        with Phase(nc, "dense") as ph:
            h2, h3, t = ph.sb("h2", [P, NB, 64]), ph.sb("h3", [P, NB, 64]), ph.sb("t", [P, NB, 4])
            b2, b3, b4 = ph.sb("b2", [P, 64]), ph.sb("b3", [P, 64]), ph.sb("b4", [P, 3])
            w3, w4 = ph.sb("w3", [64, 64]), ph.sb("w4", [64, 4])
            w5 = ph.sb("w5", [D, 125 * D])
            on_vector(nc, "w40", lambda dve: dve.memset(w4[:, :], 0.0))
            load(nc, "lw3", [(b2[:, :], stn2_b.partition_broadcast(P)), (b3[:, :], stn3_b.partition_broadcast(P)),
                             (b4[:, :], stn4_b.partition_broadcast(P)), (w3[:, :], stn3_w), (w4[:, 0:3], stn4_w),
                             (w5[:, :].rearrange("i (n o) -> i n o", o=D), conv_w.rearrange("n i o -> i n o"))])
            block_sums(nc, "bs2", k, [(64, sums_64, h2)])
            elu(nc, "e2", h2, degree[:, :], b2[:, :])
            transform(nc, "t3", k, h2, 64, w3[:, :], 64, h3)
            elu(nc, "e3", h3, None, b3[:, :])
            transform(nc, "t4", k, h3, 64, w4[:, :], 4, t)
            on_vector(nc, "t4b", lambda dve: dve.tensor_tensor(t[:, :, 0:3], t[:, :, 0:3],
                                                               b4[:, :].unsqueeze(1).to_broadcast([P, NB, 3]), ALU.add))
            load(nc, "st4", [(t_table.rearrange("(b p) w -> p b w", p=P), t[:, :, :])])
            by_tile(nc, "bt", k, t_table, 4, t_spread)
            node_tables(nc, "z3", k, hs, D, w5[:, :], 4000,
                        [(lambda z: z[:, :], z_conv.rearrange("(b p m) f -> b p (m f)", p=P, m=125))])
        move_pass(nc, k, rec_src, r1, t_table, t_spread, moved)
        prepare_moved(nc, k, r1, moved, r3)

        segment_pass(nc, "c3", k, r3, R3, [(z_conv, R3["idx"][0], 32 * D)], [(D, sums_d)],
                     corner_products((near + tuple(25 + n for n in near),), D), weigh=weigh_corners(R3, ((0, 25),), D))
        with Phase(nc, "third") as ph:
            sums, b5 = ph.sb("sums", [P, NB, D]), ph.sb("b5", [P, D])
            load(nc, "lb5", [(b5[:, :], conv_b.partition_broadcast(P))])
            block_sums(nc, "bs3", k, [(D, sums_d, sums)])
            add_to_x("x2", sums, degree[:, :], b5[:, :])
        layernorm_relu(nc, "ln2", xs, hs, h_table)

        sort_edges(nc, "sb", k, dst, [(src, 1, I32), (edge_weight, 1, F32)], rec_dst, WB)
        prepare_by_target(nc, k, rec_dst, r4)
        segment_pass(nc, "p2", k, r4, R4, [(h_table, R4["col"], D)], [(D, sums_d)],
                     lambda rows, r, j, extra: [[rows[0]]], scale=R4["w"])
        with Phase(nc, "fourth") as ph:
            sums = ph.sb("sums", [P, NB, D])
            block_sums(nc, "bs4", k, [(D, sums_d, sums)])
            add_to_x("x3", sums)
        layernorm_relu(nc, "ln3", xs, hs, q_table)

        with Phase(nc, "heads") as ph:
            gat, attn = ph.sb("gat", [D, 4 * D]), ph.sb("attn", [D, 2, 4 * D])
            to_scores = ph.sb("to_scores", [D, 8])
            scores, largest, both = ph.sb("scores", [P, NB, 8]), ph.sb("largest", [P, NB, 4]), ph.sb("both", [P, NB, 8])
            load(nc, "lg", [(gat[:, :], w_gat), (attn[:, 0, :], attn_l.partition_broadcast(D)),
                            (attn[:, 1, :], attn_r.partition_broadcast(D))])

            def fold(dve):
                for side in range(2):
                    dve.tensor_tensor(attn[:, side, :], attn[:, side, :], gat[:, :], ALU.mult)
                dve.drain()
                dve.tensor_reduce(to_scores[:, :], attn[:, :, :].rearrange("p s (h f) -> p (s h) f", f=D), axis=AX, op=ALU.add)
            on_vector(nc, "fold", fold)
            transform(nc, "ts", k, hs, D, to_scores[:, :], 8, scores)
            load(nc, "sts", [(q_table[:, D:].rearrange("(b p) w -> p b w", p=P), scores[:, :, 0:4])])
            max_pass(nc, k, r4, q_table, kept_rows, maxima)
            block_sums(nc, "bs5", k, [(4, maxima, largest)])

            def bound(dve):
                dve.tensor_copy(both[:, :, 0:4], scores[:, :, 4:8])
                dve.tensor_tensor(largest[:, :, :], largest[:, :, :], scores[:, :, 4:8], ALU.add)
                dve.drain()
                dve.scalar_tensor_tensor(both[:, :, 4:8], largest[:, :, :], 0.2, largest[:, :, :], ALU.mult, ALU.max)
            on_vector(nc, "bound", bound)
            load(nc, "stm", [(m_table.rearrange("(b p) w -> p b w", p=P), both[:, :, :])])
            by_tile(nc, "bm", k, m_table, 8, m_spread)
        attention_pass(nc, k, r4, kept_rows, m_spread, sums_att)

        with Phase(nc, "update") as ph:
            gi, gh = ph.sb("gi", [P, NB, 3 * D]), ph.sb("gh", [P, NB, 3 * D])
            bi, bh = ph.sb("bi", [P, 3 * D]), ph.sb("bh", [P, 3 * D])
            gat_t, ih_t = ph.sb("gat_t", [P, P]), ph.sb("ih_t", [P, 3 * D])
            hh_t, from_heads = ph.sb("hh_t", [D, 3 * D]), ph.sb("from_heads", [P, 3 * D])
            on_vector(nc, "g0", lambda dve: dve.memset(gat_t[:, :], 0.0))
            load(nc, "lu", [(gat_t[h * D:(h + 1) * D, h * D:(h + 1) * D], w_gat[:, h * D:(h + 1) * D].rearrange("i f -> f i"))
                            for h in range(4)] +
                 [(ih_t[:, :], w_ih.rearrange("g f -> f g")), (hh_t[:, :], w_hh.rearrange("g f -> f g")),
                  (bi[:, :], b_ih.partition_broadcast(P)), (bh[:, :], b_hh.partition_broadcast(P))])
            fold_heads(nc, gat_t, ih_t, from_heads)
            with Phase(nc, "sums") as ph1:
                sums, inv = ph1.sb("sums", [P, NB, 132]), ph1.sb("inv", [P, NB, 4])
                block_sums(nc, "bs6", k, [(132, sums_att, sums)])

                def normalize(dve):
                    dve.tensor_scalar(inv[:, :, :], sums[:, :, 128:132], 1e-30, None, ALU.max)
                    dve.drain()
                    dve.reciprocal(inv[:, :, :], inv[:, :, :])
                    dve.drain()
                    for h in range(4):
                        s = sums[:, :, h * D:(h + 1) * D]
                        dve.tensor_tensor(s, s, inv[:, :, h:h + 1].to_broadcast([P, NB, D]), ALU.mult)
                on_vector(nc, "normalize", normalize)
                transform(nc, "ti", k, sums, P, from_heads[:, :], 3 * D, gi)
            transform(nc, "th", k, hs, D, hh_t[:, :], 3 * D, gh)
            gated_update(nc, gi, gh, bi, bh, hs, xs)
            elu(nc, "e4", hs)
            on_vector(nc, "x4", lambda dve: dve.tensor_tensor(xs[:, :, :], xs[:, :, :], hs[:, :, :], ALU.add))
            load(nc, "out", [(out[0:(NB - 1) * P].rearrange("(b p) f -> p b f", p=P), xs[:, 0:NB - 1, :]),
                             (out[(NB - 1) * P:N], xs[0:LASTN, NB - 1, :])])


def fold_heads(nc, gat_t, ih_t, from_heads):
    with Phase(nc, "fh") as ph:
        ps, done = ph.ps("ps", [P, 512]), ph.sem("done")
        with nc.Block() as block:
            @block.tensor
            def _(pe):
                pe.matmul(ps[:, 0:3 * D], gat_t[:, :], ih_t[:, :], start=True, stop=True).then_inc(done, 1)

            @block.vector
            def _(dve):
                dve.wait_ge(done, 1)
                dve.tensor_copy(from_heads[:, :], ps[:, 0:3 * D])


def gated_update(nc, gi, gh, bi, bh, hs, xs):
    with Phase(nc, "gu") as ph:
        added, gated, mixed, bent = (ph.sem(n) for n in ("added", "gated", "mixed", "bent"))
        rz = 2 * D
        with nc.Block() as block:
            @block.vector
            def _(dve):
                for g, b in ((gi, bi), (gh, bh)):
                    dve.tensor_tensor(g[:, :, :], g[:, :, :], b[:, :].unsqueeze(1).to_broadcast([P, NB, 3 * D]), ALU.add)
                dve.drain()
                dve.tensor_tensor(gi[:, :, 0:rz], gi[:, :, 0:rz], gh[:, :, 0:rz], ALU.add).then_inc(added, 1)
                dve.wait_ge(gated, 1)
                n = gi[:, :, rz:]
                dve.tensor_tensor(gh[:, :, rz:], gh[:, :, rz:], gi[:, :, 0:D], ALU.mult)
                dve.drain()
                dve.tensor_tensor(n, n, gh[:, :, rz:], ALU.add).then_inc(mixed, 1)
                dve.wait_ge(bent, 1)
                dve.tensor_tensor(gh[:, :, 0:D], hs[:, :, :], n, ALU.subtract)
                dve.drain()
                dve.tensor_tensor(gh[:, :, 0:D], gh[:, :, 0:D], gi[:, :, D:rz], ALU.mult)
                dve.drain()
                dve.tensor_tensor(hs[:, :, :], gh[:, :, 0:D], n, ALU.add)

            @block.scalar
            def _(act):
                act.wait_ge(added, 1)
                act.activation(gi[:, :, 0:rz], gi[:, :, 0:rz], ACT.Sigmoid).then_inc(gated, 1)
                act.wait_ge(mixed, 1)
                act.activation(gi[:, :, rz:], gi[:, :, rz:], ACT.Tanh).then_inc(bent, 1)


_INS = ["x", "src", "dst", "edge_attr_3", "edge_weight", "L1_gnn_stn1_w", "L1_gnn_stn1_b", "L1_gnn_stn2_w", "L1_gnn_stn2_b",
        "L1_gnn_stn3_w", "L1_gnn_stn3_b", "L1_gnn_stn4_w", "L1_gnn_stn4_b", "L1_gnn_conv_w", "L1_gnn_conv_b", "L3_gnn_W_gat",
        "L3_gnn_attn_l", "L3_gnn_attn_r", "L3_gnn_W_ih", "L3_gnn_W_hh", "L3_gnn_b_ih", "L3_gnn_b_hh"]
_FLAT = ("edge_attr_3", "L3_gnn_attn_l", "L3_gnn_attn_r")


def kernel(**inputs):
    import numpy as np
    import concourse.bacc as bacc
    from concourse.bass_utils import run_bass_kernel_spmd

    nc = bacc.Bacc("TRN2", target_bir_lowering=False, num_devices=1)
    arrays, args = {}, []
    for name in _INS:
        a = np.ascontiguousarray(inputs[name])
        if name in _FLAT:
            a = a.reshape(-1)
        if name == "L1_gnn_stn1_w":
            a = a.reshape(a.shape[0], a.shape[2])
        arrays[f"in_{name}"] = a
        args.append(nc.dram_tensor(f"in_{name}", list(a.shape), mybir.dt.from_np(a.dtype), kind="ExternalInput").ap())
    out = nc.dram_tensor("out", [N, D], F32, kind="ExternalOutput").ap()
    spline_gnn(nc, *args, out)
    r = run_bass_kernel_spmd(nc, [arrays], core_ids=[0])
    return r.results[0]["out"]
```

```python
from contextlib import ExitStack

import concourse.bass as bass
from concourse import mybir

F32 = mybir.dt.float32
I32 = mybir.dt.int32
BF16 = mybir.dt.bfloat16
ALU = mybir.AluOpType
ACT = mybir.ActivationFunctionType
AX = mybir.AxisListType.X

P = 128
N = 12500
E = 200000
D = 32
NB = -(-N // P)
NP = NB * P
L = 1568
SC = 16
SN = L // SC
NBIN = NB + 1
LOWS, HIGHS = 16, 8
CH = 8
RING = 4
T = 1664
NC = T // CH
NI = NC // RING
ROWS = (NC + 1) * CH * P
WA, WB = 8, 4
PIECE = NC // 8
PT = PIECE * CH
FULL = E // L
REST = E - FULL * L
LASTN = N - (NB - 1) * P
NEG = float(2.0 ** 100)
KW = 2 * 25 * 3
NZ = 2 * NI

assert P * L >= E and L % SC == 0 and T >= NB + E / P and NC % RING == 0 and NC % 8 == 0 and NZ >= NB and NZ % 8 == 0 and SN == NB and NB % 14 == 0 and NBIN <= LOWS * HIGHS


class Phase:

    def __init__(self, nc, name):
        self.nc, self.name, self.stack, self.sems = nc, name, ExitStack(), []

    def sb(self, name, shape, dt=F32):
        return self.stack.enter_context(self.nc.sbuf_tensor(f"{self.name}_{name}", shape, dt))

    def ps(self, name, shape, dt=F32):
        return self.stack.enter_context(self.nc.psum_tensor(f"{self.name}_{name}", shape, dt))

    def sem(self, name):
        s = self.nc.alloc_semaphore(f"{self.name}_{name}")
        self.sems.append(s)
        return s

    def ring(self, name):
        return [self.sem(f"{name}{q}") for q in range(RING)]

    def __enter__(self):
        return self

    def __exit__(self, *a):
        self.nc.clear_and_free_semaphores(self.sems)
        self.nc.all_engine_barrier()
        self.stack.close()


def at(ap, k):
    if isinstance(k, int):
        return ap[k]
    names = "pqr"[:len(ap.shape) - 1]
    return ap[bass.ds(k, 1)].rearrange(f"a {' '.join(names)} -> (a {names[0]}) {' '.join(names[1:])}")


def part(tile, k, size):
    return tile[:, bass.ds(k * size, size)]


def snap(eng, v):
    return v if isinstance(v, int) else eng.snap(v)


def looped(eng, n, body):
    body(0)
    with eng.Fori(1, n) as i:
        body(i)


def wait(eng, sem, value):
    if not isinstance(value, int) or value > 0:
        eng.wait_ge(sem, value)


def constants(nc, k):
    with Phase(nc, "cst") as ph:
        made = ph.sem("made")
        raw = ph.sb("raw", [P, T], I32)
        with nc.Block() as block:
            @block.gpsimd
            def _(pool):
                pool.iota(raw[:, :], pattern=[[1, T]], base=0, channel_multiplier=0).then_inc(made, 1)
                pool.iota(k["part_i"][:, :], pattern=[[0, 1]], base=0, channel_multiplier=1).then_inc(made, 1)
                pool.memset(k["ident"][:, :], 0.0).then_inc(made, 1)
                pool.memset(k["before"][:, :], 1.0).then_inc(made, 1)
                pool.wait_ge(made, 4)
                pool.affine_select(out=k["ident"][:, :], in_=k["ident"][:, :], compare_op=ALU.not_equal, fill=1.0,
                                   base=0, pattern=[[-1, P]], channel_multiplier=1).then_inc(made, 1)
                pool.affine_select(out=k["before"][:, :], in_=k["before"][:, :], compare_op=ALU.is_gt, fill=0.0,
                                   base=0, pattern=[[1, P]], channel_multiplier=-1).then_inc(made, 1)

            @block.vector
            def _(dve):
                dve.memset(k["ones"][:, :], 1.0)
                dve.memset(k["ones_b"][:, :], 1.0)
                dve.wait_ge(made, 6)
                dve.tensor_copy(k["iota"][:, :], raw[:, :])
                dve.tensor_copy(k["part"][:, :], k["part_i"][:, :])
                dve.tensor_copy(k["ident_b"][:, :], k["ident"][:, :])
                dve.tensor_copy(k["before_b"][:, :], k["before"][:, :])


def load_nodes(nc, x, xs):
    with Phase(nc, "ld") as ph:
        zeroed, loaded = ph.sem("zeroed"), ph.sem("loaded")
        with nc.Block() as block:
            @block.vector
            def _(dve):
                dve.memset(xs[:, NB - 1, :], 0.0).then_inc(zeroed, 1)

            @block.sync
            def _(sp):
                sp.dma_start(xs[:, 0:NB - 1, :], x[0:(NB - 1) * P].rearrange("(b p) f -> p b f", p=P)).then_inc(loaded, 16)
                sp.wait_ge(zeroed, 1)
                sp.dma_start(xs[0:LASTN, NB - 1, :], x[(NB - 1) * P:N]).then_inc(loaded, 16)
                sp.wait_ge(loaded, 32)


def layernorm_relu(nc, name, xs, hs, table, width=D):
    with Phase(nc, name) as ph:
        sq = ph.sb("sq", [P, NB, D])
        s, v = ph.sb("s", [P, NB]), ph.sb("v", [P, NB])
        var_ready, std_ready, h_ready, stored = (ph.sem(n) for n in ("var", "std", "h", "st"))
        with nc.Block() as block:
            @block.vector
            def _(dve):
                dve.tensor_reduce(s[:, :], xs[:, :, :], axis=AX, op=ALU.add)
                dve.drain()
                dve.tensor_scalar(s[:, :], s[:, :], 1.0 / D, None, ALU.mult)
                dve.drain()
                dve.tensor_tensor(hs[:, :, :], xs[:, :, :], s[:, :].unsqueeze(2).to_broadcast([P, NB, D]), ALU.subtract)
                dve.drain()
                dve.tensor_tensor(sq[:, :, :], hs[:, :, :], hs[:, :, :], ALU.mult)
                dve.drain()
                dve.tensor_reduce(v[:, :], sq[:, :, :], axis=AX, op=ALU.add)
                dve.drain()
                dve.tensor_scalar(v[:, :], v[:, :], 1.0 / D, 1e-5, ALU.mult, ALU.add).then_inc(var_ready, 1)
                dve.wait_ge(std_ready, 1)
                dve.reciprocal(v[:, :], s[:, :])
                dve.drain()
                dve.tensor_tensor(hs[:, :, :], hs[:, :, :], v[:, :].unsqueeze(2).to_broadcast([P, NB, D]), ALU.mult)
                dve.drain()
                dve.tensor_scalar(hs[:, :, :], hs[:, :, :], 0.0, None, ALU.max).then_inc(h_ready, 1)

            @block.scalar
            def _(act):
                act.wait_ge(var_ready, 1)
                act.activation(s[:, :], v[:, :], ACT.Sqrt).then_inc(std_ready, 1)

            if table is not None:
                @block.sync
                def _(sp):
                    sp.wait_ge(h_ready, 1)
                    sp.dma_start(table[:, 0:D].rearrange("(b p) f -> p b f", p=P), hs[:, :, :]).then_inc(stored, 16)
                    sp.wait_ge(stored, 16)


def sort_edges(nc, name, k, key, fields, rec, W, beside=None):
    with Phase(nc, name) as ph:
        recs = ph.sb("recs", [P, L, W])
        blk = ph.sb("blk", [P, L])
        base = ph.sb("base", [P, NBIN])
        hist = ph.ps("hist", [P, 512])
        rank = [ph.ps(f"rank{g}", [P, 512]) for g in range(4)]
        total = ph.ps("total", [P, 512])
        count_edges(nc, name + "c", k, key, fields, rec, W, recs, blk, base, hist, rank, total)
        place_edges(nc, name + "p", k, rec, W, recs, blk, base, hist, rank, total, beside)


def count_edges(nc, name, k, key, fields, rec, W, recs, blk, base, hist, rank, total):
    with Phase(nc, name) as ph:
        key_i = ph.sb("key_i", [P, L], I32)
        tmp_i = ph.sb("tmp_i", [P, L], I32)
        raw = [ph.sb(f"raw{n}", [P, L * w], dt) for n, (_, w, dt) in enumerate(fields)]
        fill = ph.sb("fill", [P, 152, W])
        small = ph.sb("small", [P, 8])
        small_i = ph.sb("small_i", [P, 4], I32)
        spread = ph.sb("spread", [P, T])
        halves = [ph.sb(n, [P, L]) for n in ("low", "high")]
        step_halves = [ph.sb(f"step_{n}", [P, 2, SC]) for n in ("low", "high")]
        hot_halves = [ph.sb(f"hot_{n}", [P, 2, SC, size], BF16) for n, size in (("low", LOWS), ("high", HIGHS))]
        grid = ph.sb("grid", [P, LOWS])
        has_high = ph.sb("has_high", [P, 2, NBIN])
        has_low = ph.sb("has_low", [P, LOWS])
        last_i = ph.sb("last_i", [P, 2, NB], I32)

        zeroed, loaded, filled, refilled = (ph.sem(n) for n in ("zeroed", "loaded", "filled", "refilled"))
        with nc.Block() as block:
            @block.vector
            def _(dve):
                dve.memset(key_i[:, :], NP).then_inc(zeroed, 1)
                for r in raw:
                    dve.memset(r[:, :], 0).then_inc(zeroed, 1)
                dve.memset(fill[:, :, :], 0.0)
                dve.drain()
                dve.memset(fill[:, :, 0:1], -1.0).then_inc(filled, 1)
                dve.memset(recs[:, :, :], 0.0)
                dve.wait_ge(loaded, 32 * (1 + len(raw)))
                dve.tensor_scalar(tmp_i[:, :], key_i[:, :], 7, None, ALU.logical_shift_right)
                dve.drain()
                dve.tensor_copy(blk[:, :], tmp_i[:, :])
                dve.drain()
                dve.tensor_scalar(tmp_i[:, :], tmp_i[:, :], LOWS - 1, None, ALU.bitwise_and)
                dve.drain()
                dve.tensor_copy(halves[0][:, :], tmp_i[:, :])
                dve.drain()
                dve.tensor_tensor(halves[1][:, :], blk[:, :], halves[0][:, :], ALU.subtract)
                dve.tensor_scalar(tmp_i[:, :], key_i[:, :], P - 1, None, ALU.bitwise_and)
                dve.drain()
                dve.tensor_copy(recs[:, :, 0], tmp_i[:, :])
                o = 1
                for r, (_, w, _) in zip(raw, fields):
                    dve.tensor_copy(recs[:, :, o:o + w], r[:, :].rearrange("p (l w) -> p l w", w=w))
                    o += w

            @block.sync
            def _(sp):
                sp.wait_ge(zeroed, 1 + len(raw))
                for tile, (src, w, _) in zip([key_i] + raw, [(key, 1, I32)] + list(fields)):
                    sp.dma_start(tile[0:FULL, :], src[0:FULL * L * w].rearrange("(p l) -> p l", l=L * w)).then_inc(loaded, 16)
                    sp.dma_start(tile[FULL:FULL + 1, 0:REST * w], src[FULL * L * w:E * w].rearrange("(a l) -> a l", a=1)).then_inc(loaded, 16)
                sp.wait_ge(filled, 1)
                fill_rows = rec.rearrange("(n p r) w -> n p r w", p=P, r=152)
                for n in range(fill_rows.shape[0]):
                    sp.dma_start(fill_rows[n], fill[:, :, :]).then_inc(refilled, 16)
                sp.wait_ge(refilled, 16 * fill_rows.shape[0])

        taken, hot, counted = ([ph.sem(f"{n}{q}") for q in range(2)] for n in ("taken", "hot", "counted"))

        with nc.Block() as block:
            @block.scalar
            def _(act):
                def body(i):
                    for q in range(2):
                        wait(act, hot[q], i)
                        act.activation(step_halves[0][:, q], part(halves[0], i * 2 + q, SC), ACT.Copy)
                        act.activation(step_halves[1][:, q], part(halves[1], i * 2 + q, SC), ACT.Copy,
                                       scale=1.0 / LOWS)
                        act.drain().then_inc(taken[q], 1)
                looped(act, SN // 2, body)

            @block.vector
            def _(dve):
                def body(i):
                    done = snap(dve, i + 1)
                    for q in range(2):
                        dve.wait_ge(taken[q], done)
                        wait(dve, counted[q], i)
                        for size, h, one in zip((LOWS, HIGHS), step_halves, hot_halves):
                            dve.tensor_tensor(one[:, q], k["iota"][:, 0:size].unsqueeze(1).to_broadcast([P, SC, size]),
                                              h[:, q].unsqueeze(2).to_broadcast([P, SC, size]), ALU.is_equal)
                        dve.drain().then_inc(hot[q], 1)
                looped(dve, SN // 2, body)

            @block.tensor
            def _(pe):
                def step(i, first, last):
                    for q in range(2):
                        pe.wait_ge(hot[q], i + 1)
                        for j in range(SC):
                            ins = pe.matmul(hist[0:HIGHS, 0:LOWS], hot_halves[1][:, q, j, :], hot_halves[0][:, q, j, :],
                                            start=first and q == 0 and j == 0, stop=last and q == 1 and j == SC - 1,
                                            skip_group_check=True)
                        ins.then_inc(counted[q], 1)
                step(0, True, False)
                with pe.Fori(1, SN // 2 - 1) as i:
                    step(i, False, False)
                step(SN // 2 - 1, False, True)

        tiles, start, end, is_pad, not_pad = (small[0:NBIN, n:n + 1] for n in range(5))
        count = small[0:NBIN, 5:6]
        grid_ready, grid_spread, tiles_ready, start_found, start_ready, spread_done, spread_read, keep_found, ended_ready, ended_found = (
            ph.sem(n) for n in ("grid_ready", "grid_spread", "tiles_ready", "start_found", "start_ready", "spread_done", "spread_read",
                                "keep_found", "ended_ready", "ended_found"))
        with nc.Block() as block:
            @block.vector
            def _(dve):
                dve.tensor_copy(grid[0:HIGHS, :], hist[0:HIGHS, 0:LOWS])
                dve.tensor_scalar(small[:, 6:7], k["part"][:, :], float(LOWS), None, ALU.mult)
                dve.tensor_scalar(small_i[:, 2:3], k["part_i"][:, :], LOWS - 1, None, ALU.bitwise_and)
                dve.drain()
                dve.tensor_copy(small[:, 7:8], small_i[:, 2:3])
                dve.tensor_scalar(has_high[0:HIGHS, 0, :], k["iota"][0:HIGHS, 0:NBIN], small[0:HIGHS, 6:7], None, ALU.subtract)
                dve.drain()
                dve.tensor_scalar(has_low[0:NBIN, :], k["iota"][0:NBIN, 0:LOWS], small[0:NBIN, 7:8], None, ALU.is_equal)
                dve.tensor_scalar(has_high[0:HIGHS, 1, :], has_high[0:HIGHS, 0, :], 0.0, None, ALU.is_ge)
                dve.drain()
                dve.scalar_tensor_tensor(has_high[0:HIGHS, 1, :], has_high[0:HIGHS, 0, :], float(LOWS), has_high[0:HIGHS, 1, :],
                                         ALU.is_lt, ALU.mult).then_inc(grid_ready, 1)
                dve.wait_ge(grid_spread, 1)
                dve.tensor_tensor(has_low[0:NBIN, :], has_low[0:NBIN, :], total[0:NBIN, 0:LOWS], ALU.mult)
                dve.drain()
                dve.tensor_reduce(count, has_low[0:NBIN, :], axis=AX, op=ALU.add)
                dve.drain()
                dve.tensor_scalar(small_i[0:NBIN, 0:1], count, 1.0, float(P - 1), ALU.max, ALU.add)
                dve.tensor_scalar(is_pad, k["part"][0:NBIN, :], float(NB), None, ALU.is_equal)
                dve.drain()
                dve.tensor_scalar(small_i[0:NBIN, 1:2], small_i[0:NBIN, 0:1], 7, None, ALU.logical_shift_right)
                dve.tensor_scalar(not_pad, is_pad, -1.0, 1.0, ALU.mult, ALU.add)
                dve.drain()
                dve.tensor_copy(tiles, small_i[0:NBIN, 1:2]).then_inc(tiles_ready, 1)
                dve.wait_ge(start_found, 1)
                dve.tensor_tensor(start, rank[0][0:NBIN, 0:1], not_pad, ALU.mult)
                dve.drain()
                dve.scalar_tensor_tensor(start, is_pad, float(T), start, ALU.mult, ALU.add)
                dve.drain()
                dve.tensor_tensor(end, start, tiles, ALU.add)
                dve.tensor_scalar(spread[0:NB, :], k["iota"][0:NB, :], small[0:NB, 1:2], None, ALU.is_equal)
                dve.drain().then_inc(start_ready, 1)
                dve.wait_ge(spread_done, 1)
                dve.tensor_scalar(base[:, :], rank[1][:, 0:NBIN], float(P), None, ALU.mult)
                dve.tensor_scalar(last_i[:, 0, :], rank[2][:, 0:NB], -1.0, None, ALU.add)
                dve.drain().then_inc(spread_read, 1)
                dve.tensor_scalar(last_i[:, 1, :], last_i[:, 0, :], 3, 10, ALU.logical_shift_right, ALU.logical_shift_left)
                dve.drain()
                dve.tensor_scalar(last_i[:, 0, :], last_i[:, 0, :], CH - 1, None, ALU.bitwise_and)
                dve.tensor_scalar(small_i[:, 3:4], k["part_i"][:, :], 3, None, ALU.logical_shift_left)
                dve.drain()
                dve.tensor_tensor(last_i[:, 1, :], last_i[:, 1, :], last_i[:, 0, :], ALU.bitwise_or)
                dve.drain()
                dve.tensor_tensor(k["last"][:, :], last_i[:, 1, :], small_i[:, 3:4].to_broadcast([P, NB]), ALU.bitwise_or)
                dve.wait_ge(keep_found, 1)
                for n in range(4):
                    dve.tensor_scalar(k["keep"][:, n * (T // 4):(n + 1) * (T // 4)], rank[n][:, 0:T // 4], -1.0, 1.0,
                                      ALU.mult, ALU.add)
                dve.tensor_scalar(spread[0:NB, :], k["iota"][0:NB, :], small[0:NB, 2:3], None,
                                  ALU.is_ge).then_inc(ended_ready, 1)
                dve.wait_ge(ended_found, 1)
                dve.tensor_scalar(k["tile_block"][:, :], total[:, 0:T // P], float(NB - 1), None, ALU.min)

            @block.tensor
            def _(pe):
                pe.wait_ge(grid_ready, 1)
                pe.matmul(total[0:NBIN, 0:LOWS], has_high[0:HIGHS, 1, :], grid[0:HIGHS, :], start=True,
                          stop=True).then_inc(grid_spread, 1)
                pe.wait_ge(tiles_ready, 1)
                pe.matmul(rank[0][0:NBIN, 0:1], k["before"][0:NBIN, 0:NBIN], tiles, start=True,
                          stop=True).then_inc(start_found, 1)
                pe.wait_ge(start_ready, 1)
                pe.matmul(rank[1][:, 0:NBIN], start.to_broadcast([NBIN, P]), k["ident"][0:NBIN, 0:NBIN],
                          start=True, stop=True)
                pe.matmul(rank[2][:, 0:NB], small[0:NB, 2:3].to_broadcast([NB, P]), k["ident"][0:NB, 0:NB],
                          start=True, stop=True).then_inc(spread_done, 1)
                pe.wait_ge(spread_read, 1)
                for n in range(4):
                    ins = pe.matmul(rank[n][:, 0:T // 4], k["ones"][0:NB, :],
                                    spread[0:NB, n * (T // 4):(n + 1) * (T // 4)], start=True, stop=True)
                ins.then_inc(keep_found, 1)
                pe.wait_ge(ended_ready, 1)
                for n in range(T // P):
                    ins = pe.matmul(total[:, n:n + 1], spread[0:NB, n * P:(n + 1) * P], k["ones"][0:NB, 0:1],
                                    start=True, stop=True)
                ins.then_inc(ended_found, 1)



def place_edges(nc, name, k, rec, W, recs, blk, base, hist, rank, total, beside):
    with Phase(nc, name) as ph:
        onehot = ph.sb("onehot", [P, 2, SC, NBIN], BF16)
        step_blk = ph.sb("step_blk", [P, 2, SC])
        ranked = ph.sb("ranked", [P, SC, NBIN])
        group_hot = ph.sb("group_hot", [P, 2, 4, NBIN], BF16)
        step_rec = ph.sb("step_rec", [P, 2, SC, W])
        pos = ph.sb("pos", [P, SC])
        pos_i = ph.sb("pos_i", [P, 4, SC], I32)
        row = ph.sb("row", [P, 2, SC], I32)
        iota_bins = k["iota"][:, 0:NBIN].unsqueeze(1).to_broadcast([P, SC, NBIN])
        if beside:
            beside.reserve(ph, hist)
        G = SC // 4
        step_taken, step_filled, step_hot, step_ranked, step_placed, scattered = (
            [ph.sem(f"{n}{q}") for q in range(2)] for n in ("st", "sf", "sh", "sr", "sp", "sc"))
        with nc.Block() as block:
            @block.scalar
            def _(act):
                def body(i):
                    done, gone = snap(act, i + 1), snap(act, i * (16 * SC))
                    for q in range(2):
                        wait(act, step_placed[q], i)
                        act.activation(step_blk[:, q], part(blk, i * 2 + q, SC), ACT.Copy).then_inc(step_taken[q], 1)
                        wait(act, scattered[q], gone)
                        act.activation(step_rec[:, q], part(recs, i * 2 + q, SC), ACT.Copy).then_inc(step_filled[q], 1)
                        if beside:
                            beside.scalar(act, i, q)
                looped(act, SN // 2, body)
                if beside:
                    beside.scalar_end(act)

            @block.vector
            def _(dve):
                def body(i):
                    done = snap(dve, i + 1)
                    gone = snap(dve, i * (16 * SC))
                    for q in range(2):
                        dve.wait_ge(step_taken[q], done)
                        dve.tensor_tensor(onehot[:, q], iota_bins,
                                          step_blk[:, q].unsqueeze(2).to_broadcast([P, SC, NBIN]), ALU.is_equal)
                        dve.drain()
                        with nc.allow_low_precision("counts up to 4"):
                            dve.tensor_reduce(group_hot[:, q], onehot[:, q].rearrange("p (g j) b -> p g b j", g=4), axis=AX,
                                              op=ALU.add).then_inc(step_hot[q], 1)
                        dve.wait_ge(step_ranked[q], done)
                        for g in range(4):
                            dve.tensor_tensor(ranked[:, g * G:(g + 1) * G, :],
                                              rank[g][:, 0:G * NBIN].rearrange("p (j b) -> p j b", b=NBIN),
                                              base[:, :].unsqueeze(1).to_broadcast([P, G, NBIN]), ALU.add)
                        dve.drain()
                        dve.tensor_tensor(ranked[:, :, :], ranked[:, :, :], onehot[:, q], ALU.mult)
                        dve.tensor_tensor(base[:, :], base[:, :], total[:, 0:NBIN], ALU.add)
                        dve.drain()
                        dve.tensor_reduce(pos[:, :], ranked[:, :, :], axis=AX, op=ALU.add)
                        dve.drain()
                        dve.tensor_copy(pos_i[:, 0, :], pos[:, :])
                        dve.drain()
                        dve.tensor_scalar(pos_i[:, 1, :], pos_i[:, 0, :], 10, 10, ALU.logical_shift_right,
                                          ALU.logical_shift_left)
                        dve.tensor_scalar(pos_i[:, 2, :], pos_i[:, 0, :], P - 1, 3, ALU.bitwise_and,
                                          ALU.logical_shift_left)
                        dve.tensor_scalar(pos_i[:, 3, :], pos_i[:, 0, :], 7, CH - 1, ALU.logical_shift_right,
                                          ALU.bitwise_and)
                        dve.drain()
                        dve.tensor_tensor(pos_i[:, 1, :], pos_i[:, 1, :], pos_i[:, 2, :], ALU.bitwise_or)
                        dve.drain()
                        wait(dve, scattered[q], gone)
                        dve.tensor_tensor(row[:, q, :], pos_i[:, 1, :], pos_i[:, 3, :],
                                          ALU.bitwise_or).then_inc(step_placed[q], 1)
                looped(dve, SN // 2, body)

            @block.tensor
            def _(pe):
                def body(i):
                    done = snap(pe, i + 1)
                    for q in range(2):
                        if beside:
                            beside.turn(pe, i, q)
                        pe.wait_ge(step_hot[q], done)
                        wait(pe, step_placed[1 - q], done if q else i)
                        hots = onehot[:, q]
                        for g in range(4):
                            out = rank[g]
                            pe.matmul(out[:, 0:G * NBIN], k["before_b"][:, :],
                                      hots[:, g * G:(g + 1) * G, :].rearrange("p j b -> p (j b)"),
                                      start=True, stop=False, skip_group_check=True)
                            for before in range(g):
                                pe.matmul(out[:, 0:G * NBIN], k["ones_b"][:, :],
                                          group_hot[:, q, before:before + 1, :].to_broadcast([P, G, NBIN]),
                                          start=False, stop=False, skip_group_check=True)
                            for j in range(G - 1):
                                pe.matmul(out[:, (j + 1) * NBIN:G * NBIN], k["ones_b"][:, :],
                                          hots[:, g * G + j:g * G + j + 1, :].to_broadcast([P, G - 1 - j, NBIN]),
                                          start=False, stop=j == G - 2, skip_group_check=True)
                        for g in range(4):
                            ins = pe.matmul(total[:, 0:NBIN], k["ones_b"][:, :], group_hot[:, q, g, :],
                                            start=g == 0, stop=g == 3)
                        ins.then_inc(step_ranked[q], 1)
                        if beside:
                            beside.multiply(pe, i, q)
                looped(pe, SN // 2, body)
            if beside:
                @block.sync
                def _(sp):
                    beside.store(sp)

            @block.gpsimd
            def _(pool):
                def body(i):
                    done = snap(pool, i + 1)
                    for q in range(2):
                        pool.wait_ge(step_placed[q], done)
                        pool.wait_ge(step_filled[q], done)
                        pool.nop(nofuse=True)
                        for j in range(SC):
                            pool.indirect_dma_start(
                                out=rec, out_offset=bass.IndirectOffsetOnAxis(ap=row[:, q, j:j + 1], axis=0),
                                in_=step_rec[:, q, j, :], in_offset=None).then_inc(scattered[q], 16)
                looped(pool, SN // 2, body)
                for q in range(2):
                    pool.wait_ge(scattered[q], 16 * SC * (SN // 2))


class TablesBeside:
    PIECE_COLS = 500
    LATE = 5

    def __init__(self, k, src, K, weights, F, tables):
        self.k, self.src, self.K, self.weights, self.tables = k, src, K, weights, tables
        self.plane, self.n = 25 * F, 125 * F // self.PIECE_COLS

    def reserve(self, ph, bank):
        n = self.n
        self.taken = ph.sb("taken", [P, 1, self.K])
        self.turned = ph.sb("turned", [P, P])
        self.product = ph.sb("product", [P, 5 * self.plane])
        self.bank, self.z_ps = bank, [ph.ps(f"z{b}", [P, 512]) for b in range(2)]
        self.copied, self.transposed, self.moved = (ph.sem(n) for n in ("copied", "transposed", "moved"))
        self.made, self.read = ([ph.sem(f"{name}{g}") for g in range(n)] for name in ("made", "read"))
        self.stored = [ph.sem(f"stored{a}") for a in range(5)]

    def take(self, act, pieces, before, after):
        for g in pieces:
            for a in range(5):
                if a * self.plane // self.PIECE_COLS == g:
                    wait(act, self.stored[a], snap(act, before * 16))
            act.wait_ge(self.made[g], after)
            o = g * self.PIECE_COLS
            act.activation(self.product[:, o:o + self.PIECE_COLS], self.z_ps[g % 2][:, 0:self.PIECE_COLS],
                           ACT.Copy).then_inc(self.read[g], 1)

    def scalar(self, act, i, q):
        before, after = snap(act, i * 2 + q), snap(act, i * 2 + (q + 1))
        wait(act, self.transposed, before)
        act.activation(self.taken[:, :, :], self.src[:, bass.ds(i * 2 + q, 1), 0:self.K], ACT.Copy).then_inc(self.copied, 1)
        if not (isinstance(i, int) and i == 0 and q == 0):
            self.take(act, range(self.n - self.LATE, self.n), snap(act, i * 2 + (q - 1)), before)
        act.wait_ge(self.transposed, after)
        wait(act, self.made[self.n - 1], before)
        act.activation(self.turned[0:self.K, :], self.bank[0:self.K, 0:P], ACT.Copy).then_inc(self.moved, 1)
        self.take(act, range(self.n - self.LATE), before, after)

    def scalar_end(self, act):
        self.take(act, range(self.n - self.LATE, self.n), SN - 1, SN)

    def turn(self, pe, i, q):
        pe.wait_ge(self.copied, snap(pe, i * 2 + (q + 1)))
        wait(pe, self.moved, snap(pe, i * 2 + q))
        pe.nop(nofuse=True)
        pe.transpose(self.bank[0:self.K, 0:P], self.taken[:, 0, :], self.k["ident"][:, :]).then_inc(self.transposed, 1)

    def multiply(self, pe, i, q):
        before, after = snap(pe, i * 2 + q), snap(pe, i * 2 + (q + 1))
        pe.wait_ge(self.moved, after)
        for g in range(self.n):
            wait(pe, self.read[g - 2] if g >= 2 else self.read[self.n - 2 + g], after if g >= 2 else before)
            pe.matmul(self.z_ps[g % 2][:, 0:self.PIECE_COLS], self.turned[0:self.K, :],
                      self.weights[:, g * self.PIECE_COLS:(g + 1) * self.PIECE_COLS], start=True,
                      stop=True).then_inc(self.made[g], 1)

    def store(self, sp):
        where = {a: (table, n) for planes, table in self.tables for n, a in enumerate(planes)}

        def body(i):
            for q in range(2):
                for a in range(5):
                    last = ((a + 1) * self.plane - 1) // self.PIECE_COLS
                    sp.wait_ge(self.read[last], snap(sp, i * 2 + (q + 1)))
                    table, n = where[a]
                    sp.dma_start(at(table, i * 2 + q)[:, n, :], self.product[:, a * self.plane:(a + 1) * self.plane]).then_inc(self.stored[a], 16)
        looped(sp, SN // 2, body)
        for a in range(5):
            sp.wait_ge(self.stored[a], 16 * SN)


R1 = dict(lo=0, col=8, keep=16, hats=24, words=144)
R2 = dict(lo=0, keep=8, idx=(16, 24), w=32, words=96)
R3 = dict(lo=0, keep=8, idx=(16,), w=24, words=88)
R4 = dict(lo=0, keep=8, col=16, w=24, words=32)


def piece_of(dram, i):
    return dram[bass.ds(i * PIECE, PIECE)].rearrange("c p w -> p c w")


def cells(ph):
    return {"pos": ph.sb("pos", [P, PT, 3]), "in": ph.sb("in", [P, PT, 3]), "whole": ph.sb("whole", [P, PT, 3], I32),
            "cell": ph.sb("cell", [P, PT, 3]), "w2": ph.sb("w2", [P, PT, 3, 2]), "bc": ph.sb("bc", [P, PT, 2, 2])}


def spline_cells(dve, u, s):
    dve.tensor_scalar(s["pos"][:, :, :], u, 4.0, None, ALU.mult)
    dve.drain()
    dve.tensor_scalar(s["in"][:, :, :], s["pos"][:, :, :], 0.0, 3.5, ALU.max, ALU.min)
    dve.drain()
    dve.tensor_copy(s["whole"][:, :, :], s["in"][:, :, :])
    dve.drain()
    dve.tensor_tensor(s["cell"][:, :, :], s["whole"][:, :, :], s["in"][:, :, :], ALU.is_gt)
    dve.drain()
    dve.tensor_tensor(s["cell"][:, :, :], s["whole"][:, :, :], s["cell"][:, :, :], ALU.subtract)
    dve.drain()
    dve.tensor_tensor(s["w2"][:, :, :, 1], s["pos"][:, :, :], s["cell"][:, :, :], ALU.subtract)
    dve.drain()
    dve.tensor_scalar(s["w2"][:, :, :, 0], s["w2"][:, :, :, 1], -1.0, 1.0, ALU.mult, ALU.add)
    dve.drain()
    dve.tensor_tensor(s["bc"][:, :, :, :], s["w2"][:, :, 1, :].unsqueeze(3).to_broadcast([P, PT, 2, 2]),
                      s["w2"][:, :, 2, :].unsqueeze(2).to_broadcast([P, PT, 2, 2]), ALU.mult)
    dve.drain()


def prepare_by_source(nc, k, rec, r1, r2):
    with Phase(nc, "pa") as ph:
        r = ph.sb("r", [P, 2, PT, WA])
        s = cells(ph)
        knots = ph.sb("knots", [P, PT * 3, 5])
        low = ph.sb("low", [P, PT * 3, 5])
        odd, even, w_a, t0, t1, t2 = (ph.sb(n, [P, PT]) for n in ("odd", "even", "w_a", "t0", "t1", "t2"))
        ends = ph.sb("ends", [P, PT, 2])
        corners = ph.sb("corners", [P, PT, 2, 4])
        one = ph.sb("one", [P, 2, PIECE, R1["words"]])
        two = ph.sb("two", [P, 2, PIECE, R2["words"]])
        loaded, computed, packed, stored = (
            [ph.sem(f"{n}{q}") for q in range(2)] for n in ("loaded", "computed", "packed", "stored"))
        rec3 = rec.rearrange("(c p t) w -> c p (t w)", p=P, t=CH)

        def by_chunk(ap):
            return ap.rearrange("p (c t) -> p c t", t=CH)

        with nc.Block() as block:
            @block.sync
            def _(sp):
                def body(i):
                    for q in range(2):
                        n = i * 2 + q
                        wait(sp, computed[q], i)
                        sp.dma_start(r[:, q].rearrange("p (c t) w -> p c (t w)", t=CH), piece_of(rec3, n)).then_inc(loaded[q], 16)
                looped(sp, NC // PIECE // 2, body)

            @block.vector
            def _(dve):
                def body(i):
                    for q in range(2):
                        n = i * 2 + q
                        dve.wait_ge(loaded[q], snap(dve, (i + 1) * 16))
                        if q:
                            dve.wait_ge(packed[0], i + 1)
                        else:
                            wait(dve, packed[1], i)
                        wait(dve, stored[q], snap(dve, i * 32))
                        lo, col = r[:, q, :, 0], r[:, q, :, 1]
                        spline_cells(dve, r[:, q, :, 2:5], s)
                        cell = s["cell"][:, :, :].rearrange("p t a -> p (t a)").unsqueeze(2)
                        w2 = s["w2"][:, :, :, :].rearrange("p t a w -> p (t a) w")
                        dve.tensor_tensor(low[:, :, :], k["iota"][:, 0:5].unsqueeze(1).to_broadcast([P, PT * 3, 5]),
                                          cell.to_broadcast([P, PT * 3, 5]), ALU.is_equal)
                        dve.drain()
                        dve.tensor_tensor(knots[:, :, :], low[:, :, :], w2[:, :, 0:1].to_broadcast([P, PT * 3, 5]), ALU.mult)
                        dve.drain()
                        dve.tensor_tensor(low[:, :, 0:4], low[:, :, 0:4], w2[:, :, 1:2].to_broadcast([P, PT * 3, 4]), ALU.mult)
                        dve.drain()
                        dve.tensor_tensor(knots[:, :, 1:5], knots[:, :, 1:5], low[:, :, 0:4], ALU.add)
                        ia, ib, ic = (s["cell"][:, :, n] for n in range(3))
                        dve.tensor_scalar(t0[:, :], ia, 3.0, None, ALU.is_equal)
                        dve.drain()
                        dve.scalar_tensor_tensor(odd[:, :], ia, 1.0, t0[:, :], ALU.is_equal, ALU.add)
                        dve.drain()
                        dve.tensor_scalar(even[:, :], odd[:, :], -1.0, 1.0, ALU.mult, ALU.add)
                        dve.drain()
                        lo_w, hi_w = s["w2"][:, :, 0, 0], s["w2"][:, :, 0, 1]
                        dve.tensor_tensor(t0[:, :], lo_w, even[:, :], ALU.mult)
                        dve.tensor_tensor(t1[:, :], hi_w, odd[:, :], ALU.mult)
                        dve.tensor_tensor(t2[:, :], lo_w, odd[:, :], ALU.mult)
                        dve.tensor_tensor(w_a[:, :], hi_w, even[:, :], ALU.mult)
                        dve.drain()
                        dve.tensor_tensor(ends[:, :, 0], t0[:, :], t1[:, :], ALU.add)
                        dve.tensor_tensor(ends[:, :, 1], t2[:, :], w_a[:, :], ALU.add)
                        dve.drain()
                        dve.tensor_tensor(corners[:, :, :, :], ends[:, :, :].unsqueeze(3).to_broadcast([P, PT, 2, 4]),
                                          s["bc"][:, :, :, :].rearrange("p t b c -> p t (b c)").unsqueeze(2).to_broadcast([P, PT, 2, 4]),
                                          ALU.mult)
                        dve.scalar_tensor_tensor(t2[:, :], ib, 5.0, ic, ALU.mult, ALU.add)
                        dve.tensor_tensor(t0[:, :], ia, odd[:, :], ALU.add)
                        dve.tensor_tensor(t1[:, :], ia, odd[:, :], ALU.subtract)
                        dve.drain()
                        dve.scalar_tensor_tensor(t0[:, :], t0[:, :], 12.5, t2[:, :], ALU.mult, ALU.add)
                        dve.scalar_tensor_tensor(t1[:, :], t1[:, :], 12.5, t2[:, :], ALU.mult, ALU.add)
                        dve.drain()
                        for o, t, rows in zip(R2["idx"], (t0, t1), (75.0, 50.0)):
                            dve.scalar_tensor_tensor(two[:, q, :, o:o + CH].bitcast(I32), by_chunk(col), rows, by_chunk(t[:, :]),
                                                     ALU.mult, ALU.add)
                        dve.tensor_copy(one[:, q, :, R1["col"]:R1["col"] + CH].bitcast(I32), by_chunk(col))
                        for dst, rr in ((one[:, q], R1), (two[:, q], R2)):
                            dve.tensor_copy(dst[:, :, rr["lo"]:rr["lo"] + CH], by_chunk(lo))
                            dve.tensor_copy(dst[:, :, rr["keep"]:rr["keep"] + CH], by_chunk(part(k["keep"], n, PT)))
                        dve.drain().then_inc(computed[q], 1)
                looped(dve, NC // PIECE // 2, body)

            @block.scalar
            def _(act):
                def body(i):
                    for q in range(2):
                        n = i * 2 + q
                        act.wait_ge(computed[q], i + 1)
                        act.activation(one[:, q, :, R1["hats"]:], knots[:, :, :].rearrange("p (c t) n -> p c (t n)", t=CH * 3), ACT.Copy)
                        act.activation(two[:, q, :, R2["w"]:], corners[:, :, :, :].rearrange("p (c t) a w -> p c (t a w)", t=CH), ACT.Copy)
                        act.drain().then_inc(packed[q], 1)
                        act.wait_ge(packed[q], i + 1)
                        act.dma_start(piece_of(r1, n), one[:, q]).then_inc(stored[q], 16)
                        act.dma_start(piece_of(r2, n), two[:, q]).then_inc(stored[q], 16)
                looped(act, NC // PIECE // 2, body)
                for q in range(2):
                    act.wait_ge(stored[q], 32 * (NC // PIECE // 2))


def prepare_moved(nc, k, r1, moved, r3):
    with Phase(nc, "pm") as ph:
        old = ph.sb("old", [P, 2, PIECE, 24])
        u = ph.sb("u", [P, 2, PIECE, CH * 3])
        s = cells(ph)
        t0, t1 = ph.sb("t0", [P, PT]), ph.sb("t1", [P, PT])
        corners = ph.sb("corners", [P, PT, 4, 2])
        out = ph.sb("out", [P, 2, PIECE, R3["words"]])
        loaded, computed, packed, stored = (
            [ph.sem(f"{n}{q}") for q in range(2)] for n in ("loaded", "computed", "packed", "stored"))
        with nc.Block() as block:
            @block.sync
            def _(sp):
                def body(i):
                    for q in range(2):
                        n = i * 2 + q
                        wait(sp, computed[q], i)
                        sp.dma_start(old[:, q], piece_of(r1[:, :, 0:24], n)).then_inc(loaded[q], 16)
                        sp.dma_start(u[:, q], piece_of(moved, n)).then_inc(loaded[q], 16)
                looped(sp, NC // PIECE // 2, body)

            @block.vector
            def _(dve):
                def body(i):
                    for q in range(2):
                        n = i * 2 + q
                        dve.wait_ge(loaded[q], snap(dve, (i + 1) * 32))
                        if q:
                            dve.wait_ge(packed[0], i + 1)
                        else:
                            wait(dve, packed[1], i)
                        wait(dve, stored[q], snap(dve, i * 16))
                        spline_cells(dve, u[:, q, :, :].rearrange("p c (t a) -> p (c t) a", a=3), s)
                        dve.tensor_tensor(corners[:, :, :, :], s["w2"][:, :, 0, :].unsqueeze(2).to_broadcast([P, PT, 4, 2]),
                                          s["bc"][:, :, :, :].rearrange("p t b c -> p t (b c)").unsqueeze(3).to_broadcast([P, PT, 4, 2]),
                                          ALU.mult)
                        ia, ib, ic = (s["cell"][:, :, n] for n in range(3))
                        dve.scalar_tensor_tensor(t0[:, :], ib, 5.0, ic, ALU.mult, ALU.add)
                        dve.tensor_scalar(t1[:, :], ia, 2.0, 73.0, ALU.is_ge, ALU.mult)
                        dve.drain()
                        dve.scalar_tensor_tensor(t0[:, :], t0[:, :], 3.0, ia, ALU.mult, ALU.add)
                        dve.drain()
                        dve.tensor_tensor(t0[:, :], t0[:, :], t1[:, :], ALU.add)
                        dve.drain()
                        o = R3["idx"][0]
                        dve.scalar_tensor_tensor(out[:, q, :, o:o + CH].bitcast(I32), old[:, q, :, R1["col"]:R1["col"] + CH].bitcast(I32),
                                                 float(KW), t0[:, :].rearrange("p (c t) -> p c t", t=CH), ALU.mult, ALU.add)
                        dve.tensor_copy(out[:, q, :, 0:CH], old[:, q, :, 0:CH])
                        dve.tensor_copy(out[:, q, :, R3["keep"]:R3["keep"] + CH], old[:, q, :, R1["keep"]:R1["keep"] + CH])
                        dve.drain().then_inc(computed[q], 1)
                looped(dve, NC // PIECE // 2, body)

            @block.scalar
            def _(act):
                def body(i):
                    for q in range(2):
                        n = i * 2 + q
                        act.wait_ge(computed[q], i + 1)
                        act.activation(out[:, q, :, R3["w"]:], corners[:, :, :, :].rearrange("p (c t) a w -> p c (t a w)", t=CH), ACT.Copy)
                        act.drain().then_inc(packed[q], 1)
                        act.wait_ge(packed[q], i + 1)
                        act.dma_start(piece_of(r3, n), out[:, q]).then_inc(stored[q], 16)
                looped(act, NC // PIECE // 2, body)
                for q in range(2):
                    act.wait_ge(stored[q], 16 * (NC // PIECE // 2))


def prepare_by_target(nc, k, rec, r4):
    with Phase(nc, "pb") as ph:
        r = ph.sb("r", [P, PT, WB])
        out = ph.sb("out", [P, PIECE, R4["words"]])
        loaded, packed, stored = (ph.sem(n) for n in ("loaded", "packed", "stored"))
        rec3 = rec.rearrange("(c p t) w -> c p (t w)", p=P, t=CH)
        with nc.Block() as block:
            @block.sync
            def _(sp):
                def body(i):
                    wait(sp, packed, i)
                    sp.dma_start(r[:, :, :].rearrange("p (c t) w -> p c (t w)", t=CH), piece_of(rec3, i)).then_inc(loaded, 16)
                    sp.wait_ge(packed, i + 1)
                    sp.dma_start(piece_of(r4, i), out[:, :, :]).then_inc(stored, 16)
                looped(sp, NC // PIECE, body)
                sp.wait_ge(stored, 16 * (NC // PIECE))

            @block.vector
            def _(dve):
                def body(i):
                    dve.wait_ge(loaded, (i + 1) * 16)
                    wait(dve, stored, i * 16)
                    for o, field in ((R4["lo"], 0), (R4["w"], 2)):
                        dve.tensor_copy(out[:, :, o:o + CH], r[:, :, field].rearrange("p (c t) -> p c t", t=CH))
                    dve.tensor_copy(out[:, :, R4["col"]:R4["col"] + CH].bitcast(I32), r[:, :, 1].rearrange("p (c t) -> p c t", t=CH))
                    dve.tensor_copy(out[:, :, R4["keep"]:R4["keep"] + CH],
                                    part(k["keep"], i, PT).rearrange("p (c t) -> p c t", t=CH))
                    dve.drain().then_inc(packed, 1)

                looped(dve, NC // PIECE, body)
class Count:

    def __init__(self, eng, i):
        self.eng, self.i, self.known = eng, i, {}

    def __call__(self, times, more):
        if (times, more) not in self.known:
            v = (self.i + more) * times
            self.known[times, more] = v if isinstance(v, int) else self.eng.snap(v)
        return self.known[times, more]


def stages(eng, steps):
    def body(c, first, last):
        for q in range(RING):
            for lag, step in steps:
                if (first and q < lag) or (last and q >= lag):
                    continue
                step(c, (q - lag) % RING, 1 if q >= lag else 0)
    body(Count(eng, 0), True, False)
    with eng.Fori(1, NI) as i:
        body(Count(eng, i), False, False)
    body(Count(eng, NI), False, True)


def two_before(q, m):
    return (q + 2) % RING, m if q >= 2 else m - 1


def banks_of(ph, name, width):
    per = min(CH, 512 // width)
    tiles = [[ph.ps(f"{name}{r}_{b}", [P, 512]) for b in range(-(-CH // per))] for r in range(2)]
    return lambda r, j: tiles[r][j // per][:, (j % per) * width:(j % per + 1) * width]


def segment_pass(nc, name, k, rec, r, gathers, outs, products, prepare=None, weigh=None, scale=None):
    words, ng = r["words"], len(gathers)
    with Phase(nc, name) as ph:
        recs = ph.sb("recs", [P, RING, words])
        rows = [ph.sb(f"rows{n}", [P, RING, CH, run]) for n, (_, _, run) in enumerate(gathers)]
        onehot = ph.sb("onehot", [P, 2, CH, P])
        carried = [ph.sb(f"carried{n}", [P, 2, CH, w]) for n, (w, _) in enumerate(outs)]
        sums = [banks_of(ph, f"sums{n}", w) for n, (w, _) in enumerate(outs)]
        extra = prepare(ph) if prepare else None
        loaded, gathered, built, summed, chained, stored = (
            ph.ring(n) for n in ("ld", "ga", "bu", "su", "ch", "st"))
        GATHERED, STORED = 16 * CH * ng, 16 * len(outs)

        with nc.Block() as block:
            @block.sync
            def _(sp):
                def load(c, q, m):
                    wait(sp, chained[q], c(1, m - 1))
                    sp.dma_start(recs[:, q, :], at(rec, chunk(c, q, m))).then_inc(loaded[q], 16)
                stages(sp, [(0, load)])

            @block.gpsimd
            def _(pool):
                def gather(c, q, m):
                    pool.wait_ge(loaded[q], c(16, m))
                    wait(pool, summed[q], c(1, m - 1))
                    pool.nop(nofuse=True)
                    for j in range(CH):
                        for (table, col, run), dst in zip(gathers, rows):
                            pool.indirect_dma_start(
                                out=dst[:, q, j, :], out_offset=None, in_=table,
                                in_offset=bass.IndirectOffsetOnAxis(ap=recs[:, q, col + j:col + j + 1].bitcast(I32), axis=0),
                            ).then_inc(gathered[q], 16)
                stages(pool, [(0, gather)])

            @block.vector
            def _(dve):
                for t in carried:
                    dve.memset(t[:, :, :, :], 0.0)
                if extra:
                    extra["init"](dve)
                dve.drain()

                def build(c, q, m):
                    free, n = two_before(q, m)
                    dve.wait_ge(loaded[q], c(16, m))
                    wait(dve, summed[free], c(1, n))
                    for j in range(CH):
                        lo = recs[:, q, r["lo"] + j:r["lo"] + j + 1]
                        if scale is None:
                            dve.tensor_scalar(onehot[:, q % 2, j, :], k["iota"][:, 0:P], lo, None, ALU.is_equal)
                        else:
                            dve.tensor_scalar(onehot[:, q % 2, j, :], k["iota"][:, 0:P], lo,
                                              recs[:, q, scale + j:scale + j + 1], ALU.is_equal, ALU.mult)
                    if extra:
                        extra["build"](dve, recs[:, q, :], q % 2)
                    if weigh:
                        dve.wait_ge(gathered[q], c(GATHERED, m))
                        weigh(dve, recs[:, q, :], [t[:, q] for t in rows])
                    dve.drain().then_inc(built[q], 1)

                def chain(c, q, m):
                    free, n = two_before(q, m)
                    dve.wait_ge(summed[q], c(1, m))
                    wait(dve, stored[free], c(STORED, n))
                    for j in range(CH):
                        for t, s in zip(carried, sums):
                            before = t[:, q % 2, j - 1, :] if j else t[:, 1 - q % 2, CH - 1, :]
                            dve.scalar_tensor_tensor(t[:, q % 2, j, :], before, recs[:, q, r["keep"] + j:r["keep"] + j + 1],
                                                     s(q % 2, j), ALU.mult, ALU.add)
                        last = dve.drain()
                    last.then_inc(chained[q], 1)
                stages(dve, [(0, build), (1, chain)])

            @block.tensor
            def _(pe):
                def multiply(c, q, m):
                    free, n = two_before(q, m)
                    pe.wait_ge(built[q], c(1, m))
                    pe.wait_ge(gathered[q], c(GATHERED, m))
                    wait(pe, chained[free], c(1, n))
                    for j in range(CH):
                        for out, operands in enumerate(products([t[:, q, j] for t in rows], q % 2, j, extra)):
                            for a, rhs in enumerate(operands):
                                ins = pe.matmul(sums[out](q % 2, j), onehot[:, q % 2, j, :], rhs,
                                                start=a == 0, stop=a == len(operands) - 1)
                    ins.then_inc(summed[q], 1)
                stages(pe, [(0, multiply)])

            @block.scalar
            def _(act):
                def store(c, q, m):
                    act.wait_ge(chained[q], c(1, m))
                    for t, (w, dram) in zip(carried, outs):
                        act.dma_start(at(dram, chunk(c, q, m)), t[:, q % 2].rearrange("p j w -> p (j w)")).then_inc(stored[q], 16)
                stages(act, [(0, store)])
                for q in range(RING):
                    act.wait_ge(stored[q], STORED * NI)


def chunk(c, q, m):
    return (c.i + (m - 1)) * RING + q


def block_sums(nc, name, k, results):
    READ = 28
    LAST_ROW = (NC - 1) * CH * P + CH - 1
    with Phase(nc, name) as ph:
        got = [ph.sem(f"got{n}") for n in range(3)]
        by_row = [bass.AP(dram.tensor, dram.offset, [[w, LAST_ROW + 1], [CH * w, P], [1, w]]) for w, dram, _ in results]

        def read(eng, n):
            with eng.Fori(n * READ, (n + 1) * READ) as b:
                row = eng.value_load(k["last"][0:1, bass.ds(b, 1)], min_val=0, max_val=LAST_ROW)
                for rows, (_, _, tile) in zip(by_row, results):
                    eng.dma_start(tile[:, bass.ds(b, 1), :].rearrange("p b w -> p (b w)"), at(rows, row)).then_inc(got[n], 16)
            eng.wait_ge(got[n], 16 * READ * len(results))

        with nc.Block() as block:
            @block.sync
            def _(sp):
                read(sp, 0)

            @block.scalar
            def _(act):
                read(act, 1)

            @block.gpsimd
            def _(pool):
                for w, dram, tile in results:
                    rows = dram.rearrange("c p (j w) -> (c p j) w", w=w)
                    for b in range(2 * READ, NB):
                        pool.indirect_dma_start(out=tile[:, b, :], out_offset=None, in_=rows,
                                                in_offset=bass.IndirectOffsetOnAxis(ap=k["last"][:, b:b + 1], axis=0)
                                                ).then_inc(got[2], 16)
                pool.wait_ge(got[2], 16 * (NB - 2 * READ) * len(results))


def corners_of(rows, groups, run, step):
    return [bass.AP(t.tensor, t.offset + o * run, [t.ap[0], [step * run, 2], [1, 2 * run]])
            for t, first in zip(rows, groups) for o in first]


def corner_products(groups, run, step, width):
    def of(rows, r, j, extra):
        corners = corners_of(rows, groups, run, step)
        return [corners if width == 4 * run else [v[:, pair, :] for v in corners for pair in range(2)]]
    return of


def weigh_corners(r, groups, run, step):
    def of(dve, rec, rows):
        w = rec[:, r["w"]:r["w"] + 8 * CH].rearrange("p (t g b c) -> p t g b c", t=CH, g=2, b=2)
        for j in range(CH):
            for g, v in enumerate(corners_of([t[:, j] for t in rows], groups, run, step)):
                v = v.rearrange("p b (c f) -> p b c f", c=2)
                dve.tensor_tensor(v, v, w[:, j, g].unsqueeze(3).to_broadcast([P, 2, 2, run]), ALU.mult)
    return of


def transform(nc, name, k, src, K, weights, M, dst):
    G = 7
    per = 512 // M
    with Phase(nc, name) as ph:
        taken = ph.sb("taken", [P, 2, G, K])
        turned = ph.sb("turned", [P, 2, G * P])
        t_ps = [[ph.ps(f"t{r}{n}", [P, 512]) for n in range(2)] for r in range(2)]
        o_ps = [[ph.ps(f"o{r}{n}", [P, 512]) for n in range(-(-G // per))] for r in range(2)]
        copied, transposed, moved, multiplied, out_copied = (
            [ph.sem(f"{n}{r}") for r in range(2)] for n in ("copied", "transposed", "moved", "multiplied", "out_copied"))

        with nc.Block() as block:
            @block.scalar
            def _(act):
                def take(r, i):
                    wait(act, transposed[r], i)
                    act.activation(taken[:, r], part(src, i * 2 + r, G)[:, :, 0:K], ACT.Copy).then_inc(copied[r], 1)

                def copy_out(r, i):
                    act.wait_ge(multiplied[r], snap(act, i + 1))
                    for n, o in enumerate(o_ps[r]):
                        g = min(per, G - n * per)
                        act.activation(dst[:, bass.ds((i * 2 + r) * G + n * per, g), :],
                                       o[:, 0:g * M].rearrange("p (g m) -> p g m", m=M), ACT.Copy)
                    act.drain().then_inc(out_copied[r], 1)

                def body(i):
                    for r in range(2):
                        take(r, i)
                        if not isinstance(i, int):
                            copy_out(r, i - 1)
                looped(act, NB // G // 2, body)
                for r in range(2):
                    copy_out(r, NB // G // 2 - 1)

            @block.vector
            def _(dve):
                def body(i):
                    for r in range(2):
                        dve.wait_ge(transposed[r], snap(dve, i + 1))
                        wait(dve, multiplied[r], i)
                        dve.tensor_copy(turned[0:K, r, 0:4 * P], t_ps[r][0][0:K, :])
                        dve.tensor_copy(turned[0:K, r, 4 * P:], t_ps[r][1][0:K, 0:(G - 4) * P])
                        dve.drain().then_inc(moved[r], 1)
                looped(dve, NB // G // 2, body)

            @block.tensor
            def _(pe):
                def transpose(r, i):
                    pe.wait_ge(copied[r], snap(pe, i + 1))
                    wait(pe, moved[r], i)
                    pe.nop(nofuse=True)
                    for g in range(G):
                        ins = pe.transpose(t_ps[r][g // 4][0:K, (g % 4) * P:(g % 4 + 1) * P], taken[:, r, g, :], k["ident"][:, :])
                    ins.then_inc(transposed[r], 1)

                def multiply(r, i):
                    pe.wait_ge(moved[r], snap(pe, i + 1))
                    wait(pe, out_copied[r], i)
                    for g in range(G):
                        ins = pe.matmul(o_ps[r][g // per][:, (g % per) * M:(g % per + 1) * M],
                                        turned[0:K, r, g * P:(g + 1) * P], weights, start=True, stop=True)
                    ins.then_inc(multiplied[r], 1)

                def body(i, first=False):
                    transpose(0, i)
                    if not first:
                        multiply(1, i - 1)
                    transpose(1, i)
                    multiply(0, i)
                body(0, first=True)
                body(1)
                with pe.Fori(2, NB // G // 2) as i:
                    body(i)
                multiply(1, NB // G // 2 - 1)


def turn_blocks(nc, name, k, src, K, blocks, dst):
    with Phase(nc, name) as ph:
        taken = ph.sb("taken", [P, 2, 4, K])
        t_ps = [ph.ps(f"t{r}", [P, 512]) for r in range(2)]
        copied, transposed, moved = ([ph.sem(f"{n}{r}") for r in range(2)] for n in ("copied", "transposed", "moved"))
        with nc.Block() as block:
            @block.scalar
            def _(act):
                def body(i):
                    for r in range(2):
                        wait(act, transposed[r], i)
                        act.activation(taken[:, r], part(src, i * 2 + r, 4), ACT.Copy).then_inc(copied[r], 1)
                looped(act, blocks // 8, body)

            @block.vector
            def _(dve):
                def body(i):
                    done = snap(dve, i + 1)
                    for r in range(2):
                        dve.wait_ge(transposed[r], done)
                        dve.tensor_copy(dst[0:K, bass.ds((i * 2 + r) * (4 * P), 4 * P)], t_ps[r][0:K, :]).then_inc(moved[r], 1)
                looped(dve, blocks // 8, body)

            @block.tensor
            def _(pe):
                def body(i):
                    done = snap(pe, i + 1)
                    for r in range(2):
                        pe.wait_ge(copied[r], done)
                        wait(pe, moved[r], i)
                        pe.nop(nofuse=True)
                        for g in range(4):
                            ins = pe.transpose(t_ps[r][0:K, g * P:(g + 1) * P], taken[:, r, g, :], k["ident"][:, :])
                        ins.then_inc(transposed[r], 1)
                looped(pe, blocks // 8, body)


def elu(nc, name, h, scale=None, bias=None):
    M = h.shape[2]
    with Phase(nc, name) as ph:
        low = ph.sb("low", [P, NB, M])
        ready, powered = ph.sem("ready"), ph.sem("powered")
        with nc.Block() as block:
            @block.vector
            def _(dve):
                if scale is not None:
                    dve.tensor_tensor(h[:, :, :], h[:, :, :], scale.unsqueeze(2).to_broadcast([P, NB, M]), ALU.mult)
                    dve.drain()
                if bias is not None:
                    dve.tensor_tensor(h[:, :, :], h[:, :, :], bias.unsqueeze(1).to_broadcast([P, NB, M]), ALU.add)
                    dve.drain()
                dve.tensor_scalar(low[:, :, :], h[:, :, :], 0.0, None, ALU.min).then_inc(ready, 1)
                dve.tensor_scalar(h[:, :, :], h[:, :, :], 0.0, None, ALU.max)
                dve.wait_ge(powered, 1)
                dve.drain()
                dve.scalar_tensor_tensor(h[:, :, :], low[:, :, :], -1.0, h[:, :, :], ALU.add, ALU.add)

            @block.scalar
            def _(act):
                act.wait_ge(ready, 1)
                act.activation(low[:, :, :], low[:, :, :], ACT.Exp).then_inc(powered, 1)


def on_vector(nc, name, work):
    with nc.Block() as block:
        @block.vector
        def _(dve):
            work(dve)


def load(nc, name, pairs):
    with Phase(nc, name) as ph:
        moved = ph.sem("moved")
        with nc.Block() as block:
            @block.sync
            def _(sp):
                with nc.allow_non_contiguous_dma(reason="small transposed weights"):
                    for dst, src in pairs:
                        sp.dma_start(dst, src).then_inc(moved, 16)
                sp.wait_ge(moved, 16 * len(pairs))


def split_parts(dve, x, rest, parts):
    for n in range(3):
        dve.tensor_copy(parts[:, :, n, :], x if n == 0 else rest)
        dve.drain()
        if n < 2:
            dve.tensor_tensor(rest, x if n == 0 else rest, parts[:, :, n, :], ALU.subtract)
            dve.drain()


def by_tile(nc, name, k, table, w, spread):
    with Phase(nc, name) as ph:
        rows = ph.sb("rows", [P, T // P, P * w], BF16)
        got, stored = ph.sem("got"), ph.sem("stored")
        blocks = table.rearrange("(b p) w -> b (p w)", p=P)
        with nc.Block() as block:
            @block.gpsimd
            def _(pool):
                for n in range(T // P):
                    pool.indirect_dma_start(out=rows[:, n, :], out_offset=None, in_=blocks,
                                            in_offset=bass.IndirectOffsetOnAxis(ap=k["tile_block"][:, n:n + 1], axis=0)
                                            ).then_inc(got, 16)

            @block.sync
            def _(sp):
                sp.wait_ge(got, 16 * (T // P))
                sp.dma_start(spread.rearrange("(n p) w -> p n w", p=P), rows[:, :, :]).then_inc(stored, 16)
                sp.wait_ge(stored, 16)


def turn_steps(ph, k, recs, lo, loaded, per_load, users_done, onehot, turned, t_ps, hot, transposed, copied):
    def make_hot(dve):
        def step(c, q, m):
            free, n = two_before(q, m)
            dve.wait_ge(loaded[q], c(per_load, m))
            wait(dve, users_done[free], c(1, n))
            for j in range(CH):
                dve.tensor_scalar(onehot[:, q % 2, j, :], k["iota"][:, 0:P], recs[:, q, lo + j:lo + j + 1], None, ALU.is_equal)
            dve.drain().then_inc(hot[q], 1)
        return step

    def transpose(pe):
        def step(c, q, m):
            free, n = two_before(q, m)
            pe.wait_ge(hot[q], c(1, m))
            wait(pe, copied[free], c(1, n))
            for j in range(CH):
                ins = pe.transpose(t_ps[q % 2][:, j * P:(j + 1) * P], onehot[:, q % 2, j, :], k["ident_b"][:, :])
            ins.then_inc(transposed[q], 1)
        return step

    def copy(act):
        def step(c, q, m):
            free, n = two_before(q, m)
            act.wait_ge(transposed[q], c(1, m))
            wait(act, users_done[free], c(1, n))
            act.activation(turned[:, q % 2, :], t_ps[q % 2][:, :], ACT.Copy).then_inc(copied[q], 1)
        return step
    return make_hot, transpose, copy


def move_pass(nc, k, rec, r1, table, spread, moved, turned_src, K, weights, z_table):
    W = 4
    GROUPS = 5
    PIECE_Z = weights.shape[1] // (2 * GROUPS)
    with Phase(nc, "mv") as ph:
        recs = ph.sb("recs", [P, RING, 24])
        raw = ph.sb("raw", [P, RING, CH, WA])
        tabs = ph.sb("tabs", [P, RING, CH, 3 * W], BF16)
        own = ph.sb("own", [P, CH, W])
        rows = ph.sb("rows", [P, 2, CH, W])
        out = ph.sb("out", [P, 2, CH, 3])
        onehot = ph.sb("onehot", [P, 2, CH, P], BF16)
        turned = ph.sb("turned", [P, 2, CH * P], BF16)
        t_ps = [ph.ps(f"t{r}", [P, CH * P], BF16) for r in range(2)]
        l_ps = [ph.ps(f"l{r}", [P, 512]) for r in range(2)]
        z_ps = [ph.ps(f"z_ps{r}", [P, 512]) for r in range(2)]
        operand = ph.sb("operand", [P, 2, P])
        z = [ph.sb(f"z{r}", [P, weights.shape[1]]) for r in range(2)]
        picked, z_stored = ([ph.sem(f"{n}{r}") for r in range(2)] for n in ("picked", "z_stored"))
        z_made, z_read = ([[ph.sem(f"{n}{q}{g}") for g in range(GROUPS)] for q in range(RING)] for n in ("z_made", "z_read"))
        loaded, gathered, hot, transposed, copied, looked, finished, stored = (
            ph.ring(n) for n in ("ld", "ga", "ho", "tr", "co", "lo", "fi", "st"))
        make_hot, transpose, copy = turn_steps(ph, k, recs, R1["lo"], loaded, 48, finished, onehot, turned, t_ps,
                                               hot, transposed, copied)
        rec3 = rec.rearrange("(c p t) w -> c p (t w)", p=P, t=CH)
        spread4 = spread.rearrange("(c t) (n w) -> c n t w", t=CH, w=3 * W)
        with nc.Block() as block:
            @block.sync
            def _(sp):
                def step(c, q, m):
                    wait(sp, finished[q], c(1, m - 1))
                    n = chunk(c, q, m)
                    sp.dma_start(recs[:, q, :], at(r1[:, :, 0:24], n)).then_inc(loaded[q], 16)
                    sp.dma_start(raw[:, q].rearrange("p t w -> p (t w)"), at(rec3, n)).then_inc(loaded[q], 16)
                    sp.dma_start(tabs[:, q], at(spread4, n)).then_inc(loaded[q], 16)

                def store_z(c, q, m):
                    if q % 2:
                        sp.wait_ge(z_read[q][GROUPS - 1], c(1, m))
                        sp.dma_start(at(z_table, c.i * 2 + (q // 2 + 2 * (m - 1))), z[q // 2][:, :]).then_inc(z_stored[q // 2], 16)
                stages(sp, [(0, step), (2, store_z)])
                for r in range(2):
                    sp.wait_ge(z_stored[r], 16 * NI)

            @block.gpsimd
            def _(pool):
                def step(c, q, m):
                    free, n = two_before(q, m)
                    pool.wait_ge(loaded[q], c(48, m))
                    wait(pool, finished[free], c(1, n))
                    pool.nop(nofuse=True)
                    for j in range(CH):
                        o = R1["col"] + j
                        pool.indirect_dma_start(out=rows[:, q % 2, j, :], out_offset=None, in_=table,
                                                in_offset=bass.IndirectOffsetOnAxis(ap=recs[:, q, o:o + 1].bitcast(I32), axis=0)
                                                ).then_inc(gathered[q], 16)
                stages(pool, [(0, step)])

            @block.vector
            def _(dve):
                def finish(c, q, m):
                    free, n = two_before(q, m)
                    dve.wait_ge(gathered[q], c(16 * CH, m))
                    dve.wait_ge(looked[q], c(1, m))
                    wait(dve, stored[free], c(16, n))
                    o = out[:, q % 2]
                    dve.tensor_reduce(own[:, :, :], l_ps[q % 2][:, 0:CH * 3 * W].rearrange("p (t s w) -> p t w s", s=3, w=W),
                                      axis=AX, op=ALU.add)
                    dve.tensor_tensor(o, raw[:, q, :, 2:5], rows[:, q % 2, :, 0:3], ALU.add)
                    dve.drain()
                    dve.tensor_tensor(o, o, own[:, :, 0:3], ALU.subtract)
                    dve.drain()
                    dve.tensor_scalar(o, o, 0.0, 1.0, ALU.max, ALU.min).then_inc(finished[q], 1)

                def pick(c, q, m):
                    if q % 2 == 0:
                        wait(dve, z_made[q + 1][GROUPS - 1], c(1, m - 1))
                        dve.tensor_copy(operand[0:K, q // 2, :],
                                        turned_src[0:K, bass.ds((c.i * 2 + q // 2) * P, P)]).then_inc(picked[q // 2], 1)
                stages(dve, [(0, pick), (0, make_hot(dve)), (1, finish)])

            @block.tensor
            def _(pe):
                def look_up(c, q, m):
                    free, n = two_before(q, m)
                    pe.wait_ge(copied[q], c(1, m))
                    pe.wait_ge(loaded[q], c(48, m))
                    wait(pe, finished[free], c(1, n))
                    for j in range(CH):
                        ins = pe.matmul(l_ps[q % 2][:, j * 3 * W:(j + 1) * 3 * W], turned[:, q % 2, j * P:(j + 1) * P], tabs[:, q, j, :],
                                        start=True, stop=True)
                    ins.then_inc(looked[q], 1)

                def multiply(c, q, m):
                    if q % 2 == 0:
                        pe.wait_ge(picked[q // 2], c(1, m))
                    for g in range(GROUPS):
                        if g >= 2:
                            pe.wait_ge(z_read[q][g - 2], c(1, m))
                        else:
                            wait(pe, z_read[(q + 3) % RING][GROUPS - 2 + g], c(1, m if q else m - 1))
                        o = ((q % 2) * GROUPS + g) * PIECE_Z
                        pe.matmul(z_ps[(q * GROUPS + g) % 2][:, 0:PIECE_Z], operand[0:K, q // 2, :], weights[:, o:o + PIECE_Z],
                                  start=True, stop=True).then_inc(z_made[q][g], 1)
                stages(pe, [(0, transpose(pe)), (1, look_up), (0, multiply)])

            @block.scalar
            def _(act):
                def store(c, q, m):
                    act.wait_ge(finished[q], c(1, m))
                    act.dma_start(at(moved, chunk(c, q, m)), out[:, q % 2].rearrange("p t w -> p (t w)")).then_inc(stored[q], 16)

                def take(c, q, m):
                    if q % 2 == 0:
                        wait(act, z_stored[q // 2], c(16, m - 1))
                    for g in range(GROUPS):
                        act.wait_ge(z_made[q][g], c(1, m))
                        o = ((q % 2) * GROUPS + g) * PIECE_Z
                        act.activation(z[q // 2][:, o:o + PIECE_Z], z_ps[(q * GROUPS + g) % 2][:, 0:PIECE_Z],
                                       ACT.Copy).then_inc(z_read[q][g], 1)
                stages(act, [(0, copy(act)), (1, store), (0, take)])
                for q in range(RING):
                    act.wait_ge(stored[q], 16 * NI)


def max_pass(nc, k, r4, table, kept_rows, maxima):
    W = D + 4
    HALF = CH // 2
    with Phase(nc, "mx") as ph:
        recs = ph.sb("recs", [P, RING, R4["words"]])
        rows = ph.sb("rows", [P, RING, CH, W])
        other = ph.sb("other", [P, 2, CH, P], BF16)
        tile_max = ph.sb("tile_max", [P, CH, 4])
        drop = ph.sb("drop", [P, CH])
        carried = ph.sb("carried", [P, 2, CH, 4])
        banks = [ph.ps(f"s{n}", [P, 512]) for n in range(CH)]
        loaded, gathered, masked, chained, stored, rows_stored = (ph.ring(n) for n in ("ld", "ga", "ma", "ch", "st", "rs"))
        scored, reduced = ([[ph.sem(f"{n}{q}{h}") for h in range(2)] for q in range(RING)] for n in ("sc", "re"))

        def one_before(q, m):
            return (q + 3) % RING, m if q >= 1 else m - 1

        with nc.Block() as block:
            @block.sync
            def _(sp):
                def step(c, q, m):
                    wait(sp, chained[q], c(1, m - 1))
                    sp.dma_start(recs[:, q, :], at(r4, chunk(c, q, m))).then_inc(loaded[q], 16)

                def keep_rows(c, q, m):
                    sp.wait_ge(gathered[q], c(16 * CH, m))
                    sp.dma_start(at(kept_rows, chunk(c, q, m)), rows[:, q].rearrange("p j w -> p (j w)")).then_inc(rows_stored[q], 16)
                stages(sp, [(0, step), (2, keep_rows)])
                for q in range(RING):
                    sp.wait_ge(rows_stored[q], 16 * NI)

            @block.gpsimd
            def _(pool):
                def step(c, q, m):
                    pool.wait_ge(loaded[q], c(16, m))
                    wait(pool, scored[q][1], c(1, m - 1))
                    wait(pool, rows_stored[q], c(16, m - 1))
                    pool.nop(nofuse=True)
                    for j in range(CH):
                        o = R4["col"] + j
                        pool.indirect_dma_start(out=rows[:, q, j, :], out_offset=None, in_=table,
                                                in_offset=bass.IndirectOffsetOnAxis(ap=recs[:, q, o:o + 1].bitcast(I32), axis=0)
                                                ).then_inc(gathered[q], 16)
                stages(pool, [(0, step)])

            @block.vector
            def _(dve):
                dve.memset(carried[:, :, :, :], 0.0)
                dve.drain()

                def mask(c, q, m):
                    free, n = two_before(q, m)
                    dve.wait_ge(loaded[q], c(16, m))
                    wait(dve, scored[free][1], c(1, n))
                    for j in range(CH):
                        o = R4["lo"] + j
                        dve.tensor_scalar(other[:, q % 2, j, :], k["iota"][:, 0:P], recs[:, q, o:o + 1], -NEG, ALU.not_equal, ALU.mult)
                    dve.drain().then_inc(masked[q], 1)

                def chain(c, q, m):
                    free, n = two_before(q, m)
                    dve.tensor_scalar(drop[:, :], recs[:, q, R4["keep"]:R4["keep"] + CH], -1.0, NEG, ALU.add, ALU.mult)
                    for h in range(2):
                        dve.wait_ge(scored[q][h], c(1, m))
                        for j in range(HALF * h, HALF * (h + 1)):
                            ins = dve.tensor_reduce(tile_max[:, j, :], banks[j][:, :].rearrange("p (h e) -> p h e", e=P), axis=AX, op=ALU.max)
                        ins.then_inc(reduced[q][h], 1)
                    dve.drain()
                    wait(dve, stored[free], c(16, n))
                    for j in range(CH):
                        if j:
                            dve.drain()
                        before = carried[:, q % 2, j - 1, :] if j else carried[:, 1 - q % 2, CH - 1, :]
                        dve.scalar_tensor_tensor(carried[:, q % 2, j, :], before, drop[:, j:j + 1], tile_max[:, j, :], ALU.add, ALU.max)
                    dve.drain().then_inc(chained[q], 1)
                stages(dve, [(0, mask), (1, chain)])

            @block.tensor
            def _(pe):
                def score(c, q, m):
                    free, n = one_before(q, m)
                    pe.wait_ge(masked[q], c(1, m))
                    pe.wait_ge(gathered[q], c(16 * CH, m))
                    for h in range(2):
                        wait(pe, reduced[free][h], c(1, n))
                        for j in range(HALF * h, HALF * (h + 1)):
                            pe.matmul(banks[j][:, :], other[:, q % 2, j, :], k["ident_b"][:, :].unsqueeze(1).to_broadcast([P, 4, P]),
                                      start=True, stop=False, skip_group_check=True)
                            for head in range(4):
                                ins = pe.matmul(banks[j][:, head * P:(head + 1) * P],
                                                rows[:, q, j, D + head:D + head + 1].to_broadcast([P, P]), k["ident"][:, :],
                                                start=False, stop=head == 3, skip_group_check=True)
                        ins.then_inc(scored[q][h], 1)
                stages(pe, [(0, score)])

            @block.scalar
            def _(act):
                def store(c, q, m):
                    act.wait_ge(chained[q], c(1, m))
                    act.dma_start(at(maxima, chunk(c, q, m)), carried[:, q % 2].rearrange("p j w -> p (j w)")).then_inc(stored[q], 16)
                stages(act, [(0, store)])
                for q in range(RING):
                    act.wait_ge(stored[q], 16 * NI)


def attention_pass(nc, k, r4, kept_rows, spread, result):
    W, OUT = 8, 4 * D + 4
    with Phase(nc, "at") as ph:
        recs = ph.sb("recs", [P, RING, R4["words"]])
        rows = ph.sb("rows", [P, RING, CH, D + 4])
        tabs = ph.sb("tabs", [P, RING, CH, 3 * W], BF16)
        own = ph.sb("own", [P, CH, W])
        onehot = ph.sb("onehot", [P, RING, CH, P])
        turned = ph.sb("turned", [P, 2, CH * P], BF16)
        score = ph.sb("score", [P, 2, CH, 4])
        weighted = ph.sb("weighted", [P, 2, CH, OUT])
        carried = ph.sb("carried", [P, 2, CH, OUT])
        t_ps = [ph.ps(f"t{b}", [P, 512]) for b in range(2)]
        s_ps = [[ph.ps(f"s{r}{b}", [P, 512]) for b in range(3)] for r in range(2)]
        l_ps = [s[2][:, 512 - CH * 3 * W:512] for s in s_ps]
        loaded, hot, transposed, copied, looked, scored, powered, built, summed, chained, stored = (
            ph.ring(n) for n in ("ld", "ho", "tr", "co", "lo", "sd", "po", "bu", "su", "ch", "st"))
        spread4 = spread.rearrange("(c t) (n w) -> c n t w", t=CH, w=3 * W)

        def one_before(q, m):
            return (q + 3) % RING, m if q >= 1 else m - 1

        with nc.Block() as block:
            @block.sync
            def _(sp):
                def step(c, q, m):
                    wait(sp, chained[q], c(1, m - 1))
                    n = chunk(c, q, m)
                    sp.dma_start(recs[:, q, :], at(r4, n)).then_inc(loaded[q], 16)
                    sp.dma_start(rows[:, q].rearrange("p j w -> p (j w)"), at(kept_rows, n)).then_inc(loaded[q], 16)
                    sp.dma_start(tabs[:, q], at(spread4, n)).then_inc(loaded[q], 16)
                stages(sp, [(0, step)])

            @block.gpsimd
            def _(pool):
                def make_hot(c, q, m):
                    pool.wait_ge(loaded[q], c(48, m))
                    wait(pool, summed[q], c(1, m - 1))
                    pool.nop(nofuse=True)
                    for j in range(CH):
                        o = R4["lo"] + j
                        pool.tensor_scalar(onehot[:, q, j, :], k["iota"][:, 0:P], recs[:, q, o:o + 1], None, ALU.is_equal)
                    pool.drain().then_inc(hot[q], 1)
                stages(pool, [(0, make_hot)])

            @block.vector
            def _(dve):
                dve.memset(carried[:, :, :, :], 0.0)
                dve.drain()

                def scores(c, q, m):
                    dve.wait_ge(looked[q], c(1, m))
                    dve.tensor_reduce(own[:, :, :], l_ps[q % 2].rearrange("p (t s w) -> p t w s", s=3, w=W), axis=AX, op=ALU.add)
                    dve.drain()
                    s = score[:, q % 2]
                    dve.tensor_tensor(s, rows[:, q, :, D:D + 4], own[:, :, 0:4], ALU.add)
                    dve.drain()
                    dve.scalar_tensor_tensor(s, s, 0.2, s, ALU.mult, ALU.max)
                    dve.drain()
                    dve.tensor_tensor(s, s, own[:, :, 4:8], ALU.subtract)
                    dve.drain()
                    dve.tensor_scalar(s, s, 1.0, None, ALU.min).then_inc(scored[q], 1)

                def weigh(c, q, m):
                    dve.wait_ge(powered[q], c(1, m))
                    wt = weighted[:, q % 2]
                    for head in range(4):
                        dve.tensor_tensor(wt[:, :, head * D:(head + 1) * D], rows[:, q, :, 0:D],
                                          wt[:, :, 4 * D + head:4 * D + head + 1].to_broadcast([P, CH, D]), ALU.mult)
                    dve.drain().then_inc(built[q], 1)

                def chain(c, q, m):
                    free, n = two_before(q, m)
                    dve.wait_ge(summed[q], c(1, m))
                    wait(dve, stored[free], c(16, n))
                    for j in range(CH):
                        before = carried[:, q % 2, j - 1, :] if j else carried[:, 1 - q % 2, CH - 1, :]
                        o = R4["keep"] + j
                        dve.scalar_tensor_tensor(carried[:, q % 2, j, :], before, recs[:, q, o:o + 1],
                                                 s_ps[q % 2][j // 3][:, (j % 3) * OUT:(j % 3 + 1) * OUT], ALU.mult, ALU.add)
                        last = dve.drain()
                    last.then_inc(chained[q], 1)
                stages(dve, [(1, scores), (1, weigh), (2, chain)])

            @block.tensor
            def _(pe):
                def transpose(c, q, m):
                    before, n = one_before(q, m)
                    pe.wait_ge(hot[q], c(1, m))
                    wait(pe, copied[before], c(1, n))
                    for j in range(CH):
                        ins = pe.transpose(t_ps[j // 4][:, (j % 4) * P:(j % 4 + 1) * P], onehot[:, q, j, :], k["ident"][:, :])
                    ins.then_inc(transposed[q], 1)

                def look_up(c, q, m):
                    free, n = two_before(q, m)
                    pe.wait_ge(copied[q], c(1, m))
                    wait(pe, chained[free], c(1, n))
                    for j in range(CH):
                        ins = pe.matmul(l_ps[q % 2][:, j * 3 * W:(j + 1) * 3 * W], turned[:, q % 2, j * P:(j + 1) * P], tabs[:, q, j, :],
                                        start=True, stop=True)
                    ins.then_inc(looked[q], 1)

                def multiply(c, q, m):
                    free, n = two_before(q, m)
                    pe.wait_ge(built[q], c(1, m))
                    wait(pe, chained[free], c(1, n))
                    for j in range(CH):
                        ins = pe.matmul(s_ps[q % 2][j // 3][:, (j % 3) * OUT:(j % 3 + 1) * OUT], onehot[:, q, j, :],
                                        weighted[:, q % 2, j, :], start=True, stop=True)
                    ins.then_inc(summed[q], 1)
                stages(pe, [(2, multiply), (1, look_up), (0, transpose)])

            @block.scalar
            def _(act):
                def copy(c, q, m):
                    free, n = two_before(q, m)
                    act.wait_ge(transposed[q], c(1, m))
                    wait(act, looked[free], c(1, n))
                    for b in range(2):
                        act.activation(turned[:, q % 2, b * 4 * P:(b + 1) * 4 * P], t_ps[b][:, :], ACT.Copy)
                    act.drain().then_inc(copied[q], 1)

                def power(c, q, m):
                    free, n = two_before(q, m)
                    act.wait_ge(scored[q], c(1, m))
                    wait(act, summed[free], c(1, n))
                    act.activation(weighted[:, q % 2, :, 4 * D:OUT], score[:, q % 2], ACT.Exp).then_inc(powered[q], 1)

                def store(c, q, m):
                    act.wait_ge(chained[q], c(1, m))
                    act.dma_start(at(result, chunk(c, q, m)), carried[:, q % 2].rearrange("p j w -> p (j w)")).then_inc(stored[q], 16)
                stages(act, [(1, power), (0, copy), (2, store)])
                for q in range(RING):
                    act.wait_ge(stored[q], 16 * NI)


def spline_gnn(nc, x, src, dst, edge_attr, edge_weight, stn1_w, stn1_b, stn2_w, stn2_b, stn3_w, stn3_b, stn4_w, stn4_b,
               conv_w, conv_b, w_gat, attn_l, attn_r, w_ih, w_hh, b_ih, b_hh, out):
    def dram(name, shape, dt=F32):
        return nc.dram_tensor(name, shape, dt, kind="Internal").ap()

    rec_src, rec_dst = dram("rec_src", [ROWS, WA]), dram("rec_dst", [ROWS, WB])
    r1, r2, r3, r4 = (dram(f"r{n}", [NC, P, r["words"]]) for n, r in enumerate((R1, R2, R3, R4), 1))
    h_table = dram("h_table", [NP, D])
    sums_d, sums_knots = dram("sums_d", [NC, P, CH * D]), dram("sums_knots", [NC, P, CH * 126])
    sums_pairs = dram("sums_pairs", [NC, P, CH * 128])
    z_even, z_odd = dram("z_even", [NP * 75, 64]), dram("z_odd", [NP * 50, 64])
    z_conv = dram("z_conv", [NZ * P * KW, D])
    t_table = dram("t_table", [NP, 4])
    t_parts, t_spread = dram("t_parts", [NP, 12], BF16), dram("t_spread", [T, P * 12], BF16)
    moved = dram("moved", [NC, P, CH * 3])
    q_table, kept_rows = dram("q_table", [NP, D + 4]), dram("kept_rows", [NC, P, CH * (D + 4)])
    maxima = dram("maxima", [NC, P, CH * 4])
    m_parts, m_spread = dram("m_parts", [NP, 24], BF16), dram("m_spread", [T, P * 24], BF16)
    sums_att = dram("sums_att", [NC, P, CH * 132])

    with ExitStack() as whole:
        def sb(name, shape, dt=F32):
            return whole.enter_context(nc.sbuf_tensor(name, shape, dt))

        k = {"iota": sb("iota", [P, T]), "part": sb("part", [P, 1]), "part_i": sb("part_i", [P, 1], I32),
             "ident": sb("ident", [P, P]), "before": sb("before", [P, P]), "ident_b": sb("ident_b", [P, P], BF16),
             "before_b": sb("before_b", [P, P], BF16), "ones": sb("ones", [P, P]), "ones_b": sb("ones_b", [P, P], BF16),
             "keep": sb("keep", [P, T]), "last": sb("last", [P, NB], I32), "tile_block": sb("tile_block", [P, T // P], I32)}
        xs, hs_padded = sb("xs", [P, NB, D]), sb("hs", [P, NZ, D])
        hs = hs_padded[:, 0:NB, :]
        degree = sb("degree", [P, NB])

        def add_to_x(name, sums, scale=None, bias=None):
            def work(dve):
                if scale is not None:
                    dve.tensor_tensor(sums[:, :, :], sums[:, :, :], scale.unsqueeze(2).to_broadcast([P, NB, D]), ALU.mult)
                    dve.drain()
                if bias is not None:
                    dve.tensor_tensor(sums[:, :, :], sums[:, :, :], bias.unsqueeze(1).to_broadcast([P, NB, D]), ALU.add)
                    dve.drain()
                dve.tensor_tensor(xs[:, :, :], xs[:, :, :], sums[:, :, :], ALU.add)
            on_vector(nc, name, work)

        by_dst = dict(k, last=sb("last_dst", [P, NB], I32), tile_block=sb("tile_block_dst", [P, T // P], I32))
        constants(nc, k)
        on_vector(nc, "hs0", lambda dve: dve.memset(hs_padded[:, NB:, :], 0.0))
        load_nodes(nc, x, xs)
        layernorm_relu(nc, "ln0", xs, hs, h_table)
        sort_edges(nc, "sa", k, src, [(dst, 1, I32), (edge_attr, 3, F32)], rec_src, WA)
        prepare_by_source(nc, k, rec_src, r1, r2)

        def knot_products(ph):
            bc = ph.sb("bc", [P, CH, 5, 5])
            knots = ph.sb("knots", [P, 2, CH, 126])

            def init(dve):
                dve.memset(knots[:, :, :, :], 1.0)

            def build(dve, rec, r):
                v = rec[:, R1["hats"]:].rearrange("p (t a n) -> p t a n", t=CH, a=3)
                dve.tensor_tensor(bc[:, :, :, :], v[:, :, 1, :].unsqueeze(3).to_broadcast([P, CH, 5, 5]),
                                  v[:, :, 2, :].unsqueeze(2).to_broadcast([P, CH, 5, 5]), ALU.mult)
                dve.drain()
                dve.tensor_tensor(knots[:, r, :, 0:125].rearrange("p t (a n) -> p t a n", a=5),
                                  v[:, :, 0, :].unsqueeze(3).to_broadcast([P, CH, 5, 25]),
                                  bc[:, :, :, :].rearrange("p t b c -> p t (b c)").unsqueeze(2).to_broadcast([P, CH, 5, 25]),
                                  ALU.mult)
            return {"knots": knots, "init": init, "build": build}

        segment_pass(nc, "p1", k, r1, R1, [(h_table, R1["col"], D)], [(D, sums_d), (126, sums_knots)],
                     lambda rows, r, j, extra: [[rows[0]], [extra["knots"][:, r, j, :]]], prepare=knot_products)

        with Phase(nc, "tables") as ph:
            h1 = ph.sb("h1", [P, NB, 64])
            with Phase(nc, "first") as ph1:
                knots, sums = ph1.sb("knots", [P, NB, 126]), ph1.sb("sums", [P, NB, D])
                w1, b1 = ph1.sb("w1", [125, 64]), ph1.sb("b1", [P, 64])
                load(nc, "lw1", [(w1[:, :], stn1_w), (b1[:, :], stn1_b.partition_broadcast(P))])
                block_sums(nc, "bs1", k, [(D, sums_d, sums), (126, sums_knots, knots)])
                add_to_x("x1", sums)

                def invert(dve):
                    dve.tensor_scalar(degree[:, :], knots[:, :, 125], 1.0, None, ALU.max)
                    dve.drain()
                    dve.reciprocal(degree[:, :], degree[:, :])
                on_vector(nc, "degree", invert)
                transform(nc, "t1", k, knots, 125, w1[:, :], 64, h1)
                elu(nc, "e1", h1, degree[:, :], b1[:, :])
            layernorm_relu(nc, "ln1", xs, hs, None)
            w2 = ph.sb("w2", [64, 125 * 64])
            load(nc, "lw2", [(w2[:, :].rearrange("i (n o) -> i n o", o=64), stn2_w.rearrange("n i o -> i n o"))])
            sort_edges(nc, "sb", by_dst, dst, [(src, 1, I32), (edge_weight, 1, F32)], rec_dst, WB,
                       TablesBeside(k, h1, 64, w2, 64, [
                           ((0, 2, 4), z_even.rearrange("(b p a m) f -> b p a (m f)", p=P, a=3, m=25)),
                           ((1, 3), z_odd.rearrange("(b p a m) f -> b p a (m f)", p=P, a=2, m=25))]))
        prepare_by_target(nc, by_dst, rec_dst, r4)

        segment_pass(nc, "c2", k, r2, R2, [(z_even, R2["idx"][0], 7 * 64), (z_odd, R2["idx"][1], 7 * 64)], [(128, sums_pairs)],
                     corner_products(((0,), (0,)), 64, 5, 128), weigh=weigh_corners(R2, ((0,), (0,)), 64, 5))

        with Phase(nc, "dense") as ph:
            h2, h3, t = ph.sb("h2", [P, NB, 64]), ph.sb("h3", [P, NB, 64]), ph.sb("t", [P, NB, 4])
            b2, b3, b4 = ph.sb("b2", [P, 64]), ph.sb("b3", [P, 64]), ph.sb("b4", [P, 3])
            w3, w4 = ph.sb("w3", [64, 64]), ph.sb("w4", [64, 4])
            on_vector(nc, "w40", lambda dve: dve.memset(w4[:, :], 0.0))
            load(nc, "lw3", [(b2[:, :], stn2_b.partition_broadcast(P)), (b3[:, :], stn3_b.partition_broadcast(P)),
                             (b4[:, :], stn4_b.partition_broadcast(P)), (w3[:, :], stn3_w), (w4[:, 0:3], stn4_w)])
            with Phase(nc, "pairs") as ph1:
                pairs = ph1.sb("pairs", [P, NB, 128])
                block_sums(nc, "bs2", k, [(128, sums_pairs, pairs)])
                on_vector(nc, "pair", lambda dve: dve.tensor_tensor(h2[:, :, :], pairs[:, :, 0:64], pairs[:, :, 64:], ALU.add))
            elu(nc, "e2", h2, degree[:, :], b2[:, :])
            transform(nc, "t3", k, h2, 64, w3[:, :], 64, h3)
            elu(nc, "e3", h3, None, b3[:, :])
            transform(nc, "t4", k, h3, 64, w4[:, :], 4, t)
            on_vector(nc, "t4b", lambda dve: dve.tensor_tensor(t[:, :, 0:3], t[:, :, 0:3],
                                                               b4[:, :].unsqueeze(1).to_broadcast([P, NB, 3]), ALU.add))
            rest, parts = ph.sb("rest", [P, NB, 4]), ph.sb("parts", [P, NB, 3, 4], BF16)
            on_vector(nc, "tp", lambda dve: split_parts(dve, t[:, :, :], rest[:, :, :], parts))
            load(nc, "st4", [(t_table.rearrange("(b p) w -> p b w", p=P), t[:, :, :]),
                             (t_parts.rearrange("(b p) w -> p b w", p=P), parts[:, :, :, :].rearrange("p b s w -> p b (s w)"))])
            by_tile(nc, "bt", k, t_parts, 12, t_spread)
        with Phase(nc, "moving") as ph:
            w5, turned = ph.sb("w5", [D, KW * D]), ph.sb("turned", [D, NZ * P])
            w5_planes = w5[:, :].rearrange("i (h n a o) -> i h n a o", h=2, a=3, o=D)
            load(nc, "lw5", [(w5_planes[:, h, :, a, :], conv_w[(2 * h + a) * 25:(2 * h + a + 1) * 25].rearrange("n i o -> i n o"))
                             for h in range(2) for a in range(3)])
            turn_blocks(nc, "tb", k, hs_padded, D, NZ, turned)
            move_pass(nc, k, rec_src, r1, t_table, t_spread, moved, turned, D, w5,
                      z_conv.rearrange("(b p m) f -> b p (m f)", p=P, m=KW))
        prepare_moved(nc, k, r1, moved, r3)

        segment_pass(nc, "c3", k, r3, R3, [(z_conv, R3["idx"][0], 20 * D)], [(4 * D, sums_pairs)],
                     corner_products(((0, 15),), D, 3, 4 * D), weigh=weigh_corners(R3, ((0, 15),), D, 3))
        with Phase(nc, "third") as ph:
            quads, sums, b5 = ph.sb("quads", [P, NB, 4 * D]), ph.sb("sums", [P, NB, D]), ph.sb("b5", [P, D])
            load(nc, "lb5", [(b5[:, :], conv_b.partition_broadcast(P))])
            block_sums(nc, "bs3", k, [(4 * D, sums_pairs, quads)])

            def fold_quads(dve):
                dve.tensor_tensor(quads[:, :, 0:2 * D], quads[:, :, 0:2 * D], quads[:, :, 2 * D:], ALU.add)
                dve.drain()
                dve.tensor_tensor(sums[:, :, :], quads[:, :, 0:D], quads[:, :, D:2 * D], ALU.add)
            on_vector(nc, "quads", fold_quads)
            add_to_x("x2", sums, degree[:, :], b5[:, :])
        layernorm_relu(nc, "ln2", xs, hs, h_table)

        segment_pass(nc, "p2", by_dst, r4, R4, [(h_table, R4["col"], D)], [(D, sums_d)],
                     lambda rows, r, j, extra: [[rows[0]]], scale=R4["w"])
        with Phase(nc, "fourth") as ph:
            sums = ph.sb("sums", [P, NB, D])
            block_sums(nc, "bs4", by_dst, [(D, sums_d, sums)])
            add_to_x("x3", sums)
        layernorm_relu(nc, "ln3", xs, hs, q_table)

        with Phase(nc, "heads") as ph:
            gat, attn = ph.sb("gat", [D, 4 * D]), ph.sb("attn", [D, 2, 4 * D])
            to_scores = ph.sb("to_scores", [D, 8])
            scores, largest, both = ph.sb("scores", [P, NB, 8]), ph.sb("largest", [P, NB, 4]), ph.sb("both", [P, NB, 8])
            load(nc, "lg", [(gat[:, :], w_gat), (attn[:, 0, :], attn_l.partition_broadcast(D)),
                            (attn[:, 1, :], attn_r.partition_broadcast(D))])

            def fold(dve):
                for side in range(2):
                    dve.tensor_tensor(attn[:, side, :], attn[:, side, :], gat[:, :], ALU.mult)
                dve.drain()
                dve.tensor_reduce(to_scores[:, :], attn[:, :, :].rearrange("p s (h f) -> p (s h) f", f=D), axis=AX, op=ALU.add)
            on_vector(nc, "fold", fold)
            transform(nc, "ts", k, hs, D, to_scores[:, :], 8, scores)
            load(nc, "sts", [(q_table[:, D:].rearrange("(b p) w -> p b w", p=P), scores[:, :, 0:4])])
            max_pass(nc, k, r4, q_table, kept_rows, maxima)
            block_sums(nc, "bs5", by_dst, [(4, maxima, largest)])

            def bound(dve):
                dve.tensor_copy(both[:, :, 0:4], scores[:, :, 4:8])
                dve.tensor_tensor(largest[:, :, :], largest[:, :, :], scores[:, :, 4:8], ALU.add)
                dve.drain()
                dve.scalar_tensor_tensor(both[:, :, 4:8], largest[:, :, :], 0.2, largest[:, :, :], ALU.mult, ALU.max)
            on_vector(nc, "bound", bound)
            rest, parts = ph.sb("rest", [P, NB, 8]), ph.sb("parts", [P, NB, 3, 8], BF16)
            on_vector(nc, "mp", lambda dve: split_parts(dve, both[:, :, :], rest[:, :, :], parts))
            load(nc, "stm", [(m_parts.rearrange("(b p) w -> p b w", p=P), parts[:, :, :, :].rearrange("p b s w -> p b (s w)"))])
            by_tile(nc, "bm", by_dst, m_parts, 24, m_spread)
        attention_pass(nc, k, r4, kept_rows, m_spread, sums_att)

        with Phase(nc, "update") as ph:
            gi, gh = ph.sb("gi", [P, NB, 3 * D]), ph.sb("gh", [P, NB, 3 * D])
            bi, bh = ph.sb("bi", [P, 3 * D]), ph.sb("bh", [P, 3 * D])
            gat_t, ih_t = ph.sb("gat_t", [P, P]), ph.sb("ih_t", [P, 3 * D])
            hh_t, from_heads = ph.sb("hh_t", [D, 3 * D]), ph.sb("from_heads", [P, 3 * D])
            on_vector(nc, "g0", lambda dve: dve.memset(gat_t[:, :], 0.0))
            load(nc, "lu", [(gat_t[h * D:(h + 1) * D, h * D:(h + 1) * D], w_gat[:, h * D:(h + 1) * D].rearrange("i f -> f i"))
                            for h in range(4)] +
                 [(ih_t[:, :], w_ih.rearrange("g f -> f g")), (hh_t[:, :], w_hh.rearrange("g f -> f g")),
                  (bi[:, :], b_ih.partition_broadcast(P)), (bh[:, :], b_hh.partition_broadcast(P))])
            fold_heads(nc, gat_t, ih_t, from_heads)
            with Phase(nc, "sums") as ph1:
                sums, inv = ph1.sb("sums", [P, NB, 132]), ph1.sb("inv", [P, NB, 4])
                block_sums(nc, "bs6", by_dst, [(132, sums_att, sums)])

                def normalize(dve):
                    dve.tensor_scalar(inv[:, :, :], sums[:, :, 128:132], 1e-30, None, ALU.max)
                    dve.drain()
                    dve.reciprocal(inv[:, :, :], inv[:, :, :])
                    dve.drain()
                    for h in range(4):
                        s = sums[:, :, h * D:(h + 1) * D]
                        dve.tensor_tensor(s, s, inv[:, :, h:h + 1].to_broadcast([P, NB, D]), ALU.mult)
                on_vector(nc, "normalize", normalize)
                transform(nc, "ti", k, sums, P, from_heads[:, :], 3 * D, gi)
            transform(nc, "th", k, hs, D, hh_t[:, :], 3 * D, gh)
            gated_update(nc, gi, gh, bi, bh, hs, xs)
            elu(nc, "e4", hs)
            on_vector(nc, "x4", lambda dve: dve.tensor_tensor(xs[:, :, :], xs[:, :, :], hs[:, :, :], ALU.add))
            load(nc, "out", [(out[0:(NB - 1) * P].rearrange("(b p) f -> p b f", p=P), xs[:, 0:NB - 1, :]),
                             (out[(NB - 1) * P:N], xs[0:LASTN, NB - 1, :])])


def fold_heads(nc, gat_t, ih_t, from_heads):
    with Phase(nc, "fh") as ph:
        ps, done = ph.ps("ps", [P, 512]), ph.sem("done")
        with nc.Block() as block:
            @block.tensor
            def _(pe):
                pe.matmul(ps[:, 0:3 * D], gat_t[:, :], ih_t[:, :], start=True, stop=True).then_inc(done, 1)

            @block.vector
            def _(dve):
                dve.wait_ge(done, 1)
                dve.tensor_copy(from_heads[:, :], ps[:, 0:3 * D])


def gated_update(nc, gi, gh, bi, bh, hs, xs):
    with Phase(nc, "gu") as ph:
        added, gated, mixed, bent = (ph.sem(n) for n in ("added", "gated", "mixed", "bent"))
        rz = 2 * D
        with nc.Block() as block:
            @block.vector
            def _(dve):
                for g, b in ((gi, bi), (gh, bh)):
                    dve.tensor_tensor(g[:, :, :], g[:, :, :], b[:, :].unsqueeze(1).to_broadcast([P, NB, 3 * D]), ALU.add)
                dve.drain()
                dve.tensor_tensor(gi[:, :, 0:rz], gi[:, :, 0:rz], gh[:, :, 0:rz], ALU.add).then_inc(added, 1)
                dve.wait_ge(gated, 1)
                n = gi[:, :, rz:]
                dve.tensor_tensor(gh[:, :, rz:], gh[:, :, rz:], gi[:, :, 0:D], ALU.mult)
                dve.drain()
                dve.tensor_tensor(n, n, gh[:, :, rz:], ALU.add).then_inc(mixed, 1)
                dve.wait_ge(bent, 1)
                dve.tensor_tensor(gh[:, :, 0:D], hs[:, :, :], n, ALU.subtract)
                dve.drain()
                dve.tensor_tensor(gh[:, :, 0:D], gh[:, :, 0:D], gi[:, :, D:rz], ALU.mult)
                dve.drain()
                dve.tensor_tensor(hs[:, :, :], gh[:, :, 0:D], n, ALU.add)

            @block.scalar
            def _(act):
                act.wait_ge(added, 1)
                act.activation(gi[:, :, 0:rz], gi[:, :, 0:rz], ACT.Sigmoid).then_inc(gated, 1)
                act.wait_ge(mixed, 1)
                act.activation(gi[:, :, rz:], gi[:, :, rz:], ACT.Tanh).then_inc(bent, 1)


_INS = ["x", "src", "dst", "edge_attr_3", "edge_weight", "L1_gnn_stn1_w", "L1_gnn_stn1_b", "L1_gnn_stn2_w", "L1_gnn_stn2_b",
        "L1_gnn_stn3_w", "L1_gnn_stn3_b", "L1_gnn_stn4_w", "L1_gnn_stn4_b", "L1_gnn_conv_w", "L1_gnn_conv_b", "L3_gnn_W_gat",
        "L3_gnn_attn_l", "L3_gnn_attn_r", "L3_gnn_W_ih", "L3_gnn_W_hh", "L3_gnn_b_ih", "L3_gnn_b_hh"]
_FLAT = ("edge_attr_3", "L3_gnn_attn_l", "L3_gnn_attn_r")


def kernel(**inputs):
    import numpy as np
    import concourse.bacc as bacc
    from concourse.bass_utils import run_bass_kernel_spmd

    nc = bacc.Bacc("TRN2", target_bir_lowering=False, num_devices=1)
    arrays, args = {}, []
    for name in _INS:
        a = np.ascontiguousarray(inputs[name])
        if name in _FLAT:
            a = a.reshape(-1)
        if name == "L1_gnn_stn1_w":
            a = a.reshape(a.shape[0], a.shape[2])
        arrays[f"in_{name}"] = a
        args.append(nc.dram_tensor(f"in_{name}", list(a.shape), mybir.dt.from_np(a.dtype), kind="ExternalInput").ap())
    out = nc.dram_tensor("out", [N, D], F32, kind="ExternalOutput").ap()
    spline_gnn(nc, *args, out)
    r = run_bass_kernel_spmd(nc, [arrays], core_ids=[0])
    return r.results[0]["out"]
```
